# Optimizing a Trainium2 kernel written in Bass

```python
import numpy as np
import jax
import jax.numpy as jnp

def _softmax(x, axis=-1):
    return jax.nn.softmax(x, axis=axis)

def _gelu(x):
    return jax.nn.gelu(x, approximate=True)

def _silu(x):
    return jax.nn.silu(x)

def _sigmoid(x):
    return jax.nn.sigmoid(x)

def _layernorm(x, axis=-1, eps=1e-05):
    m = jnp.mean(x, axis=axis, keepdims=True)
    v = jnp.var(x, axis=axis, keepdims=True)
    return (x - m) / jnp.sqrt(v + eps)

def _scatter_add(tgt, idx, src, axis=0):
    return tgt.at[idx].add(src)

def _segment_sum(src, seg, n):
    return jax.ops.segment_sum(src, seg, n)
kernel_name = 'mk_macaron_d4_jaxref_r8_a52e1c'

def setup_inputs(seed: int=0):
    np.random.seed(seed)
    _w = jnp.asarray

    def _L0_attn_setup():
        import jax, jax.numpy as jnp
        import numpy as np
        B, S, D, H = (4, 512, 128, 8)
        HD = D // H
        key = jax.random.key(seed)
        k1, k2, k3 = jax.random.split(key, 3)
        x = jax.random.normal(k1, (B, S, D), dtype=jnp.float32)
        w_qkv = jax.random.normal(k2, (D, 3 * D), dtype=jnp.float32) * (1.0 / np.sqrt(D))
        w_out = jax.random.normal(k3, (D, D), dtype=jnp.float32) * (1.0 / np.sqrt(D))
        return {'x': x, 'w_qkv': w_qkv, 'w_out': w_out}
    _L0_attn_in = _L0_attn_setup()

    def _L0_ffn_setup():
        import jax, jax.numpy as jnp
        import numpy as np
        DIM = 128
        DEPTH = 2
        HEADS = 8
        DIM_HEAD = 64
        WINDOW = 64
        INNER = HEADS * DIM_HEAD
        HID = int(DIM * 4 * 2 / 3)
        B, N = (2, 1024)
        QK_SCALE = 8.0

        def shift_token(t):
            t1, t2 = jnp.split(t, 2, axis=-1)
            t2 = jnp.pad(t2, ((0, 0), (1, 0), (0, 0)))[:, :-1]
            return jnp.concatenate([t1, t2], axis=-1)

        def l2norm(t):
            return t / jnp.clip(jnp.linalg.norm(t, axis=-1, keepdims=True), 1e-12)

        def rotate_half(x):
            x1, x2 = jnp.split(x, 2, axis=-1)
            return jnp.concatenate([-x2, x1], axis=-1)

        def rotary_xpos(q, k):
            n = q.shape[-2]
            half_idx = jnp.arange(0, DIM_HEAD, 2, dtype=jnp.float32)
            inv_freq = 1.0 / 10000.0 ** (half_idx / DIM_HEAD)
            t = jnp.arange(n, dtype=jnp.float32)
            freqs = t[:, None] * inv_freq[None, :]
            freqs = jnp.concatenate([freqs, freqs], axis=-1)
            base = (half_idx + 0.4 * DIM_HEAD) / (1.4 * DIM_HEAD)
            power = (t - n // 2) / float(WINDOW // 2)
            scale = base[None, :] ** power[:, None]
            scale = jnp.concatenate([scale, scale], axis=-1)
            cos, sin = (jnp.cos(freqs), jnp.sin(freqs))
            q = q * cos * scale + rotate_half(q) * sin * scale
            k = k * cos / scale + rotate_half(k) * sin / scale
            return (q, k)

        def local_attention(q, k, v):
            b, h, n, d = q.shape
            w = n // WINDOW
            bq = q.reshape(b, h, w, WINDOW, d) * QK_SCALE
            bk = k.reshape(b, h, w, WINDOW, d)
            bv = v.reshape(b, h, w, WINDOW, d)

            def look_around(t):
                p = jnp.pad(t, ((0, 0), (0, 0), (1, 0), (0, 0), (0, 0)))
                return jnp.concatenate([p[:, :, :w], p[:, :, 1:]], axis=3)
            bk, bv = (look_around(bk), look_around(bv))
            bt = jnp.arange(n).reshape(w, WINDOW)
            btp = jnp.pad(bt, ((1, 0), (0, 0)), constant_values=-1)
            btk = jnp.concatenate([btp[:w], btp[1:]], axis=1)
            sim = jnp.einsum('bhwid,bhwjd->bhwij', bq, bk)
            i = bt[:, :, None]
            j = btk[:, None, :]
            mask = (i < j) | (i > j + WINDOW) | (j == -1)
            sim = jnp.where(mask, -jnp.finfo(sim.dtype).max, sim)
            attn = jax.nn.softmax(sim, axis=-1)
            out = jnp.einsum('bhwij,bhwjd->bhwid', attn, bv)
            return out.reshape(b, h, n, d)

        def _layer(x, wqkv, qs, ksc, wo, lg, lb, w1, b1, w2, b2):
            b, n, _ = x.shape
            h = shift_token(x)
            qkv = h @ wqkv
            q, k, v = jnp.split(qkv, 3, axis=-1)
            to_heads = lambda t: t.reshape(b, n, HEADS, DIM_HEAD).transpose(0, 2, 1, 3)
            q, k, v = (to_heads(q), to_heads(k), to_heads(v))
            q = l2norm(q) * qs
            k = l2norm(k) * ksc
            q, k = rotary_xpos(q, k)
            o = local_attention(q, k, v)
            o = o.transpose(0, 2, 1, 3).reshape(b, n, INNER)
            x = x + o @ wo
            h = shift_token(x)
            mu = h.mean(-1, keepdims=True)
            var = h.var(-1, keepdims=True)
            h = (h - mu) / jnp.sqrt(var + 1e-05) * lg + lb
            h = h @ w1 + b1
            a, g = jnp.split(h, 2, axis=-1)
            h = a * jax.nn.gelu(g, approximate=False)
            x = x + h @ w2 + b2
            return x
        key = jax.random.key(seed)
        ks = jax.random.split(key, 6)
        return {'x': jax.random.normal(ks[0], (B, N, DIM), jnp.float32), 'wqkv': jax.random.normal(ks[1], (DEPTH, DIM, 3 * INNER), jnp.float32) * 0.02, 'q_scale': jnp.ones((DEPTH, DIM_HEAD), jnp.float32), 'k_scale': jnp.ones((DEPTH, DIM_HEAD), jnp.float32), 'wo': jax.random.normal(ks[2], (DEPTH, INNER, DIM), jnp.float32) * 0.02, 'ln_g': jnp.ones((DEPTH, DIM), jnp.float32), 'ln_b': jnp.zeros((DEPTH, DIM), jnp.float32), 'w1': jax.random.normal(ks[3], (DEPTH, DIM, 2 * HID), jnp.float32) * 0.02, 'b1': jnp.zeros((DEPTH, 2 * HID), jnp.float32), 'w2': jax.random.normal(ks[4], (DEPTH, HID, DIM), jnp.float32) * 0.02, 'b2': jnp.zeros((DEPTH, DIM), jnp.float32)}
    _L0_ffn_in = _L0_ffn_setup()

    def _L1_attn_setup():
        import jax, jax.numpy as jnp
        import numpy as np
        D_MODEL = 128
        N_HEADS = 16
        D_HEAD = D_MODEL // N_HEADS
        key = jax.random.key(seed)
        ks = jax.random.split(key, 5)
        s = 0.02
        return {'x': jax.random.normal(ks[0], (4, 256, D_MODEL), dtype=jnp.float32), 'w_qkv': jax.random.normal(ks[1], (D_MODEL, 3 * D_MODEL), dtype=jnp.float32) * s, 'b_qkv': jnp.zeros((3 * D_MODEL,), dtype=jnp.float32), 'w_out': jax.random.normal(ks[2], (D_MODEL, D_MODEL), dtype=jnp.float32) * s, 'b_out': jnp.zeros((D_MODEL,), dtype=jnp.float32)}
    _L1_attn_in = _L1_attn_setup()

    def _L1_ffn_setup():
        import jax, jax.numpy as jnp
        import numpy as np
        import math
        BETA = 0.9
        THRESHOLD = 1.0
        NUM_STEPS = 5
        ALPHA = 2.0

        @jax.custom_vjp
        def spike_fn(u):
            return (u > 0).astype(u.dtype)

        def _spike_fwd(u):
            return (spike_fn(u), u)

        def _spike_bwd(u, g):
            s = jnp.pi / 2.0 * ALPHA * u
            return (g * (ALPHA / 2.0) / (1.0 + s * s),)
        spike_fn.defvjp(_spike_fwd, _spike_bwd)
        key = jax.random.key(seed)
        k1, k2, k3 = jax.random.split(key, 3)
        n_embd = 128
        x = jax.random.normal(k1, (4, 256, n_embd), dtype=jnp.float32)
        W_fc = jax.random.normal(k2, (4 * n_embd, n_embd), dtype=jnp.float32) / math.sqrt(n_embd)
        W_proj = jax.random.normal(k3, (n_embd, 4 * n_embd), dtype=jnp.float32) / math.sqrt(4 * n_embd)
        return {'x': x, 'W_fc': W_fc, 'W_proj': W_proj}
    _L1_ffn_in = _L1_ffn_setup()

    def _L2_attn_setup():
        import jax, jax.numpy as jnp
        import numpy as np
        DIM = 128
        B, S = (4, 512)
        key = jax.random.key(seed)
        ks = jax.random.split(key, 12)
        d = DIM

        def lin(k, out_d, in_d):
            bound = 1.0 / np.sqrt(in_d)
            kw, kb = jax.random.split(k)
            W = jax.random.uniform(kw, (out_d, in_d), jnp.float32, -bound, bound)
            b = jax.random.uniform(kb, (out_d,), jnp.float32, -bound, bound)
            return (W, b)
        x = jax.random.normal(ks[0], (B, S, d), jnp.float32)
        random_phases = jax.random.normal(ks[1], (d,), jnp.float32) * (2.0 * np.pi)
        W_mag, b_mag = lin(ks[2], d, d)
        W_q, b_q = lin(ks[3], d, d)
        ln_g = jnp.ones((4 * d,), jnp.float32)
        ln_b = jnp.zeros((4 * d,), jnp.float32)
        W1, b1 = lin(ks[4], 2 * d, 4 * d)
        W2, b2 = lin(ks[5], d, 2 * d)
        return {'x': x, 'random_phases': random_phases, 'W_mag': W_mag, 'b_mag': b_mag, 'W_q': W_q, 'b_q': b_q, 'ln_g': ln_g, 'ln_b': ln_b, 'W1': W1, 'b1': b1, 'W2': W2, 'b2': b2}
    _L2_attn_in = _L2_attn_setup()

    def _L2_ffn_setup():
        import jax, jax.numpy as jnp
        import numpy as np
        key = jax.random.key(seed)
        k1, k2, k3, k4, k5 = jax.random.split(key, 5)
        d_in, d_out, r = (128, 128, 32)
        x = jax.random.normal(k1, (8, 1024, d_in), dtype=jnp.float32)
        W = jax.random.normal(k2, (d_out, d_in), dtype=jnp.float32) * (1.0 / np.sqrt(d_in))
        b = jax.random.normal(k3, (d_out,), dtype=jnp.float32) * 0.01
        V_r = jax.random.normal(k4, (d_in, r), dtype=jnp.float32) * (1.0 / np.sqrt(d_in))
        C = jax.random.normal(k5, (d_out, r), dtype=jnp.float32) * (1.0 / np.sqrt(r))
        return {'x': x, 'W': W, 'b': b, 'V_r': V_r, 'C': C}
    _L2_ffn_in = _L2_ffn_setup()

    def _L3_attn_setup():
        import jax, jax.numpy as jnp
        import numpy as np
        DIM = 128
        EPS = 1e-12

        def _rmsnorm(x, gamma):
            norm = jnp.sqrt(jnp.sum(x * x, axis=-1, keepdims=True))
            scale = jnp.asarray(np.sqrt(x.shape[-1]), x.dtype)
            return x / jnp.maximum(norm, EPS) * scale * gamma
        key = jax.random.key(seed)
        k1, k2, k3 = jax.random.split(key, 3)
        b, n, d = (2, 512, DIM)
        x = jax.random.normal(k1, (b, n, d), dtype=jnp.float32)
        w_qkva = jax.random.normal(k2, (3 * d, d), dtype=jnp.float32) * (1.0 / np.sqrt(d))
        gamma = jnp.ones((d,), dtype=jnp.float32)
        return {'x': x, 'gamma': gamma, 'w_qkva': w_qkva}
    _L3_attn_in = _L3_attn_setup()

    def _L3_ffn_setup():
        import jax, jax.numpy as jnp
        import numpy as np
        B, S, D, H, M, E, K = (4, 128, 128, 16, 2, 8, 2)
        KD = D // H
        F = 2 * D
        EPS = 1e-06

        def _ln(x, g, b):
            m = jnp.mean(x, axis=-1, keepdims=True)
            v = jnp.mean(jnp.square(x - m), axis=-1, keepdims=True)
            return (x - m) * jax.lax.rsqrt(v + EPS) * g + b
        key = jax.random.key(seed)
        ks = jax.random.split(key, 12)
        r = lambda i, shape: jax.random.normal(ks[i], shape, jnp.float32) * 0.02
        return {'x': jax.random.normal(ks[0], (B, S, D), jnp.float32), 'ln1_g': jnp.ones((D,), jnp.float32), 'ln1_b': jnp.zeros((D,), jnp.float32), 'ln2_g': jnp.ones((D,), jnp.float32), 'ln2_b': jnp.zeros((D,), jnp.float32), 'mha_wq': r(1, (M, D, H, KD)), 'mha_bq': jnp.zeros((M, H, KD), jnp.float32), 'mha_wk': r(2, (M, D, H, KD)), 'mha_bk': jnp.zeros((M, H, KD), jnp.float32), 'mha_wv': r(3, (M, D, H, KD)), 'mha_bv': jnp.zeros((M, H, KD), jnp.float32), 'mha_wo': r(4, (M, H, KD, D)), 'mha_bo': jnp.zeros((M, D), jnp.float32), 'mha_rw': r(5, (D, M)), 'mha_rb': jnp.zeros((M,), jnp.float32), 'ffn_rw': r(6, (D, E)), 'ffn_rb': jnp.zeros((E,), jnp.float32), 'fw1': r(7, (E, D, F)), 'fw2': r(8, (E, F, D))}
    _L3_ffn_in = _L3_ffn_setup()
    _d = {'L0_attn_x': _L0_attn_in['x'], 'L0_attn_w_qkv': _L0_attn_in['w_qkv'], 'L0_attn_w_out': _L0_attn_in['w_out'], 'L0_ffn_wqkv': _L0_ffn_in['wqkv'], 'L0_ffn_q_scale': _L0_ffn_in['q_scale'], 'L0_ffn_k_scale': _L0_ffn_in['k_scale'], 'L0_ffn_wo': _L0_ffn_in['wo'], 'L0_ffn_ln_g': _L0_ffn_in['ln_g'], 'L0_ffn_ln_b': _L0_ffn_in['ln_b'], 'L0_ffn_w1': _L0_ffn_in['w1'], 'L0_ffn_b1': _L0_ffn_in['b1'], 'L0_ffn_w2': _L0_ffn_in['w2'], 'L0_ffn_b2': _L0_ffn_in['b2'], 'L1_attn_w_qkv': _L1_attn_in['w_qkv'], 'L1_attn_b_qkv': _L1_attn_in['b_qkv'], 'L1_attn_w_out': _L1_attn_in['w_out'], 'L1_attn_b_out': _L1_attn_in['b_out'], 'L1_ffn_W_fc': _L1_ffn_in['W_fc'], 'L1_ffn_W_proj': _L1_ffn_in['W_proj'], 'L2_attn_random_phases': _L2_attn_in['random_phases'], 'L2_attn_W_mag': _L2_attn_in['W_mag'], 'L2_attn_b_mag': _L2_attn_in['b_mag'], 'L2_attn_W_q': _L2_attn_in['W_q'], 'L2_attn_b_q': _L2_attn_in['b_q'], 'L2_attn_ln_g': _L2_attn_in['ln_g'], 'L2_attn_ln_b': _L2_attn_in['ln_b'], 'L2_attn_W1': _L2_attn_in['W1'], 'L2_attn_b1': _L2_attn_in['b1'], 'L2_attn_W2': _L2_attn_in['W2'], 'L2_attn_b2': _L2_attn_in['b2'], 'L2_ffn_W': _L2_ffn_in['W'], 'L2_ffn_b': _L2_ffn_in['b'], 'L2_ffn_V_r': _L2_ffn_in['V_r'], 'L2_ffn_C': _L2_ffn_in['C'], 'L3_attn_gamma': _L3_attn_in['gamma'], 'L3_attn_w_qkva': _L3_attn_in['w_qkva'], 'L3_ffn_ln1_g': _L3_ffn_in['ln1_g'], 'L3_ffn_ln1_b': _L3_ffn_in['ln1_b'], 'L3_ffn_ln2_g': _L3_ffn_in['ln2_g'], 'L3_ffn_ln2_b': _L3_ffn_in['ln2_b'], 'L3_ffn_mha_wq': _L3_ffn_in['mha_wq'], 'L3_ffn_mha_bq': _L3_ffn_in['mha_bq'], 'L3_ffn_mha_wk': _L3_ffn_in['mha_wk'], 'L3_ffn_mha_bk': _L3_ffn_in['mha_bk'], 'L3_ffn_mha_wv': _L3_ffn_in['mha_wv'], 'L3_ffn_mha_bv': _L3_ffn_in['mha_bv'], 'L3_ffn_mha_wo': _L3_ffn_in['mha_wo'], 'L3_ffn_mha_bo': _L3_ffn_in['mha_bo'], 'L3_ffn_mha_rw': _L3_ffn_in['mha_rw'], 'L3_ffn_mha_rb': _L3_ffn_in['mha_rb'], 'L3_ffn_ffn_rw': _L3_ffn_in['ffn_rw'], 'L3_ffn_ffn_rb': _L3_ffn_in['ffn_rb'], 'L3_ffn_fw1': _L3_ffn_in['fw1'], 'L3_ffn_fw2': _L3_ffn_in['fw2']}
    _x0 = _d['L0_attn_x']
    _d['L0_attn_x'] = jax.random.normal(jax.random.fold_in(jax.random.key(seed), 1), (8, 256, 128), dtype=_x0.dtype)
    del _x0
    return _d

def reference(L0_attn_x, L0_attn_w_qkv, L0_attn_w_out, L0_ffn_wqkv, L0_ffn_q_scale, L0_ffn_k_scale, L0_ffn_wo, L0_ffn_ln_g, L0_ffn_ln_b, L0_ffn_w1, L0_ffn_b1, L0_ffn_w2, L0_ffn_b2, L1_attn_w_qkv, L1_attn_b_qkv, L1_attn_w_out, L1_attn_b_out, L1_ffn_W_fc, L1_ffn_W_proj, L2_attn_random_phases, L2_attn_W_mag, L2_attn_b_mag, L2_attn_W_q, L2_attn_b_q, L2_attn_ln_g, L2_attn_ln_b, L2_attn_W1, L2_attn_b1, L2_attn_W2, L2_attn_b2, L2_ffn_W, L2_ffn_b, L2_ffn_V_r, L2_ffn_C, L3_attn_gamma, L3_attn_w_qkva, L3_ffn_ln1_g, L3_ffn_ln1_b, L3_ffn_ln2_g, L3_ffn_ln2_b, L3_ffn_mha_wq, L3_ffn_mha_bq, L3_ffn_mha_wk, L3_ffn_mha_bk, L3_ffn_mha_wv, L3_ffn_mha_bv, L3_ffn_mha_wo, L3_ffn_mha_bo, L3_ffn_mha_rw, L3_ffn_mha_rb, L3_ffn_ffn_rw, L3_ffn_ffn_rb, L3_ffn_fw1, L3_ffn_fw2):

    def _L0_attn_ref(x, w_qkv, w_out):
        import jax, jax.numpy as jnp
        import numpy as np
        B, S, D, H = (4, 512, 128, 8)
        HD = D // H
        b, s, d = x.shape
        qkv = x @ w_qkv
        q, k, v = jnp.split(qkv, 3, axis=-1)
        q = q.reshape(b, s, H, HD)
        k = k.reshape(b, s, H, HD)
        v = v.reshape(b, s, H, HD)
        fq = jnp.fft.fft(q, axis=-1)
        fk = jnp.fft.fft(k, axis=-1)
        fv = jnp.fft.fft(v, axis=-1)
        kv = fk * fv
        kv = jnp.cumsum(kv, axis=1)
        vals = jnp.fft.ifft(kv * jnp.conj(fq), axis=-1).real.astype(x.dtype)
        vals = vals.reshape(b, s, d)
        return vals @ w_out

    def _L0_ffn_ref(x, wqkv, q_scale, k_scale, wo, ln_g, ln_b, w1, b1, w2, b2):
        import jax, jax.numpy as jnp
        import numpy as np
        DIM = 128
        DEPTH = 2
        HEADS = 8
        DIM_HEAD = 64
        WINDOW = 64
        INNER = HEADS * DIM_HEAD
        HID = int(DIM * 4 * 2 / 3)
        B, N = (2, 1024)
        QK_SCALE = 8.0

        def shift_token(t):
            t1, t2 = jnp.split(t, 2, axis=-1)
            t2 = jnp.pad(t2, ((0, 0), (1, 0), (0, 0)))[:, :-1]
            return jnp.concatenate([t1, t2], axis=-1)

        def l2norm(t):
            return t / jnp.clip(jnp.linalg.norm(t, axis=-1, keepdims=True), 1e-12)

        def rotate_half(x):
            x1, x2 = jnp.split(x, 2, axis=-1)
            return jnp.concatenate([-x2, x1], axis=-1)

        def rotary_xpos(q, k):
            n = q.shape[-2]
            half_idx = jnp.arange(0, DIM_HEAD, 2, dtype=jnp.float32)
            inv_freq = 1.0 / 10000.0 ** (half_idx / DIM_HEAD)
            t = jnp.arange(n, dtype=jnp.float32)
            freqs = t[:, None] * inv_freq[None, :]
            freqs = jnp.concatenate([freqs, freqs], axis=-1)
            base = (half_idx + 0.4 * DIM_HEAD) / (1.4 * DIM_HEAD)
            power = (t - n // 2) / float(WINDOW // 2)
            scale = base[None, :] ** power[:, None]
            scale = jnp.concatenate([scale, scale], axis=-1)
            cos, sin = (jnp.cos(freqs), jnp.sin(freqs))
            q = q * cos * scale + rotate_half(q) * sin * scale
            k = k * cos / scale + rotate_half(k) * sin / scale
            return (q, k)

        def local_attention(q, k, v):
            b, h, n, d = q.shape
            w = n // WINDOW
            bq = q.reshape(b, h, w, WINDOW, d) * QK_SCALE
            bk = k.reshape(b, h, w, WINDOW, d)
            bv = v.reshape(b, h, w, WINDOW, d)

            def look_around(t):
                p = jnp.pad(t, ((0, 0), (0, 0), (1, 0), (0, 0), (0, 0)))
                return jnp.concatenate([p[:, :, :w], p[:, :, 1:]], axis=3)
            bk, bv = (look_around(bk), look_around(bv))
            bt = jnp.arange(n).reshape(w, WINDOW)
            btp = jnp.pad(bt, ((1, 0), (0, 0)), constant_values=-1)
            btk = jnp.concatenate([btp[:w], btp[1:]], axis=1)
            sim = jnp.einsum('bhwid,bhwjd->bhwij', bq, bk)
            i = bt[:, :, None]
            j = btk[:, None, :]
            mask = (i < j) | (i > j + WINDOW) | (j == -1)
            sim = jnp.where(mask, -jnp.finfo(sim.dtype).max, sim)
            attn = jax.nn.softmax(sim, axis=-1)
            out = jnp.einsum('bhwij,bhwjd->bhwid', attn, bv)
            return out.reshape(b, h, n, d)

        def _layer(x, wqkv, qs, ksc, wo, lg, lb, w1, b1, w2, b2):
            b, n, _ = x.shape
            h = shift_token(x)
            qkv = h @ wqkv
            q, k, v = jnp.split(qkv, 3, axis=-1)
            to_heads = lambda t: t.reshape(b, n, HEADS, DIM_HEAD).transpose(0, 2, 1, 3)
            q, k, v = (to_heads(q), to_heads(k), to_heads(v))
            q = l2norm(q) * qs
            k = l2norm(k) * ksc
            q, k = rotary_xpos(q, k)
            o = local_attention(q, k, v)
            o = o.transpose(0, 2, 1, 3).reshape(b, n, INNER)
            x = x + o @ wo
            h = shift_token(x)
            mu = h.mean(-1, keepdims=True)
            var = h.var(-1, keepdims=True)
            h = (h - mu) / jnp.sqrt(var + 1e-05) * lg + lb
            h = h @ w1 + b1
            a, g = jnp.split(h, 2, axis=-1)
            h = a * jax.nn.gelu(g, approximate=False)
            x = x + h @ w2 + b2
            return x
        for l in range(DEPTH):
            x = _layer(x, wqkv[l], q_scale[l], k_scale[l], wo[l], ln_g[l], ln_b[l], w1[l], b1[l], w2[l], b2[l])
        return x

    def _L1_attn_ref(x, w_qkv, b_qkv, w_out, b_out):
        import jax, jax.numpy as jnp
        import numpy as np
        D_MODEL = 128
        N_HEADS = 16
        D_HEAD = D_MODEL // N_HEADS
        B, T, C = x.shape
        qkv = jnp.einsum('btc,cd->btd', x, w_qkv) + b_qkv
        q, k, v = jnp.split(qkv, 3, axis=2)
        q = q.reshape(B, T, N_HEADS, D_HEAD).transpose(0, 2, 1, 3)
        k = k.reshape(B, T, N_HEADS, D_HEAD).transpose(0, 2, 1, 3)
        v = v.reshape(B, T, N_HEADS, D_HEAD).transpose(0, 2, 1, 3)
        scale = jnp.float32(1.0) / jnp.sqrt(jnp.float32(D_HEAD))
        scores = jnp.einsum('bhqd,bhkd->bhqk', q, k) * scale
        causal = jnp.tril(jnp.ones((T, T), dtype=bool))
        scores = jnp.where(causal, scores, jnp.finfo(scores.dtype).min)
        attn = jax.nn.softmax(scores, axis=-1)
        out = jnp.einsum('bhqk,bhkd->bhqd', attn, v)
        out = out.transpose(0, 2, 1, 3).reshape(B, T, C)
        return jnp.einsum('btc,cd->btd', out, w_out) + b_out

    def _L1_ffn_ref(x, W_fc, W_proj):
        import jax, jax.numpy as jnp
        import numpy as np
        import math
        BETA = 0.9
        THRESHOLD = 1.0
        NUM_STEPS = 5
        ALPHA = 2.0

        @jax.custom_vjp
        def spike_fn(u):
            return (u > 0).astype(u.dtype)

        def _spike_fwd(u):
            return (spike_fn(u), u)

        def _spike_bwd(u, g):
            s = jnp.pi / 2.0 * ALPHA * u
            return (g * (ALPHA / 2.0) / (1.0 + s * s),)
        spike_fn.defvjp(_spike_fwd, _spike_bwd)
        h = jnp.square(jax.nn.relu(jnp.einsum('bsd,fd->bsf', x, W_fc)))
        y = jnp.einsum('bsf,df->bsd', h, W_proj)

        def step(mem, _):
            reset = jax.lax.stop_gradient(spike_fn(mem - THRESHOLD))
            mem_new = BETA * mem + y - reset * THRESHOLD
            spk = spike_fn(mem_new - THRESHOLD)
            return (mem_new, spk)
        mem0 = jnp.zeros_like(y)
        _, spks = jax.lax.scan(step, mem0, None, length=NUM_STEPS)
        return jnp.sum(spks, axis=0) / NUM_STEPS

    def _L2_attn_ref(x, random_phases, W_mag, b_mag, W_q, b_q, ln_g, ln_b, W1, b1, W2, b2):
        import jax, jax.numpy as jnp
        import numpy as np
        DIM = 128
        B, S = (4, 512)
        Bx, Sx, D = x.shape
        magnitude = jax.nn.sigmoid(jnp.einsum('bsd,ed->bse', x, W_mag) + b_mag) * 5.0
        position = jnp.arange(Sx, dtype=x.dtype)[None, :, None]
        phi = random_phases[None, None, :] * position * 0.01
        cos_phi = jnp.cos(phi)
        sin_phi = jnp.sin(phi)
        weighted = magnitude * x
        mem_r = jnp.cumsum(weighted * cos_phi, axis=1)
        mem_i = jnp.cumsum(weighted * sin_phi, axis=1)
        acc_mag = jnp.cumsum(magnitude, axis=1)
        inv_sqrt = 1.0 / jnp.sqrt(acc_mag + 1e-08)
        mr = mem_r * inv_sqrt
        mi = mem_i * inv_sqrt
        q_off = jnp.einsum('bsd,ed->bse', x, W_q) + b_q
        phi_q = phi + q_off
        cq = jnp.cos(phi_q)
        sq = jnp.sin(phi_q)
        retrieved_r = mr * cq + mi * sq
        retrieved_i = mi * cq - mr * sq
        context = jnp.concatenate([x * cos_phi, x * sin_phi, retrieved_r, retrieved_i], axis=-1)
        mu = jnp.mean(context, axis=-1, keepdims=True)
        var = jnp.mean((context - mu) ** 2, axis=-1, keepdims=True)
        h = (context - mu) / jnp.sqrt(var + 1e-05) * ln_g + ln_b
        h = jax.nn.gelu(jnp.einsum('bsf,gf->bsg', h, W1) + b1, approximate=False)
        out = jnp.einsum('bsg,dg->bsd', h, W2) + b2
        return x + out

    def _L2_ffn_ref(x, W, b, V_r, C):
        import jax, jax.numpy as jnp
        import numpy as np
        base = jnp.einsum('bsd,od->bso', x, W) + b
        correction = jnp.einsum('bsr,or->bso', jnp.einsum('bsd,dr->bsr', x, V_r), C)
        return base + correction

    def _L3_attn_ref(x, gamma, w_qkva):
        import jax, jax.numpy as jnp
        import numpy as np
        DIM = 128
        EPS = 1e-12

        def _rmsnorm(x, gamma):
            norm = jnp.sqrt(jnp.sum(x * x, axis=-1, keepdims=True))
            scale = jnp.asarray(np.sqrt(x.shape[-1]), x.dtype)
            return x / jnp.maximum(norm, EPS) * scale * gamma
        d = x.shape[-1]
        xn = _rmsnorm(x, gamma)
        qkva = jnp.einsum('bnd,ed->bne', xn, w_qkva)
        q, kv, a = (qkva[..., :d], qkva[..., d:2 * d], qkva[..., 2 * d:])
        a = jax.nn.sigmoid(a)

        def binary_operator(e_i, e_j):
            a_i, kv_i = e_i
            a_j, kv_j = e_j
            return (a_j * a_i, a_j * kv_i + kv_j)
        _, kv_scan = jax.lax.associative_scan(binary_operator, (a, kv), axis=1)
        return q * kv_scan

    def _L3_ffn_ref(x, ln1_g, ln1_b, ln2_g, ln2_b, mha_wq, mha_bq, mha_wk, mha_bk, mha_wv, mha_bv, mha_wo, mha_bo, mha_rw, mha_rb, ffn_rw, ffn_rb, fw1, fw2):
        import jax, jax.numpy as jnp
        import numpy as np
        B, S, D, H, M, E, K = (4, 128, 128, 16, 2, 8, 2)
        KD = D // H
        F = 2 * D
        EPS = 1e-06

        def _ln(x, g, b):
            m = jnp.mean(x, axis=-1, keepdims=True)
            v = jnp.mean(jnp.square(x - m), axis=-1, keepdims=True)
            return (x - m) * jax.lax.rsqrt(v + EPS) * g + b
        n1 = _ln(x, ln1_g, ln1_b)
        mha_probs = jax.nn.softmax(jnp.mean(n1, axis=1) @ mha_rw + mha_rb, axis=-1)
        q = jnp.einsum('btd,mdhk->mbhtk', n1, mha_wq) + mha_bq[:, None, :, None, :]
        kk = jnp.einsum('btd,mdhk->mbhtk', n1, mha_wk) + mha_bk[:, None, :, None, :]
        v = jnp.einsum('btd,mdhk->mbhtk', n1, mha_wv) + mha_bv[:, None, :, None, :]
        scores = jnp.einsum('mbhtk,mbhsk->mbhts', q, kk) / jnp.sqrt(jnp.float32(KD))
        attn = jax.nn.softmax(scores, axis=-1)
        ctx = jnp.einsum('mbhts,mbhsk->mbthk', attn, v)
        mha_out = jnp.einsum('mbthk,mhkd->mbtd', ctx, mha_wo) + mha_bo[:, None, None, :]
        x = x + jnp.einsum('mbtd,bm->btd', mha_out, mha_probs)
        n2 = _ln(x, ln2_g, ln2_b)
        ffn_probs = jax.nn.softmax(jnp.mean(n2, axis=1) @ ffn_rw + ffn_rb, axis=-1)
        topk_p, topk_i = jax.lax.top_k(ffn_probs, K)
        topk_p = topk_p / jnp.sum(topk_p, axis=-1, keepdims=True)
        sw1 = fw1[topk_i]
        sw2 = fw2[topk_i]
        h = jax.nn.gelu(jnp.einsum('btd,bkdf->bktf', n2, sw1), approximate=False)
        eo = jnp.einsum('bktf,bkfd->bktd', h, sw2)
        return x + jnp.einsum('bktd,bk->btd', eo, topk_p)
    x = L0_attn_x
    x = x + 0.5 * _L0_ffn_ref(_layernorm(x, axis=-1), L0_ffn_wqkv, L0_ffn_q_scale, L0_ffn_k_scale, L0_ffn_wo, L0_ffn_ln_g, L0_ffn_ln_b, L0_ffn_w1, L0_ffn_b1, L0_ffn_w2, L0_ffn_b2)
    x = x + _L0_attn_ref(_layernorm(x, axis=-1), L0_attn_w_qkv, L0_attn_w_out)
    x = x + 0.5 * _L0_ffn_ref(_layernorm(x, axis=-1), L0_ffn_wqkv, L0_ffn_q_scale, L0_ffn_k_scale, L0_ffn_wo, L0_ffn_ln_g, L0_ffn_ln_b, L0_ffn_w1, L0_ffn_b1, L0_ffn_w2, L0_ffn_b2)
    x = x + 0.5 * _L1_ffn_ref(_layernorm(x, axis=-1), L1_ffn_W_fc, L1_ffn_W_proj)
    x = x + _L1_attn_ref(_layernorm(x, axis=-1), L1_attn_w_qkv, L1_attn_b_qkv, L1_attn_w_out, L1_attn_b_out)
    x = x + 0.5 * _L1_ffn_ref(_layernorm(x, axis=-1), L1_ffn_W_fc, L1_ffn_W_proj)
    x = x + 0.5 * _L2_ffn_ref(_layernorm(x, axis=-1), L2_ffn_W, L2_ffn_b, L2_ffn_V_r, L2_ffn_C)
    x = x + _L2_attn_ref(_layernorm(x, axis=-1), L2_attn_random_phases, L2_attn_W_mag, L2_attn_b_mag, L2_attn_W_q, L2_attn_b_q, L2_attn_ln_g, L2_attn_ln_b, L2_attn_W1, L2_attn_b1, L2_attn_W2, L2_attn_b2)
    x = x + 0.5 * _L2_ffn_ref(_layernorm(x, axis=-1), L2_ffn_W, L2_ffn_b, L2_ffn_V_r, L2_ffn_C)
    x = x + 0.5 * _L3_ffn_ref(_layernorm(x, axis=-1), L3_ffn_ln1_g, L3_ffn_ln1_b, L3_ffn_ln2_g, L3_ffn_ln2_b, L3_ffn_mha_wq, L3_ffn_mha_bq, L3_ffn_mha_wk, L3_ffn_mha_bk, L3_ffn_mha_wv, L3_ffn_mha_bv, L3_ffn_mha_wo, L3_ffn_mha_bo, L3_ffn_mha_rw, L3_ffn_mha_rb, L3_ffn_ffn_rw, L3_ffn_ffn_rb, L3_ffn_fw1, L3_ffn_fw2)
    x = x + _L3_attn_ref(_layernorm(x, axis=-1), L3_attn_gamma, L3_attn_w_qkva)
    x = x + 0.5 * _L3_ffn_ref(_layernorm(x, axis=-1), L3_ffn_ln1_g, L3_ffn_ln1_b, L3_ffn_ln2_g, L3_ffn_ln2_b, L3_ffn_mha_wq, L3_ffn_mha_bq, L3_ffn_mha_wk, L3_ffn_mha_bk, L3_ffn_mha_wv, L3_ffn_mha_bv, L3_ffn_mha_wo, L3_ffn_mha_bo, L3_ffn_mha_rw, L3_ffn_mha_rb, L3_ffn_ffn_rw, L3_ffn_ffn_rb, L3_ffn_fw1, L3_ffn_fw2)
    return x

_drawn_inputs = setup_inputs


def setup_inputs(seed=0):
    import zlib

    import numpy as np

    out = dict(_drawn_inputs(seed))
    spreads = {'L0_ffn_q_scale': (1.0, 0.6),
     'L0_ffn_k_scale': (1.0, 0.6),
     'L0_ffn_ln_g': (1.0, 0.6),
     'L0_ffn_ln_b': (0.0, 0.8),
     'L0_ffn_b1': (0.0, 0.8),
     'L0_ffn_b2': (0.0, 0.1),
     'L1_attn_b_qkv': (0.0, 2.0),
     'L1_attn_b_out': (0.0, 2.0),
     'L2_attn_ln_g': (1.0, 0.6),
     'L2_attn_ln_b': (0.0, 0.8),
     'L3_attn_gamma': (1.0, 0.6),
     'L3_ffn_ln1_g': (1.0, 0.6),
     'L3_ffn_ln1_b': (0.0, 2.0),
     'L3_ffn_ln2_g': (1.0, 0.6),
     'L3_ffn_ln2_b': (0.0, 2.0),
     'L3_ffn_mha_bq': (0.0, 2.0),
     'L3_ffn_mha_bk': (0.0, 2.0),
     'L3_ffn_mha_bv': (0.0, 2.0),
     'L3_ffn_mha_bo': (0.0, 2.0),
     'L3_ffn_mha_rb': (0.0, 2.0),
     'L3_ffn_ffn_rb': (0.0, 2.0)}
    factors = {'L0_ffn_wqkv': 3.622,
     'L0_ffn_wo': 3.578,
     'L0_ffn_w1': 6.435,
     'L0_ffn_w2': 6.25,
     'L1_attn_w_qkv': 8.0,
     'L1_attn_w_out': 8.0,
     'L1_ffn_W_fc': 200.0,
     'L1_ffn_W_proj': 200.0,
     'L2_attn_random_phases': 8.0,
     'L2_attn_W_mag': 8.0,
     'L2_attn_b_mag': 64.0,
     'L2_attn_W_q': 8.0,
     'L2_attn_b_q': 8.0,
     'L2_attn_W1': 8.0,
     'L2_attn_b1': 64.0,
     'L2_attn_W2': 8.0,
     'L2_attn_b2': 64.0,
     'L2_ffn_W': 8.0,
     'L2_ffn_b': 200.0,
     'L2_ffn_V_r': 8.0,
     'L2_ffn_C': 8.0,
     'L3_attn_w_qkva': 8.0,
     'L3_ffn_mha_wq': 39.71,
     'L3_ffn_mha_wk': 32.587,
     'L3_ffn_mha_wv': 26.26,
     'L3_ffn_mha_wo': 27.303,
     'L3_ffn_mha_rw': 29.622,
     'L3_ffn_ffn_rw': 61.46,
     'L3_ffn_fw1': 32.84,
     'L3_ffn_fw2': 27.519}
    for name, (base, spread) in spreads.items():
        noise = np.random.default_rng([zlib.crc32(name.encode()), seed]).standard_normal(out[name].shape)
        drawn = base * np.exp(spread * noise) if base else spread * noise
        out[name] = jnp.asarray(drawn.astype(out[name].dtype))
    for name, factor in factors.items():
        out[name] = (out[name] * factor).astype(out[name].dtype)
    return out
```

```python
from contextlib import ExitStack

import numpy as np
import concourse.bass as bass
from concourse import mybir

F32 = mybir.dt.float32
BF16 = mybir.dt.bfloat16
ALU = mybir.AluOpType
ACT = mybir.ActivationFunctionType
AXX = mybir.AxisListType.X

P = 128
BATCH, SEQ = 8, 256
TOKENS = BATCH * SEQ
CHUNK = 512
NCHUNK = TOKENS // CHUNK
PER = CHUNK // SEQ
BANK = 512
BANKS = 8
MASKED = -3.0e38

DEPTH, L0_HEADS, L0_DIM, WINDOW = 2, 8, 64, 64
INNER = L0_HEADS * L0_DIM
HID = int(P * 4 * 2 / 3)
HID_BLOCKS = [(i, min(P, HID - i)) for i in range(0, HID, P)]
SPIKE_HID, SPIKE_STEPS, BETA = 4 * P, 5, 0.9
HEADS, KD = 16, P // 16
GROUPS = HEADS // 4
M_EXPERTS, EXPERTS, TOP_K, FF = 2, 8, 2, 2 * P
RANK = 32


class Token:

    def __init__(self, stage):
        self.stage, self.waited_for, self.sem, self.value = stage, False, None, None


class Queue:

    def __init__(self, program, name):
        self.program, self.name, self.items, self.last, self.held = program, name, [], None, []

    def __call__(self, method, *args, w=(), **kw):
        token = Token(self.program.stage)
        waits = [t for t in list(w) + self.held if t is not None]
        self.held = []
        for t in waits:
            t.waited_for = True
        self.items.append((method, args, kw, waits, token))
        self.last = token
        return token

    def load(self, out, in_, sem, w=()):
        token = Token(None)
        token.sem, token.value = sem, 16
        for t in w:
            t.waited_for = True
        self.items.append((None, (out, in_), {}, list(w), token))
        return token

    def count(self, sems):
        reached = {}
        for _, _, _, _, t in self.items:
            if t.waited_for and t.sem is None:
                key = (self.name, t.stage)
                if key not in sems:
                    sems[key] = self.program.sem(f"{self.name}_stage{t.stage}")
                reached[key] = reached.get(key, 0) + 1
                t.sem, t.value = sems[key], reached[key]

    def emit(self, eng):
        passed = {}
        for method, args, kw, waits, token in self.items:
            for t in waits:
                if passed.get(t.sem.name, 0) < t.value:
                    eng.wait_ge(t.sem, t.value)
                    passed[t.sem.name] = t.value
            if method is None:
                eng.dma_start(*args).then_inc(token.sem, 16)
            else:
                done = method(*args, **kw)
                if token.waited_for:
                    done.then_inc(token.sem, 1)


class Program:
    def __init__(self, nc, ctx):
        self.nc, self.ctx, self.stage = nc, ctx, 0
        self.pe, self.act, self.dve, self.pool, self.sp = (
            Queue(self, n) for n in ("tensor", "scalar", "vector", "gpsimd", "sync"))
        self.engines = [self.pe, self.act, self.dve, self.pool]

    def sem(self, name):
        return self.ctx.enter_context(self.nc.semaphore(name))

    def sbuf(self, name, shape, dtype=F32):
        return self.ctx.enter_context(self.nc.sbuf_tensor(name, shape, dtype))

    def next_stage(self):
        last = [q.last for q in self.engines if q.last is not None]
        for q in self.engines:
            q.held = q.held + last
        self.stage += 1


class Arena:

    def __init__(self, whole, columns):
        self.whole, self.columns, self.used = whole, columns, 0

    def reset(self):
        self.used = 0

    def take(self, columns, rows=P):
        at = self.used
        self.used += columns
        assert self.used <= self.columns, (self.used, self.columns)
        return self.whole[0:rows, at:at + columns]

    def take_bf16(self, columns, rows=P):
        return self.take((columns + 1) // 2, rows).bitcast(BF16)


def packed(parts):
    at, out = 0, {}
    for name, columns in parts:
        out[name] = (at, columns)
        at += columns
    return out, at


COLUMNS = ([f"L0_{n}{l}" for l in range(DEPTH) for n in ("qs", "qsr", "ks", "ksr", "lg", "lb", "b2")]
           + [f"L0_b1{l}_{i}" for l in range(DEPTH) for i in range(2 * len(HID_BLOCKS))]
           + [f"L1_bq{g}" for g in range(GROUPS)] + [f"L1_bk{g}" for g in range(GROUPS)] + ["L1_bo"]
           + ["L2_b", "ph", "bmag", "bq"] + [f"L2_lg{i}" for i in range(4)] + [f"L2_lb{i}" for i in range(4)]
           + ["L2_b1_0", "L2_b1_1", "L2_b2", "gamma", "ln1_g", "ln1_b", "ln2_g", "ln2_b"]
           + [f"L3_bq{i}" for i in range(M_EXPERTS * GROUPS)] + [f"L3_bk{i}" for i in range(M_EXPERTS * GROUPS)]
           + ["bo0", "bo1", "eps5", "eps6", "eps8", "zero"])
COL = {n: i for i, n in enumerate(COLUMNS)}
ROUTE = M_EXPERTS + EXPERTS

CONST, CONST_N = packed([("ident", P), ("center", P), ("mean", P), ("causal_q", P), ("causal_k", P),
                         ("local_q1", 3 * WINDOW), ("local_k0", 3 * WINDOW), ("negsel", 32),
                         ("cos_q", SEQ), ("sin_q", SEQ), ("cos_k", SEQ), ("sin_k", SEQ),
                         ("pos", SEQ), ("headsum", 8 * 16), ("dft_k1", P), ("dft_k2", P), ("dft_v1", P), ("dft_v2", P),
                         ("idft1", P), ("idft2", P), ("earlier", EXPERTS * EXPERTS)])
HEADROW_N = 8 * P
W, W_N = {}, {}
for _l in range(DEPTH):
    W[f"L0f{_l}"], W_N[f"L0f{_l}"] = packed([("qkv", 3 * INNER), ("rot", 2 * INNER), ("wo", INNER),
                                             ("w1", 2 * HID), ("w2", len(HID_BLOCKS) * P)])
W["L0a"], W_N["L0a"] = packed([("qT", P), ("kT", P), ("vT", P), ("out", P)])
W["L1f"], W_N["L1f"] = packed([("fcT", SPIKE_HID), ("projT", SPIKE_HID)])
W["L1a"], W_N["L1a"] = packed([("wq", GROUPS * P), ("wk", GROUPS * P), ("wv", P), ("wo", P)])
W["L2"], W_N["L2"] = packed([("fT", P), ("magT", P), ("qT", P), ("w1T", 4 * 2 * P), ("w2T", 2 * P)])
W["L3a"], W_N["L3a"] = packed([("qkvaT", 3 * P)])
W["L3m"], W_N["L3m"] = packed([("wq", M_EXPERTS * GROUPS * P), ("wk", M_EXPERTS * GROUPS * P),
                               ("wv", M_EXPERTS * P), ("wo", M_EXPERTS * P), ("rw", ROUTE), ("rb", ROUTE)])
W["L3e"], W_N["L3e"] = packed([("fw1", EXPERTS * FF), ("fw2", EXPERTS * FF)])


def program(nc, ins, out, stages=tuple(range(12))):
    with ExitStack() as ctx:
        pr = Program(nc, ctx)
        pe, act, dve, pool, sp = pr.pe, pr.act, pr.dve, pr.pool, pr.sp
        T, V, S, G = nc.tensor, nc.vector, nc.scalar, nc.gpsimd
        pool_queue = pool

        def pool(method, *args, w=(), **kw):
            return pool_queue(method, *args, w=list(w) + [pool_queue.last], **kw)

        X = pr.sbuf("residual", [P, TOKENS])
        X0 = pr.sbuf("stream", [P, TOKENS])
        const = pr.sbuf("const", [P, CONST_N])
        cols = pr.sbuf("cols", [P, len(COLUMNS)])
        headrow = pr.sbuf("headrow", [16, HEADROW_N])
        rows = pr.sbuf("rows", [1, P + M_EXPERTS * P + P])
        low = pr.sbuf("low_rank", [RANK, 2 * P])
        wt = {n: pr.sbuf(f"w_{n}", [P, k]) for n, k in W_N.items()}
        ident_b = pr.sbuf("ident_b", [P, P], BF16)
        masks_b = pr.sbuf("masks_b", [P, 2 * P + 6 * WINDOW], BF16)
        negsel = pr.sbuf("negsel", [96, 32, P], BF16)
        fold = pr.sbuf("folded", [P, 10 * P])
        probs = pr.sbuf("probs", [P, 16 * BATCH])
        ARENA = 20200
        arena = Arena(pr.sbuf("arena", [P, ARENA]), ARENA)
        ps = ctx.enter_context(nc.psum_tensor("ps", [P, BANKS, BANK], F32))
        bank_free = [None] * BANKS

        def K(name):
            at, n = CONST[name]
            return const[:, at:at + n]

        def C(name):
            return cols[:, COL[name]:COL[name] + 1]

        def wp(group, name):
            at, n = W[group][name]
            return wt[group][:, at:at + n]

        def mm(o, lhsT, rhs, start=True, stop=True, w=()):
            return pe(T.matmul, o, lhsT, rhs, start=start, stop=stop, skip_group_check=True, w=w)

        def seqs(ap, n=PER):
            return ap.rearrange("p (b s) -> p b s", b=n)

        def table(ap, n=PER):
            return ap.unsqueeze(1).to_broadcast([ap.shape[0], n, SEQ])

        loads = {}

        def load(name, dst, src):
            loads[name] = sp.load(dst, src, pr.sem(f"loaded_{name}"))

        load("x", X[:], ins["x"])
        load("const", const[:], ins["const"])
        load("cols", cols[:], ins["cols"])
        load("headrow", headrow[:], ins["headrow"])
        load("rows", rows[:], ins["rows"])
        load("low", low[:], ins["low"])
        for n in ("L0f0", "L0f1", "L0a", "L1f", "L1a", "L2", "L3a", "L3m", "L3e"):
            load(n, wt[n][:], ins[n])

        t = dve(V.tensor_copy, ident_b[:], K("ident"), w=[loads["const"]])
        dve(V.tensor_copy, masks_b[:, 0:2 * P + 6 * WINDOW],
            const[:, CONST["causal_q"][0]:CONST["causal_q"][0] + 2 * P + 6 * WINDOW])
        dve(V.tensor_copy, negsel[:], K("negsel")[0:96, :].unsqueeze(2).to_broadcast([96, 32, P]))
        causal_q, causal_k = masks_b[:, 0:P], masks_b[:, P:2 * P]
        local_q1 = masks_b[:, 2 * P:2 * P + 3 * WINDOW]
        local_k0 = masks_b[:, 2 * P + 3 * WINDOW:2 * P + 6 * WINDOW]

        def layernorm(src, dst, eps, ready, scale=None, shift=None, work=None):
            sq, sd = work
            done, st = [], []
            for c in range(NCHUNK):
                cs = slice(c * CHUNK, (c + 1) * CHUNK)
                a, b = 2 * c, 2 * c + 1
                centred = mm(ps[:, a, :], K("center"), src[:, cs], w=[bank_free[a], ready[c], loads["const"]])
                squared = act(S.activation, sq[:, cs], ps[:, a, :], ACT.Square, w=[centred])
                st.append(squared)
            for c in range(NCHUNK):
                cs = slice(c * CHUNK, (c + 1) * CHUNK)
                a, b = 2 * c, 2 * c + 1
                var = mm(ps[:, b, :], K("mean"), sq[:, cs], w=[bank_free[b], st[c]])
                root = act(S.activation, sd[:, cs], ps[:, b, :], ACT.Sqrt, bias=C(eps), w=[var, loads["cols"]])
                bank_free[b] = root
                inv = dve(V.reciprocal, sd[:, cs], sd[:, cs], w=[root])
                h = dve(V.tensor_tensor, dst[:, cs], ps[:, a, :], sd[:, cs], ALU.mult, w=[inv])
                bank_free[a] = h
                if scale is not None:
                    h = dve(V.tensor_scalar, dst[:, cs], dst[:, cs], C(scale), C(shift), ALU.mult, ALU.add, w=[h])
                done.append(h)
            return done

        def start_stage():
            pr.next_stage()
            arena.reset()

        x_ready = [loads["x"]] * NCHUNK

        class Attention:

            def __init__(self, heads, dim, scale, q1, k1, masks_q, masks_k, o_heads):
                self.heads, self.dim, self.scale = heads, dim, scale
                self.q1, self.k1 = q1, k1
                self.masks_q, self.masks_k, self.o_heads = masks_q, masks_k, o_heads
                self.mx = [arena.take(2 * heads) for _ in range(2)]
                self.split = [arena.take_bf16(SEQ, 96) for _ in range(2)]
                self.rest = arena.take(2 * SEQ, 32)
                self.mid = arena.take_bf16(SEQ, 32)
                self.pt = [arena.take(2 * BANK) for _ in range(2)]
                self.rinv = [arena.take(2 * heads) for _ in range(2)]
                self.ctx = [arena.take(2 * P) for _ in range(2)]
                self.max_done, self.split_done, self.split_read = [None] * 2, [None] * 2, [None] * 2
                self.pt_read, self.ctx_read = [None] * 2, [None] * 2
                self.zeroed = [dve(V.memset, s, 0.0) for s in self.split]
                self.unit = 0

            def pass1(self, b, q, k, ready):
                i, H = b % 2, self.heads
                mx = self.mx[i].rearrange("p (t h) -> p t h", t=2)
                ks, nk = self.q1
                n0 = SEQ if not self.masks_q else P
                found = []

                def scores(h):
                    bank = h % 2
                    m = mm(ps[:, bank, 0:n0], q(h)[:, 0:P], k(h)[:, 0:n0], stop=not self.masks_q,
                           w=[bank_free[bank]] + ready)
                    if self.masks_q:
                        mm(ps[:, bank, 0:P], ident_b[:], self.masks_q[0], start=False)
                    m = mm(ps[:, bank, n0:n0 + nk], q(h)[:, P:SEQ], k(h)[:, ks:ks + nk], stop=not self.masks_q)
                    if self.masks_q:
                        mk = self.masks_q[1]
                        m = mm(ps[:, bank, n0 + nk - mk.shape[1]:n0 + nk], ident_b[:], mk, start=False)
                    free = self.max_done[i] if h == 0 else None
                    if n0 == nk:
                        m = dve(V.tensor_reduce, mx[:, :, h:h + 1], ps[:, bank, 0:2 * nk].rearrange("p (t s) -> p t s", t=2),
                                AXX, ALU.max, w=[m, free])
                    else:
                        dve(V.tensor_reduce, mx[:, 0, h:h + 1], ps[:, bank, 0:n0], AXX, ALU.max, w=[m, free])
                        m = dve(V.tensor_reduce, mx[:, 1, h:h + 1], ps[:, bank, n0:n0 + nk], AXX, ALU.max)
                    bank_free[bank] = m
                    found.append(m)

                def split():
                    for t in range(2):
                        tr = pe(T.transpose, ps[0:H, 7, t * P:(t + 1) * P], mx[:, t, :], K("ident"),
                                w=[bank_free[7]] + found[-1:])
                    self.max_done[i] = tr
                    src, s = ps[0:H, 7, 0:SEQ], self.split[i]
                    r1, r2 = self.rest[0:H, 0:SEQ], self.rest[0:H, SEQ:2 * SEQ]
                    hi = dve(V.tensor_copy, s[0:H, :], src, w=[tr, self.split_read[i], self.zeroed[i]])
                    a = dve(V.tensor_tensor, r1, src, s[0:H, :], ALU.subtract, w=[hi, self.split_done[1 - i]])
                    bank_free[7] = a
                    mid = dve(V.tensor_copy, self.mid[0:H, :], r1, w=[a])
                    dve(V.tensor_copy, s[32:32 + H, :], self.mid[0:H, :], w=[mid])
                    self.split_done[i] = dve(V.tensor_tensor, s[64:64 + H, :], r1, self.mid[0:H, :], ALU.subtract)

                return [lambda h=h: scores(h) for h in range(H)] + [split]

            def pass2(self, b, q, k, v, ready, finish):
                i, H = b % 2, self.heads
                (i0, n0), (i1, n1) = self.k1

                def two(h0):
                    u = self.unit % 2
                    self.unit += 1
                    for h in (h0, h0 + 1):
                        bank = 2 + 2 * u + h - h0
                        for t, (st, n, at) in enumerate(((i0, n0, 0), (i1, n1, n0))):
                            o = ps[:, bank, at:at + n]
                            mm(o, k(h)[:, t * P:(t + 1) * P], q(h)[:, st:st + n], stop=False,
                               w=[bank_free[bank]] + ready)
                            if self.masks_k:
                                mk = self.masks_k[t]
                                mm(ps[:, bank, at:at + mk.shape[1]], ident_b[:], mk, start=False, stop=False)
                            m = mm(o, negsel[:, h, :], self.split[i][:, st:st + n], start=False,
                                   w=[self.split_done[i]])
                    self.split_read[i] = m
                    both = n0 + n1
                    pt = self.pt[u].rearrange("p (h c) -> p h c", h=2)
                    e = act(S.activation, pt[:, :, 0:both], ps[:, 2 + 2 * u:4 + 2 * u, 0:both], ACT.Exp,
                            scale=self.scale, w=[m, self.pt_read[u]])
                    bank_free[2 + 2 * u] = bank_free[3 + 2 * u] = e
                    D = self.dim + 1
                    for h in (h0, h0 + 1):
                        slot = h % self.o_heads
                        pth = pt[:, h - h0, :]
                        for t in range(2):
                            at = (t * self.o_heads + slot) * D
                            if t == 0:
                                parts = [(0, P, pth[:, 0:P])] + ([(1, P, pth[:, n0:n0 + P])] if i1 == 0 else [])
                            else:
                                m1 = n0 - P
                                at1 = n0 + P - i1
                                parts = [(1, P, pth[:, at1:at1 + P]), (0, m1, pth[:, P:P + m1])]
                            for j, (kt, n, lhsT) in enumerate(parts):
                                o = mm(ps[0:n, 6, at:at + D], lhsT, v(kt, h), start=j == 0, stop=j == len(parts) - 1,
                                       w=[e] + ([bank_free[6]] if slot == 0 else []))
                    self.pt_read[u] = o
                    if slot == self.o_heads - 1:
                        finish(b, h0 + 1, o)

                return [lambda h=h: two(h) for h in range(0, H, 2)]

            def normalise(self, n, o, factor=None):
                oh, D = self.o_heads, self.dim + 1
                k = n % 2
                ov = ps[:, 6, 0:2 * oh * D].rearrange("p (a d) -> p a d", d=D)
                rinv = self.rinv[k][:, 0:2 * oh]
                r = dve(V.reciprocal, rinv, ov[:, :, self.dim:D].rearrange("p a d -> p (a d)"), w=[o])
                if factor is not None:
                    r = dve(V.tensor_scalar, rinv, rinv, factor, None, ALU.mult, w=[r])
                ctxv = self.ctx[k].rearrange("p (a d) -> p a d", d=self.dim)
                c = dve(V.tensor_tensor, ctxv, ov[:, :, 0:self.dim],
                        rinv.unsqueeze(2).to_broadcast([P, 2 * oh, self.dim]), ALU.mult, w=[r, self.ctx_read[k]])
                bank_free[6] = c
                for t in range(2):
                    tr = pe(T.transpose, ps[:, 7, t * P:(t + 1) * P], self.ctx[k][:, t * P:(t + 1) * P], K("ident"),
                            w=[c, bank_free[7]])
                self.ctx_read[k] = tr
                return tr

        def interleave(first, second):
            n = max(len(first), len(second))
            a = b = 0
            for i in range(n):
                while a < len(first) and a * n < (i + 1) * len(first):
                    first[a]()
                    a += 1
                while b < len(second) and b * n < (i + 1) * len(second):
                    second[b]()
                    b += 1

        def l0_layer(l, last, x_in):
            start_stage()
            w0 = f"L0f{l}"
            ready = [loads[w0], loads["cols"], loads["const"], loads["headrow"]]
            H = arena.take(TOKENS)
            oT = arena.take(PER * 4 * SEQ).rearrange("p (b j s) -> p b j s", b=PER, j=4)
            tabs = {n: arena.take(SEQ) for n in ("aq", "bq", "ak", "bk")}
            qk = [arena.take(8 * CHUNK).rearrange("p (j s) -> p j s", j=8) for _ in range(1)]
            t1 = [arena.take(CHUNK) for _ in range(2)]
            t2 = [arena.take(CHUNK) for _ in range(2)]
            sqs = [arena.take(CHUNK) for _ in range(2)]
            rn = arena.take(CHUNK, 16)
            va = [arena.take(2 * L0_HEADS * 65).rearrange("p (t h d) -> p t h d", t=2, h=L0_HEADS) for _ in range(2)]
            att = Attention(L0_HEADS, L0_DIM, 1.0, (WINDOW, 3 * WINDOW), ((0, 3 * WINDOW), (P, P)),
                            (local_q1[:, WINDOW:], local_q1), (local_k0, local_k0[:, 0:P]), 2)
            for v in va:
                ones = dve(V.memset, v[:, :, :, L0_DIM:L0_DIM + 1], 1.0)
            tab_ready = []
            for o, tname, cname in (("aq", "cos_q", "qs"), ("bq", "sin_q", "qsr"), ("ak", "cos_k", "ks"), ("bk", "sin_k", "ksr")):
                tab_ready.append(dve(V.tensor_scalar, tabs[o], K(tname), C(f"L0_{cname}{l}"), None, ALU.mult,
                                     w=[loads["cols"], loads["const"]]))

            def shifted(chunk_src, H, ready_c, cs):
                lower = pool(G.tensor_copy, H[0:64, cs], chunk_src[0:64, cs], w=[ready_c])
                hv, sv = seqs(H[64:P, cs]), seqs(chunk_src[64:P, cs])
                first = pool(G.memset, hv[:, :, 0:1], 0.0, w=[lower])
                return pool(G.tensor_copy, hv[:, :, 1:SEQ], sv[:, :, 0:SEQ - 1], w=[first])

            h_done = [shifted(X0, H, x_in[c], slice(c * CHUNK, (c + 1) * CHUNK)) for c in range(NCHUNK)]
            qk_free = [None]
            rn_free = [None]
            va_free = [None, None]
            sq_read, t_read = [None, None], [None, None]
            x1 = []

            for c in range(NCHUNK):
                cs = slice(c * CHUNK, (c + 1) * CHUNK)
                Q = qk[0]
                placed = []
                for j in range(8):
                    a, r = 2 * (j % 2), 2 * (j % 2) + 1
                    k = j % 2
                    p1 = mm(ps[:, a, :], wp(w0, "qkv")[:, j * P:(j + 1) * P], H[:, cs],
                            w=[bank_free[a], h_done[c]] + ready)
                    p2 = mm(ps[:, r, :], wp(w0, "rot")[:, j * P:(j + 1) * P], H[:, cs], w=[bank_free[r]])
                    sq = act(S.activation, sqs[k], ps[:, a, :], ACT.Square, w=[p1, sq_read[k]])
                    nsum = mm(ps[0:16, 6, :], K("headsum")[:, j * 16:(j + 1) * 16], sqs[k], start=j == 0, stop=j == 7,
                              w=[sq, bank_free[6]])
                    sq_read[k] = nsum
                    ta, tb = ("aq", "bq") if j < 4 else ("ak", "bk")
                    m1 = dve(V.tensor_tensor, seqs(t1[k]), seqs(ps[:, a, :]), table(tabs[ta]), ALU.mult,
                             w=[p2, sq, t_read[k]] + tab_ready)
                    m2 = dve(V.tensor_tensor, seqs(t2[k]), seqs(ps[:, r, :]), table(tabs[tb]), ALU.mult)
                    bank_free[a], bank_free[r] = m2, m2
                    ad = pool(G.tensor_tensor, Q[:, j, :], t1[k], t2[k], ALU.add, w=[m2, qk_free[0]])
                    t_read[k] = ad
                    placed.append(ad)
                root = act(S.activation, rn, ps[0:16, 6, :], ACT.Sqrt, bias=C("zero")[0:16, :], w=[nsum, rn_free[0]])
                bank_free[6] = root
                cl = dve(V.tensor_scalar, rn, rn, 1e-12, None, ALU.max, w=[root])
                inv = dve(V.reciprocal, rn, rn, w=[cl])
                normed = []
                for j in range(8):
                    a = 4 + j % 2
                    bc = mm(ps[:, a, :], headrow[:, j * P:(j + 1) * P], rn, w=[bank_free[a], inv])
                    nm = dve(V.tensor_tensor, Q[:, j, :], Q[:, j, :], ps[:, a, :], ALU.mult, w=[bc, placed[j]])
                    bank_free[a] = nm
                    normed.append(nm)
                rn_free[0] = bc
                vdone = []
                for bb in range(PER):
                    for t_ in range(2):
                        a = t_
                        tok = slice(c * CHUNK + bb * SEQ + t_ * P, c * CHUNK + bb * SEQ + (t_ + 1) * P)
                        vm = mm(ps[:, a, :], H[:, tok], wp(w0, "qkv")[:, 2 * INNER:3 * INNER], w=[bank_free[a]])
                        ve = act(S.activation, va[bb][:, t_, :, 0:L0_DIM], ps[:, a, :].rearrange("p (h d) -> p h d", h=L0_HEADS),
                                 ACT.Copy, w=[vm, va_free[bb], ones])
                        bank_free[a] = ve
                    vdone.append(ve)

                def head(ap, bb):
                    def f(h):
                        base = 64 * (h % 2)
                        off = 0 if ap == "q" else 4
                        return Q[base:base + 64, off + h // 2, bb * SEQ:(bb + 1) * SEQ]
                    return f

                o_placed = []

                def finish(bb, h, o):
                    tr = att.normalise(h // 2, o)
                    cp = act(S.activation, oT[:, bb, h // 2, :], ps[:, 7, 0:SEQ], ACT.Copy, w=[tr, o_free[0]])
                    bank_free[7] = cp
                    o_placed.append(cp)

                if c == 0:
                    o_free = [None]
                for bb in range(PER):
                    q, k_ = head("q", bb), head("k", bb)
                    interleave(att.pass1(bb, q, k_, normed), [])
                    if bb == 1:
                        pass
                    steps2 = att.pass2(bb, q, k_, lambda kt, h, bb=bb: va[bb][:, kt, h, :], [vdone[bb]], finish)
                    interleave([], steps2)
                    va_free[bb] = att.pt_read[(att.unit - 1) % 2]
                qk_free[0] = va_free[1]
                for bb in range(PER):
                    for j in range(4):
                        y = mm(ps[:, bb, 0:SEQ], wp(w0, "wo")[:, j * P:(j + 1) * P], oT[:, bb, j, :], start=j == 0,
                               stop=j == 3, w=[bank_free[bb]] + o_placed[-1:])
                    bs = slice(c * CHUNK + bb * SEQ, c * CHUNK + (bb + 1) * SEQ)
                    ad = dve(V.tensor_tensor, X0[:, bs], X0[:, bs], ps[:, bb, 0:SEQ], ALU.add, w=[y])
                    bank_free[bb] = ad
                o_free[0] = y
                x1.append(ad)

            start_stage()
            H2 = arena.take(TOKENS)
            N2 = arena.take(TOKENS)
            work = (arena.take(TOKENS), arena.take(TOKENS))
            g = [arena.take(CHUNK) for _ in range(2)]
            hh = [arena.take(3 * CHUNK) for _ in range(2)]
            h_done = [shifted(X0, H2, x1[c], slice(c * CHUNK, (c + 1) * CHUNK)) for c in range(NCHUNK)]
            n_done = layernorm(H2, N2, "eps5", h_done, f"L0_lg{l}", f"L0_lb{l}", work)
            out_done = []
            g_read, hh_read = [None, None], [None, None]
            for c in range(NCHUNK):
                cs = slice(c * CHUNK, (c + 1) * CHUNK)
                k = c % 2
                for j, (at, n) in enumerate(HID_BLOCKS):
                    a, gb = 2 * (j % 2), 2 * (j % 2) + 1
                    u = j % 2
                    pa = mm(ps[0:n, a, :], wp(w0, "w1")[:, at:at + n], N2[:, cs], w=[bank_free[a], n_done[c], loads[w0]])
                    pg = mm(ps[0:n, gb, :], wp(w0, "w1")[:, HID + at:HID + at + n], N2[:, cs], w=[bank_free[gb]])
                    ge = act(S.activation, g[u][0:n, :], ps[0:n, gb, :], ACT.Gelu,
                             bias=C(f"L0_b1{l}_{3 + j}")[0:n, :], w=[pg, g_read[u]])
                    bank_free[gb] = ge
                    pr_ = dve(V.scalar_tensor_tensor, hh[k][0:n, j * CHUNK:(j + 1) * CHUNK], ps[0:n, a, :],
                              C(f"L0_b1{l}_{j}")[0:n, :], g[u][0:n, :], ALU.add, ALU.mult, w=[ge, pa, hh_read[k]])
                    bank_free[a] = pr_
                    g_read[u] = pr_
                ob = 4 + c % 2
                for j, (at, n) in enumerate(HID_BLOCKS):
                    y = mm(ps[:, ob, :], wp(w0, "w2")[0:n, j * P:(j + 1) * P], hh[k][0:n, j * CHUNK:(j + 1) * CHUNK],
                           start=j == 0, stop=j == 2, w=[bank_free[ob], pr_])
                hh_read[k] = y
                xx = dve(V.scalar_tensor_tensor, X0[:, cs], ps[:, ob, :], C(f"L0_b2{l}"), X0[:, cs], ALU.add, ALU.add, w=[y])
                bank_free[ob] = xx
                if last:
                    xx = dve(V.scalar_tensor_tensor, X[:, cs], X0[:, cs], 0.5, X[:, cs], ALU.mult, ALU.add, w=[xx])
                out_done.append(xx)
            return out_done

        def l0_ffn(x_ready):
            start_stage()
            done = layernorm(X, X0, "eps5", x_ready, work=(arena.take(TOKENS), arena.take(TOKENS)))
            for l in range(DEPTH):
                done = l0_layer(l, l == DEPTH - 1, done)
            return done

        def l0_attn(x_ready):
            start_stage()
            h = arena.take(TOKENS)
            done = layernorm(X, h, "eps5", x_ready, work=(arena.take(TOKENS), arena.take(TOKENS)))
            spec = [("kT", "dft_k1"), ("kT", "dft_k2"), ("vT", "dft_v1"), ("vT", "dft_v2"), ("qT", "dft_v1"), ("qT", "dft_v2")]
            for i, (wn, dn) in enumerate(spec):
                bk = 0 if i < 4 else 1
                m = mm(ps[:, bk, (i % 4) * P:(i % 4 + 1) * P], wp("L0a", wn), DFT[dn],
                       w=[bank_free[bk], loads["L0a"], loads["const"]])
            for i, dn in enumerate(("idft1", "idft2")):
                m = mm(ps[:, 1, (2 + i) * P:(3 + i) * P], K(dn), wp("L0a", "out"))
            e0 = act(S.activation, fold[:, 0:BANK], ps[:, 0, :], ACT.Copy, w=[m])
            folded = act(S.activation, fold[:, BANK:2 * BANK], ps[:, 1, :], ACT.Copy)
            bank_free[0] = bank_free[1] = folded
            k1, kv, cum, t2 = (arena.take(TOKENS) for _ in range(4))
            keep = arena.take(TOKENS)
            kp = dve(V.memset, keep, 1.0)
            kp = dve(V.memset, seqs(keep, BATCH)[:, :, 0:1], 0.0, w=[kp])
            out = []
            for c in range(NCHUNK):
                cs = slice(c * CHUNK, (c + 1) * CHUNK)
                prj = []
                for i in range(6):
                    b = i if i < 4 else i + 0
                    prj.append(mm(ps[:, b, :], fold[:, i * P:(i + 1) * P], h[:, cs],
                                  w=[bank_free[b], done[c], folded]))
                c1 = act(S.activation, k1[:, cs], ps[:, 0, :], ACT.Copy, w=[prj[0]])
                c2 = act(S.activation, t2[:, cs], ps[:, 1, :], ACT.Copy, w=[prj[1]])
                bank_free[0], bank_free[1] = c1, c2
                a1 = dve(V.tensor_tensor, k1[:, cs], k1[:, cs], ps[:, 2, :], ALU.mult, w=[c1, prj[2]])
                a2 = dve(V.tensor_tensor, t2[:, cs], t2[:, cs], ps[:, 3, :], ALU.mult, w=[c2, prj[3]])
                bank_free[2], bank_free[3] = a1, a2
                s_ = pool(G.tensor_tensor, kv[:, cs], k1[:, cs], t2[:, cs], ALU.add, w=[a1, a2])
                cu = dve(V.tensor_tensor_scan, cum[:, cs], keep[:, cs], kv[:, cs], 0.0, ALU.mult, ALU.add, w=[s_, kp])
                b1 = dve(V.tensor_tensor, k1[:, cs], cum[:, cs], ps[:, 4, :], ALU.mult, w=[cu, prj[4]])
                b2 = dve(V.tensor_tensor, t2[:, cs], cum[:, cs], ps[:, 5, :], ALU.mult, w=[prj[5]])
                bank_free[4], bank_free[5] = b1, b2
                ob = 6 + c % 2
                mm(ps[:, ob, :], fold[:, 6 * P:7 * P], k1[:, cs], stop=False, w=[bank_free[ob], b1])
                y = mm(ps[:, ob, :], fold[:, 7 * P:8 * P], t2[:, cs], start=False, w=[b2])
                xx = dve(V.tensor_tensor, X[:, cs], X[:, cs], ps[:, ob, :], ALU.add, w=[y])
                bank_free[ob] = xx
                out.append(xx)
            return out

        DFT = {"dft_k1": K("dft_k1"), "dft_k2": K("dft_k2"), "dft_v2": K("dft_v2"), "dft_v1": K("dft_v1")}

        def l1_ffn(x_ready):
            start_stage()
            h = arena.take(TOKENS)
            done = layernorm(X, h, "eps5", x_ready, work=(arena.take(TOKENS), arena.take(TOKENS)))
            relu = [arena.take(4 * CHUNK) for _ in range(2)]
            y, mem, u, acc = (arena.take(TOKENS) for _ in range(4))
            out = []
            rl_read = [None, None]
            for c in range(NCHUNK):
                cs = slice(c * CHUNK, (c + 1) * CHUNK)
                k = c % 2
                sq = []
                for j in range(4):
                    p1 = mm(ps[:, j, :], wp("L1f", "fcT")[:, j * P:(j + 1) * P], h[:, cs],
                            w=[bank_free[j], done[c], loads["L1f"]])
                    js = slice(j * CHUNK, (j + 1) * CHUNK)
                    r = act(S.activation, relu[k][:, js], ps[:, j, :], ACT.Relu, w=[p1, rl_read[k]])
                    bank_free[j] = r
                    sq.append(act(S.activation, relu[k][:, js], relu[k][:, js], ACT.Square, w=[r]))
                ob = 4 + c % 2
                for j in range(4):
                    yy = mm(ps[:, ob, :], wp("L1f", "projT")[:, j * P:(j + 1) * P], relu[k][:, j * CHUNK:(j + 1) * CHUNK],
                            start=j == 0, stop=j == 3, w=[sq[j], bank_free[ob]])
                rl_read[k] = yy
                d = act(S.activation, y[:, cs], ps[:, ob, :], ACT.Copy, w=[yy])
                bank_free[ob] = d
                d = dve(V.tensor_scalar, mem[:, cs], y[:, cs], -1.0, None, ALU.mult, w=[d])
                a = dve(V.tensor_scalar, acc[:, cs], mem[:, cs], -1.0, None, ALU.is_lt, w=[d])
                for s_ in range(SPIKE_STEPS - 1):
                    d = dve(V.scalar_tensor_tensor, u[:, cs], mem[:, cs], BETA, y[:, cs], ALU.mult, ALU.subtract, w=[d])
                    d = dve(V.scalar_tensor_tensor, mem[:, cs], mem[:, cs], -1.0, u[:, cs], ALU.is_lt, ALU.add, w=[d])
                    a = dve(V.scalar_tensor_tensor, acc[:, cs], mem[:, cs], -1.0, acc[:, cs], ALU.is_lt, ALU.add, w=[d, a])
                out.append(dve(V.scalar_tensor_tensor, X[:, cs], acc[:, cs], 0.5 / SPIKE_STEPS, X[:, cs], ALU.mult, ALU.add, w=[a]))
            return out

        def small_heads_project(group, m_count, h, b, qp, kp, va, h_ready, free, bias, brow):
            bs = slice(b * SEQ, (b + 1) * SEQ)
            ready, n = [], m_count * GROUPS

            def block(i, what):
                bank = i % 2
                dst = (qp if what == "q" else kp)[:, i, :]
                m = mm(ps[:, bank, 0:SEQ], wp(group, "w" + what)[:, i * P:(i + 1) * P], h[:, bs],
                       w=[bank_free[bank], loads[group]] + h_ready)
                e = act(S.activation, dst, ps[:, bank, 0:SEQ], ACT.Identity, bias=C(f"{bias}_b{what}{i}"), w=[m] + free)
                bank_free[bank] = e
                ready.append(e)

            def values(t):
                bank = t
                cols_v = m_count * P
                mm(ps[:, bank, 0:cols_v], h[:, b * SEQ + t * P:b * SEQ + (t + 1) * P], wp(group, "wv"), stop=False,
                   w=[bank_free[bank]])
                m = mm(ps[:, bank, 0:cols_v], rows[0:1, 0:P], brow, start=False, w=[loads["rows"]])
                e = act(S.activation, va[:, t, :, 0:KD], ps[:, bank, 0:cols_v].rearrange("p (h d) -> p h d", d=KD),
                        ACT.Copy, w=[m] + free)
                bank_free[bank] = e
                ready.append(e)

            steps = [lambda i=i, x=x: block(i, x) for i in range(n) for x in ("q", "k")]
            return steps + [lambda t=t: values(t) for t in range(2)], ready

        def l1_attn(x_ready):
            start_stage()
            h = arena.take(TOKENS)
            done = layernorm(X, h, "eps5", x_ready, work=(arena.take(TOKENS), arena.take(TOKENS)))
            qp, kp = ([arena.take(GROUPS * SEQ).rearrange("p (g s) -> p g s", g=GROUPS) for _ in range(2)] for _ in range(2))
            va = [arena.take(2 * HEADS * 9).rearrange("p (t h d) -> p t h d", t=2, h=HEADS) for _ in range(2)]
            ctxT = [arena.take(SEQ) for _ in range(2)]
            att = Attention(HEADS, KD, float(1.0 / np.sqrt(np.float32(KD))), (0, SEQ), ((0, SEQ), (P, P)),
                            (causal_q, causal_q), (causal_k, causal_k), HEADS)
            for v in va:
                ones = dve(V.memset, v[:, :, :, KD:KD + 1], 1.0)
            out = [None] * BATCH
            seq_read = [None, None]
            ct_read = [None, None]

            def head(t):
                return lambda h: t[32 * (h % 4):32 * (h % 4) + KD, h // 4, :]

            def finish(b, hd, o):
                tr = att.normalise(b, o)
                cp = act(S.activation, ctxT[b % 2], ps[:, 7, 0:SEQ], ACT.Copy, w=[tr, ct_read[b % 2]])
                y = mm(ps[:, 7, SEQ:2 * SEQ], wp("L1a", "wo"), ctxT[b % 2], w=[cp])
                ct_read[b % 2] = y
                bs = slice(b * SEQ, (b + 1) * SEQ)
                out[b] = dve(V.scalar_tensor_tensor, X[:, bs], ps[:, 7, SEQ:2 * SEQ], C("L1_bo"), X[:, bs],
                             ALU.add, ALU.add, w=[y])
                bank_free[7] = out[b]

            prev = []
            for b in range(BATCH + 1):
                steps1, nxt = [], []
                if b < BATCH:
                    i = b % 2
                    free = [seq_read[i], ones] if seq_read[i] is not None else [ones]
                    st, rd = small_heads_project("L1a", 1, h, b, qp[i], kp[i], va[i], [done[b // 2]], free, "L1",
                                                 rows[0:1, P + 2 * P:P + 3 * P])
                    steps1 = st + att.pass1(b, head(qp[i]), head(kp[i]), rd)
                    j = i
                    nxt = att.pass2(b, head(qp[j]), head(kp[j]), lambda kt, hh_, j=j: va[j][:, kt, hh_, :], rd, finish)
                interleave(steps1, prev)
                if b > 0:
                    seq_read[(b - 1) % 2] = att.pt_read[(att.unit - 1) % 2]
                prev = nxt
            return [out[2 * c + 1] for c in range(NCHUNK)]

        def l2_ffn(x_ready):
            start_stage()
            mm(ps[:, 7, 0:P], K("ident"), wp("L2", "fT"), stop=False, w=[bank_free[7], loads["L2"]])
            m = mm(ps[:, 7, 0:P], low[:, 0:P], low[:, P:2 * P], start=False, w=[loads["low"]])
            wf = fold[:, 8 * P:9 * P]
            f = act(S.activation, wf, ps[:, 7, 0:P], ACT.Copy, w=[m])
            half_b = arena.take(1)
            hb = act(S.mul, half_b, C("L2_b"), 0.5, w=[loads["cols"]])
            bank_free[7] = f
            h = arena.take(TOKENS)
            done = layernorm(X, h, "eps5", x_ready, work=(arena.take(TOKENS), arena.take(TOKENS)))
            y = arena.take(TOKENS)
            out = []
            for c in range(NCHUNK):
                cs = slice(c * CHUNK, (c + 1) * CHUNK)
                b = 2 * c
                m = mm(ps[:, b, :], wf, h[:, cs], w=[bank_free[b], done[c], f])
                e = act(S.activation, y[:, cs], ps[:, b, :], ACT.Identity, bias=half_b, scale=0.5, w=[m, hb])
                bank_free[b] = e
                out.append(dve(V.tensor_tensor, X[:, cs], X[:, cs], y[:, cs], ALU.add, w=[e]))
            return out

        TWO_PI = 6.283185307179586
        HI = float(np.float32(6.28125))
        MIDP = float(np.float32(TWO_PI - HI))
        LOP = float(np.float32(TWO_PI - HI - MIDP))
        MAGIC = 12582912.0
        PI = float(np.nextafter(np.float32(np.pi), np.float32(0)))

        def sines(src, sin_out, cos_out, k, r, ready):
            last = []
            for o, quarter in ((sin_out, 0.0), (cos_out, 0.25)):
                a = dve(V.tensor_scalar, k, src, 1.0 / TWO_PI, quarter, ALU.mult, ALU.add, w=ready + last)
                a = dve(V.tensor_scalar, k, k, MAGIC, -MAGIC, ALU.add, ALU.add, w=[a])
                a = dve(V.scalar_tensor_tensor, r, k, -HI, src, ALU.mult, ALU.add, w=[a] + last)
                a = dve(V.scalar_tensor_tensor, r, k, -MIDP, r, ALU.mult, ALU.add, w=[a])
                a = dve(V.scalar_tensor_tensor, r, k, -LOP, r, ALU.mult, ALU.add, w=[a])
                if quarter:
                    a = dve(V.tensor_scalar, r, r, TWO_PI / 4, None, ALU.add, w=[a])
                a = dve(V.tensor_scalar, r, r, PI, -PI, ALU.min, ALU.max, w=[a])
                last = [act(S.activation, o, r, ACT.Sin, w=[a])]
            return last[0]

        def l2_attn(x_ready):
            start_stage()
            h = arena.take(TOKENS)
            work = (arena.take(TOKENS), arena.take(TOKENS))
            done = layernorm(X, h, "eps5", x_ready, work=work)
            phi, cphi, sphi, kq, rq = (arena.take(SEQ) for _ in range(5))
            keep = arena.take(CHUNK)
            kp = dve(V.memset, keep, 1.0)
            kp = dve(V.memset, seqs(keep)[:, :, 0:1], 0.0, w=[kp])
            a = dve(V.tensor_scalar, phi, K("pos"), C("ph"), None, ALU.mult, w=[loads["const"], loads["cols"]])
            phi_done = dve(V.tensor_scalar, phi, phi, 0.01, None, ALU.mult, w=[a])
            trig = sines(phi, sphi, cphi, kq, rq, [phi_done])
            w1 = arena.take(4 * FF).rearrange("p (i f) -> p i f", i=4)
            bias1 = arena.take(2)
            for i in range(4):
                g_ = dve(V.tensor_scalar, w1[:, i, :], wp("L2", "w1T")[:, i * FF:(i + 1) * FF], C(f"L2_lg{i}"), None, ALU.mult,
                         w=[loads["L2"], loads["cols"]])
            for o in range(2):
                for i in range(4):
                    m = mm(ps[:, 7, o:o + 1], wp("L2", "w1T")[:, i * FF + o * P:i * FF + (o + 1) * P], C(f"L2_lb{i}"),
                           start=i == 0, stop=i == 3, w=[bank_free[7], loads["L2"], loads["cols"]])
            for o in range(2):
                bb = dve(V.tensor_tensor, bias1[:, o:o + 1], ps[:, 7, o:o + 1], C(f"L2_b1_{o}"), ALU.add, w=[m])
            bank_free[7] = bb
            n = CHUNK
            mag, wx, tr, ti, mr, mi, am, pq, sq_, cq, k_, r_ = (arena.take(n) for _ in range(12))
            ctxb = arena.take(4 * n).rearrange("p (i s) -> p i s", i=4)
            sqb = work[0].rearrange("p (i s) -> p i s", i=4)
            hb = arena.take(2 * n).rearrange("p (i s) -> p i s", i=2)
            five = arena.take(1)
            out = []
            TT = V.tensor_tensor
            prev = []
            for c in range(NCHUNK):
                cs = slice(c * CHUNK, (c + 1) * CHUNK)
                hc = h[:, cs]
                pm = mm(ps[:, 0, :], wp("L2", "magT"), hc, w=[bank_free[0], done[c], loads["L2"]])
                pq_ = mm(ps[:, 1, :], wp("L2", "qT"), hc, w=[bank_free[1]])
                sg = act(S.activation, mag, ps[:, 0, :], ACT.Sigmoid, bias=C("bmag"), w=[pm] + prev)
                bank_free[0] = sg
                mg = dve(V.tensor_scalar, mag, mag, 5.0, None, ALU.mult, w=[sg])
                wxd = dve(TT, wx, mag, hc, ALU.mult, w=[mg])
                trd = dve(TT, seqs(tr), seqs(wx), table(cphi), ALU.mult, w=[wxd, trig])
                tid = dve(TT, seqs(ti), seqs(wx), table(sphi), ALU.mult)
                a1 = dve(V.tensor_tensor_scan, mr, keep, tr, 0.0, ALU.mult, ALU.add, w=[trd, kp])
                a2 = dve(V.tensor_tensor_scan, mi, keep, ti, 0.0, ALU.mult, ALU.add, w=[tid])
                a3 = dve(V.tensor_tensor_scan, am, keep, mag, 0.0, ALU.mult, ALU.add)
                rt = act(S.activation, am, am, ACT.Sqrt, bias=C("eps8"), w=[a3])
                iv = dve(V.reciprocal, am, am, w=[rt])
                a1 = dve(TT, mr, mr, am, ALU.mult, w=[iv, a1])
                a2 = dve(TT, mi, mi, am, ALU.mult, w=[a2])
                q1 = dve(V.tensor_scalar, pq, ps[:, 1, :], C("bq"), None, ALU.add, w=[pq_] + prev)
                bank_free[1] = q1
                q2 = dve(TT, seqs(pq), seqs(pq), table(phi), ALU.add, w=[q1])
                sc = sines(pq, sq_, cq, k_, r_, [q2])
                b1 = dve(TT, ctxb[:, 2, :], mr, cq, ALU.mult, w=[sc, a1] + prev)
                b2 = dve(TT, k_, mi, sq_, ALU.mult, w=[a2])
                b3 = dve(TT, ctxb[:, 3, :], mi, cq, ALU.mult)
                b4 = dve(TT, r_, mr, sq_, ALU.mult)
                b1 = dve(TT, ctxb[:, 2, :], ctxb[:, 2, :], k_, ALU.add, w=[b1, b2])
                b3 = dve(TT, ctxb[:, 3, :], ctxb[:, 3, :], r_, ALU.subtract, w=[b3, b4])
                b5 = pool(G.tensor_tensor, seqs(ctxb[:, 0, :]), seqs(hc), table(cphi), ALU.mult, w=[trig, done[c]] + prev)
                b6 = pool(G.tensor_tensor, seqs(ctxb[:, 1, :]), seqs(hc), table(sphi), ALU.mult)
                cd = [b6, b6, b1, b3]
                for i in range(4):
                    m = mm(ps[:, 2, :], K("mean"), ctxb[:, i, :], start=i == 0, stop=i == 3, w=[bank_free[2], cd[i], cd[0]])
                mean = act(S.mul, wx, ps[:, 2, :], 0.25, w=[m, tid])
                bank_free[2] = mean
                for i in range(4):
                    cdi = dve(TT, ctxb[:, i, :], ctxb[:, i, :], wx, ALU.subtract, w=[mean])
                    s = act(S.activation, sqb[:, i, :], ctxb[:, i, :], ACT.Square, w=[cdi, done[-1]] + prev)
                    m = mm(ps[:, 3, :], K("mean"), sqb[:, i, :], start=i == 0, stop=i == 3, w=[bank_free[3], s])
                rt = act(S.activation, am, ps[:, 3, :], ACT.Sqrt, bias=C("eps5"), scale=0.25, w=[m, a2, b1])
                bank_free[3] = rt
                iv = dve(V.reciprocal, am, am, w=[rt])
                for i in range(4):
                    cdi = dve(TT, ctxb[:, i, :], ctxb[:, i, :], am, ALU.mult, w=[iv])
                for o in range(2):
                    for i in range(4):
                        m = mm(ps[:, 4 + o, :], w1[:, i, o * P:(o + 1) * P], ctxb[:, i, :], start=i == 0, stop=i == 3,
                               w=[bank_free[4 + o], cdi, g_])
                    ge = act(S.activation, hb[:, o, :], ps[:, 4 + o, :], ACT.Gelu, bias=bias1[:, o:o + 1], w=[m, bb])
                    bank_free[4 + o] = ge
                for o in range(2):
                    m = mm(ps[:, 6, :], wp("L2", "w2T")[:, o * P:(o + 1) * P], hb[:, o, :], start=o == 0, stop=o == 1,
                           w=[bank_free[6], ge])
                a = dve(V.scalar_tensor_tensor, mag, ps[:, 6, :], C("L2_b2"), hc, ALU.add, ALU.add, w=[m])
                bank_free[6] = a
                a = dve(TT, X[:, cs], X[:, cs], mag, ALU.add, w=[a])
                prev = [a, m]
                out.append(a)
            return out

        def l3_attn(x_ready):
            start_stage()
            h = arena.take(TOKENS)
            work = (arena.take(TOKENS), arena.take(TOKENS))
            wg = fold[:, 0:3 * P]
            g = dve(V.tensor_scalar, wg, wp("L3a", "qkvaT"), C("gamma"), float(np.float32(np.sqrt(P))), ALU.mult, ALU.mult,
                    w=[loads["L3a"], loads["cols"]])
            done = layernorm(X, h, "eps5", x_ready, work=work)
            sq, sd = work
            a_, kv, q, cum = (arena.take(TOKENS) for _ in range(4))
            out = []
            for c in range(NCHUNK):
                cs = slice(c * CHUNK, (c + 1) * CHUNK)
                s = act(S.activation, sq[:, cs], h[:, cs], ACT.Square, w=[done[c]])
                m = mm(ps[:, 7, :], K("mean"), sq[:, cs], w=[s, bank_free[7]])
                rt = act(S.activation, sd[:, cs], ps[:, 7, :], ACT.Sqrt, scale=float(P), bias=C("zero"), w=[m])
                bank_free[7] = rt
                cl = dve(V.tensor_scalar, sd[:, cs], sd[:, cs], 1e-12, None, ALU.max, w=[rt])
                iv = dve(V.reciprocal, sd[:, cs], sd[:, cs], w=[cl])
                xn = dve(V.tensor_tensor, h[:, cs], h[:, cs], sd[:, cs], ALU.mult, w=[iv])
                k = 3 * (c % 2)
                for j in range(3):
                    m = mm(ps[:, k + j, :], wg[:, j * P:(j + 1) * P], h[:, cs], w=[bank_free[k + j], xn, g])
                sg = act(S.activation, a_[:, cs], ps[:, k + 2, :], ACT.Sigmoid, w=[m])
                e1 = act(S.activation, kv[:, cs], ps[:, k + 1, :], ACT.Copy)
                bank_free[k + 2] = bank_free[k + 1] = e1
                z = pool(G.memset, seqs(a_[:, cs])[:, :, 0:1], 0.0, w=[sg])
                cu = dve(V.tensor_tensor_scan, cum[:, cs], a_[:, cs], kv[:, cs], 0.0, ALU.mult, ALU.add, w=[z, e1])
                pq = dve(V.tensor_tensor, q[:, cs], cum[:, cs], ps[:, k, :], ALU.mult, w=[cu])
                bank_free[k] = pq
                out.append(dve(V.tensor_tensor, X[:, cs], X[:, cs], q[:, cs], ALU.add, w=[pq]))
            return out

        def softmax_small(lg, e, ready, small):
            v = lg.rearrange("p (b e) -> p b e", e=e)
            mx, = (small,)
            a = dve(V.tensor_reduce, mx, v, AXX, ALU.max, w=ready)
            a = dve(V.tensor_tensor, v, v, mx.unsqueeze(2).to_broadcast([P, BATCH, e]), ALU.subtract, w=[a])
            a = act(S.activation, lg, lg, ACT.Exp, w=[a])
            a = dve(V.tensor_reduce, mx, v, AXX, ALU.add, w=[a])
            a = dve(V.reciprocal, mx, mx, w=[a])
            return dve(V.tensor_tensor, v, v, mx.unsqueeze(2).to_broadcast([P, BATCH, e]), ALU.mult, w=[a])

        def route(n_, lo, e, lg, ready, rep, mean, small):
            a = dve(V.tensor_reduce, mean, seqs(n_, BATCH), AXX, ALU.add, w=ready)
            a = dve(V.tensor_scalar, mean, mean, 1.0 / SEQ, None, ALU.mult, w=[a])
            r = dve(V.tensor_copy, rep[:, 0:e, :], wp("L3m", "rw")[:, lo:lo + e].unsqueeze(2).to_broadcast([P, e, P]),
                    w=ready + [loads["L3m"]])
            for i in range(e):
                m = mm(ps[:, 7, i * BATCH:(i + 1) * BATCH], rep[:, i, :], mean, w=[bank_free[7], a, r])
            v = lg.rearrange("p (b e) -> p b e", e=e)
            d = dve(V.tensor_tensor, v, ps[:, 7, 0:e * BATCH].rearrange("p (e b) -> p b e", e=e),
                    wp("L3m", "rb")[:, lo:lo + e].unsqueeze(1).to_broadcast([P, BATCH, e]), ALU.add, w=[m])
            bank_free[7] = d
            return softmax_small(lg, e, [d], small)

        def l3_ffn(x_ready):
            start_stage()
            work = (arena.take(TOKENS), arena.take(TOKENS))
            n1 = arena.take(TOKENS)
            done = layernorm(X, X0, "eps5", x_ready, work=work)
            done = layernorm(X0, n1, "eps6", done, "ln1_g", "ln1_b", work)
            qp, kp = ([arena.take(8 * SEQ).rearrange("p (g s) -> p g s", g=8) for _ in range(2)] for _ in range(2))
            nh = M_EXPERTS * HEADS
            va = [arena.take(2 * nh * 9).rearrange("p (t h d) -> p t h d", t=2, h=nh) for _ in range(2)]
            ctxT = [arena.take(SEQ) for _ in range(2)]
            rep = work[0][:, 0:EXPERTS * P].rearrange("p (e c) -> p e c", e=EXPERTS)
            mean, small, bop = (arena.take(BATCH) for _ in range(3))
            mp = probs[:, 0:M_EXPERTS * BATCH]
            mp_done = route(n1, 0, M_EXPERTS, mp, done, rep, mean, small)
            mpv = mp.rearrange("p (b e) -> p b e", e=M_EXPERTS)
            a = dve(V.tensor_scalar, bop, mpv[:, :, 0:1].rearrange("p b e -> p (b e)"), C("bo0"), None, ALU.mult, w=[mp_done])
            bop_done = dve(V.scalar_tensor_tensor, bop, mpv[:, :, 1:2].rearrange("p b e -> p (b e)"), C("bo1"), bop,
                           ALU.mult, ALU.add, w=[a])
            att = Attention(nh, KD, float(1.0 / np.sqrt(np.float32(KD))), (0, SEQ), ((0, SEQ), (0, SEQ)), (), (), HEADS)
            for v in va:
                ones = dve(V.memset, v[:, :, :, KD:KD + 1], 1.0)
            out = [None] * BATCH
            seq_read, ct_read, ct_done = [None, None], [None, None], [None, None]

            def head(t):
                return lambda h: t[32 * (h % 4):32 * (h % 4) + KD, h // 4, :]

            def finish(b, hd, o):
                m = hd // HEADS
                tr = att.normalise(m, o, mp[:, b * M_EXPERTS + m:b * M_EXPERTS + m + 1])
                cp = act(S.activation, ctxT[m], ps[:, 7, 0:SEQ], ACT.Copy, w=[tr, ct_read[m]])
                ct_done[m] = cp
                bank_free[7] = cp
                if m == M_EXPERTS - 1:
                    for j in range(M_EXPERTS):
                        y = mm(ps[:, 7, SEQ:2 * SEQ], wp("L3m", "wo")[:, j * P:(j + 1) * P], ctxT[j], start=j == 0,
                               stop=j == M_EXPERTS - 1, w=ct_done)
                    ct_read[0] = ct_read[1] = y
                    bs = slice(b * SEQ, (b + 1) * SEQ)
                    out[b] = dve(V.scalar_tensor_tensor, X0[:, bs], ps[:, 7, SEQ:2 * SEQ], bop[:, b:b + 1], X0[:, bs],
                                 ALU.add, ALU.add, w=[y, bop_done])
                    bank_free[7] = out[b]

            prev = []
            for b in range(BATCH + 1):
                steps1, nxt = [], []
                if b < BATCH:
                    i = b % 2
                    free = [seq_read[i], ones] if seq_read[i] is not None else [ones]
                    st, rd = small_heads_project("L3m", M_EXPERTS, n1, b, qp[i], kp[i], va[i], [done[b // 2]], free, "L3",
                                                 rows[0:1, P:P + 2 * P])
                    steps1 = st + att.pass1(b, head(qp[i]), head(kp[i]), rd)
                    nxt = att.pass2(b, head(qp[i]), head(kp[i]), lambda kt, hh_, j=i: va[j][:, kt, hh_, :], rd, finish)
                interleave(steps1, prev)
                if b > 0:
                    seq_read[(b - 1) % 2] = att.pt_read[(att.unit - 1) % 2]
                prev = nxt
            x1 = [out[2 * c + 1] for c in range(NCHUNK)]

            start_stage()
            work = (arena.take(TOKENS), arena.take(TOKENS))
            n2 = arena.take(TOKENS)
            rep = work[0][:, 0:EXPERTS * P].rearrange("p (e c) -> p e c", e=EXPERTS)
            mean, small = (arena.take(BATCH) for _ in range(2))
            done = layernorm(X0, n2, "eps6", x1, "ln2_g", "ln2_b", work)
            ep = probs[:, 0:EXPERTS * BATCH]
            pv_ = ep.rearrange("p (b e) -> p b e", e=EXPERTS)
            epd = route(n2, M_EXPERTS, EXPERTS, ep, done, rep, mean, small)
            gt = arena.take(BATCH * EXPERTS * EXPERTS).rearrange("p (b e f) -> p b e f", b=BATCH, e=EXPERTS)
            eq = arena.take(BATCH * EXPERTS * EXPERTS).rearrange("p (b e f) -> p b e f", b=BATCH, e=EXPERTS)
            rank = arena.take(BATCH * EXPERTS)
            rv = rank.rearrange("p (b e) -> p b e", e=EXPERTS)
            for b in range(BATCH):
                mine = pv_[:, b, :].unsqueeze(2).to_broadcast([P, EXPERTS, EXPERTS])
                other = pv_[:, b, :].unsqueeze(1).to_broadcast([P, EXPERTS, EXPERTS])
                g1 = dve(V.tensor_tensor, gt[:, b], other, mine, ALU.is_gt, w=[epd])
                g2 = dve(V.tensor_tensor, eq[:, b], other, mine, ALU.is_equal)
                g2 = dve(V.tensor_tensor, eq[:, b], eq[:, b], K("earlier").rearrange("p (e f) -> p e f", e=EXPERTS), ALU.mult, w=[g2])
                g1 = dve(V.tensor_tensor, gt[:, b], gt[:, b], eq[:, b], ALU.add, w=[g1, g2])
                g1 = dve(V.tensor_reduce, rv[:, b, :], gt[:, b], AXX, ALU.add, w=[g1])
            g1 = dve(V.scalar_tensor_tensor, ep, rank, float(TOP_K), ep, ALU.is_lt, ALU.mult, w=[g1])
            g1 = dve(V.tensor_reduce, small, pv_, AXX, ALU.add, w=[g1])
            g1 = dve(V.reciprocal, small, small, w=[g1])
            gate = dve(V.tensor_tensor, pv_, pv_, small.unsqueeze(2).to_broadcast([P, BATCH, EXPERTS]), ALU.mult, w=[g1])
            hb = [arena.take(2 * CHUNK).rearrange("p (f s) -> p f s", f=2) for _ in range(2)]
            hb_read = [None, None]
            out = []
            for c in range(NCHUNK):
                cs = slice(c * CHUNK, (c + 1) * CHUNK)
                ob = 6 + c % 2

                def up(e):
                    u = e % 2
                    w_ = []
                    for f in range(2):
                        bk = 2 * u + f
                        m = mm(ps[:, bk, :], wp("L3e", "fw1")[:, e * FF + f * P:e * FF + (f + 1) * P], n2[:, cs],
                               w=[bank_free[bk], done[c], loads["L3e"]])
                    ge = act(S.activation, hb[u], ps[:, 2 * u:2 * u + 2, :], ACT.Gelu, w=[m, hb_read[u]])
                    bank_free[2 * u] = bank_free[2 * u + 1] = ge
                    for bb in range(PER):
                        b = c * PER + bb
                        s = hb[u][:, :, bb * SEQ:(bb + 1) * SEQ]
                        g = dve(V.tensor_scalar, s, s, ep[:, b * EXPERTS + e:b * EXPERTS + e + 1], None, ALU.mult, w=[ge, gate])
                    return g

                def down(e, g):
                    u = e % 2
                    for f in range(2):
                        m = mm(ps[:, ob, :], wp("L3e", "fw2")[:, (2 * e + f) * P:(2 * e + f + 1) * P], hb[u][:, f, :],
                               start=(e == 0 and f == 0), stop=(e == EXPERTS - 1 and f == 1), w=[g, bank_free[ob]])
                    hb_read[u] = m
                    return m

                g = up(0)
                for e in range(EXPERTS):
                    g2 = up(e + 1) if e + 1 < EXPERTS else None
                    m = down(e, g)
                    g = g2
                a = dve(V.tensor_tensor, X0[:, cs], X0[:, cs], ps[:, ob, :], ALU.add, w=[m])
                bank_free[ob] = a
                out.append(dve(V.scalar_tensor_tensor, X[:, cs], X0[:, cs], 0.5, X[:, cs], ALU.mult, ALU.add, w=[a]))
            return out

        order = [l0_ffn, l0_attn, l0_ffn, l1_ffn, l1_attn, l1_ffn, l2_ffn, l2_attn, l2_ffn, l3_ffn, l3_attn, l3_ffn]
        for s in stages:
            x_ready = order[s](x_ready)

        stored = pr.sem("stored")
        for c in range(NCHUNK):
            x_ready[c].waited_for = True
        sems = {}
        for q in pr.engines:
            q.count(sems)

        with nc.Block() as block:
            @block.sync
            def _(eng):
                sp.emit(eng)
                for c in range(NCHUNK):
                    cs = slice(c * CHUNK, (c + 1) * CHUNK)
                    eng.wait_ge(x_ready[c].sem, x_ready[c].value)
                    eng.dma_start(out[:, cs], X[:, cs]).then_inc(stored, 16)
                eng.wait_ge(stored, 16 * NCHUNK)
                for t in loads.values():
                    eng.wait_ge(t.sem, t.value)

            @block.tensor
            def _(eng):
                pe.emit(eng)

            @block.scalar
            def _(eng):
                act.emit(eng)

            @block.vector
            def _(eng):
                dve.emit(eng)

            @block.gpsimd
            def _(eng):
                pool_queue.emit(eng)


def constants():
    c = {}
    eye = np.eye(P)
    c["ident"], c["mean"] = eye, np.full((P, P), 1.0 / P)
    c["center"] = eye - 1.0 / P
    i, j = np.arange(P)[:, None], np.arange(P)[None, :]
    c["causal_q"] = np.where(j > i, MASKED, 0.0)
    c["causal_k"] = c["causal_q"].T
    q, k = P + i, WINDOW + np.arange(3 * WINDOW)[None, :]
    c["local_q1"] = np.where((q < k) | (q > k + WINDOW), MASKED, 0.0)
    q, k = np.arange(3 * WINDOW)[None, :], i
    c["local_k0"] = np.where((q < k) | (q > k + WINDOW), MASKED, 0.0)
    c["negsel"] = np.where(i % 32 == np.arange(32)[None, :], -1.0, 0.0)
    f4 = np.float32
    half = np.arange(0, L0_DIM, 2, dtype=f4)
    inv_freq = (f4(1.0) / f4(10000.0) ** (half / f4(L0_DIM))).astype(f4)
    t = np.arange(SEQ, dtype=f4)
    fr = (t[:, None] * inv_freq[None, :]).astype(f4)
    fr = np.concatenate([fr, fr], -1).astype(np.float64)
    base = (half + f4(0.4 * L0_DIM)) / f4(1.4 * L0_DIM)
    power = (t - SEQ // 2) / f4(WINDOW // 2)
    sc = base.astype(np.float64)[None, :] ** power.astype(np.float64)[:, None]
    sc = np.concatenate([sc, sc], -1)
    sign = np.where(np.arange(L0_DIM) < L0_DIM // 2, -1.0, 1.0)
    two = lambda a: np.concatenate([a.T, a.T], 0)
    c["cos_q"], c["sin_q"] = two(8.0 * np.cos(fr) * sc), two(8.0 * np.sin(fr) * sc * sign)
    c["cos_k"], c["sin_k"] = two(np.cos(fr) / sc), two(np.sin(fr) / sc * sign)
    c["pos"] = np.broadcast_to(t, (P, SEQ))
    hs = np.zeros((P, 8, 16))
    for b in range(8):
        for hh in range(2):
            hs[64 * hh:64 * hh + 64, b, 2 * b + hh] = 1.0
    c["headsum"] = hs.reshape(P, P)
    n = np.arange(16)
    re = np.array([np.cos(2 * np.pi * f * n / 16) for f in range(9)])
    im = np.array([-np.sin(2 * np.pi * f * n / 16) for f in range(9)])
    d = {x: np.zeros((P, P)) for x in ("dft_k1", "dft_k2", "dft_v1", "dft_v2", "idft1", "idft2")}
    for h in range(8):
        r = slice(16 * h, 16 * h + 16)
        for f in range(8):
            a, b = 8 * h + f, 64 + 8 * h + f
            d["dft_k1"][r, a], d["dft_k1"][r, b] = re[f], (re[8] if f == 0 else im[f])
            if f:
                d["dft_k2"][r, a], d["dft_k2"][r, b] = -im[f], re[f]
                d["dft_v1"][r, a], d["dft_v1"][r, b] = re[f], re[f]
                d["dft_v2"][r, a], d["dft_v2"][r, b] = im[f], im[f]
                cr, ci = 2 * np.cos(2 * np.pi * f * n / 16) / 16, -2 * np.sin(2 * np.pi * f * n / 16) / 16
                d["idft1"][r, a], d["idft1"][r, b] = cr, ci
                d["idft2"][r, a], d["idft2"][r, b] = -ci, cr
            else:
                d["dft_v1"][r, a], d["dft_v1"][r, b] = re[0], re[8]
                d["idft1"][r, a], d["idft1"][r, b] = 1.0 / 16, re[8] / 16
    c.update(d)
    c["earlier"] = np.broadcast_to((np.arange(8)[None, :] < np.arange(8)[:, None]).astype(float).reshape(1, 64), (P, 64))
    return c


def layout(a):
    f = np.float32
    a = {k: np.asarray(v) for k, v in a.items()}
    col = {}
    g = {}
    rot = np.concatenate([np.arange(32, 64), np.arange(0, 32)])
    for l in range(DEPTH):
        qs, ks = a["L0_ffn_q_scale"][l], a["L0_ffn_k_scale"][l]
        col[f"L0_qs{l}"], col[f"L0_qsr{l}"] = np.tile(qs, 2), np.tile(qs[rot], 2)
        col[f"L0_ks{l}"], col[f"L0_ksr{l}"] = np.tile(ks, 2), np.tile(ks[rot], 2)
        col[f"L0_lg{l}"], col[f"L0_lb{l}"], col[f"L0_b2{l}"] = a["L0_ffn_ln_g"][l], a["L0_ffn_ln_b"][l], a["L0_ffn_b2"][l]
        for half in range(2):
            for j, (at, n) in enumerate(HID_BLOCKS):
                v = np.zeros(P, f)
                v[:n] = a["L0_ffn_b1"][l][half * HID + at:half * HID + at + n]
                col[f"L0_b1{l}_{3 * half + j}"] = v
        wq = a["L0_ffn_wqkv"][l]
        wr = wq[:, :2 * INNER].reshape(P, 16, 64)[:, :, rot].reshape(P, 2 * INNER)
        wo = a["L0_ffn_wo"][l].reshape(4, P, P).transpose(1, 0, 2).reshape(P, INNER)
        w2 = np.zeros((3 * P, P), f)
        w2[:HID] = a["L0_ffn_w2"][l]
        w2 = w2.reshape(3, P, P).transpose(1, 0, 2).reshape(P, 3 * P)
        g[f"L0f{l}"] = [wq, wr, wo, a["L0_ffn_w1"][l], w2]
    w = a["L0_attn_w_qkv"]
    g["L0a"] = [w[:, :P].T, w[:, P:2 * P].T, w[:, 2 * P:].T, a["L0_attn_w_out"]]
    g["L1f"] = [a["L1_ffn_W_fc"].T, a["L1_ffn_W_proj"].T.reshape(4, P, P).transpose(1, 0, 2).reshape(P, 4 * P)]

    def spread(w_):
        n = w_.shape[0]
        o = np.zeros((n, GROUPS, 4, 32), f)
        o[..., :KD] = w_.reshape(n, GROUPS, 4, KD)
        return o.reshape(n, GROUPS * P)

    w, bq = a["L1_attn_w_qkv"], a["L1_attn_b_qkv"]
    g["L1a"] = [spread(w[:, :P]), spread(w[:, P:2 * P]), w[:, 2 * P:], a["L1_attn_w_out"]]
    for i, v in enumerate(spread(bq[None, :P]).reshape(GROUPS, P)):
        col[f"L1_bq{i}"] = v
    for i, v in enumerate(spread(bq[None, P:2 * P]).reshape(GROUPS, P)):
        col[f"L1_bk{i}"] = v
    col["L1_bo"] = a["L1_attn_b_out"]
    col["L2_b"], col["ph"], col["bmag"], col["bq"] = a["L2_ffn_b"], a["L2_attn_random_phases"], a["L2_attn_b_mag"], a["L2_attn_b_q"]
    for i in range(4):
        col[f"L2_lg{i}"], col[f"L2_lb{i}"] = a["L2_attn_ln_g"][i * P:(i + 1) * P], a["L2_attn_ln_b"][i * P:(i + 1) * P]
    col["L2_b1_0"], col["L2_b1_1"], col["L2_b2"] = a["L2_attn_b1"][:P], a["L2_attn_b1"][P:], a["L2_attn_b2"]
    w1T = a["L2_attn_W1"].T.reshape(4, P, FF).transpose(1, 0, 2).reshape(P, 4 * FF)
    w2T = a["L2_attn_W2"].T.reshape(2, P, P).transpose(1, 0, 2).reshape(P, 2 * P)
    g["L2"] = [a["L2_ffn_W"].T, a["L2_attn_W_mag"].T, a["L2_attn_W_q"].T, w1T, w2T]
    low = np.concatenate([a["L2_ffn_V_r"].T, a["L2_ffn_C"].T], 1)
    col["gamma"] = a["L3_attn_gamma"]
    g["L3a"] = [a["L3_attn_w_qkva"].T]
    for n in ("ln1_g", "ln1_b", "ln2_g", "ln2_b"):
        col[n] = a[f"L3_ffn_{n}"]
    for x in "qk":
        bias = a[f"L3_ffn_mha_b{x}"].reshape(M_EXPERTS, P)
        for i, v in enumerate(spread(bias).reshape(-1, P)):
            col[f"L3_b{x}{i}"] = v
    col["bo0"], col["bo1"] = a["L3_ffn_mha_bo"]
    perm = lambda w_: w_.reshape(M_EXPERTS, P, P)
    g["L3m"] = [np.concatenate([spread(m) for m in perm(a["L3_ffn_mha_wq"])], 1),
                np.concatenate([spread(m) for m in perm(a["L3_ffn_mha_wk"])], 1),
                np.concatenate(list(perm(a["L3_ffn_mha_wv"])), 1), np.concatenate(list(perm(a["L3_ffn_mha_wo"])), 1),
                a["L3_ffn_mha_rw"], a["L3_ffn_ffn_rw"],
                np.broadcast_to(a["L3_ffn_mha_rb"], (P, M_EXPERTS)), np.broadcast_to(a["L3_ffn_ffn_rb"], (P, EXPERTS))]
    g["L3e"] = [a["L3_ffn_fw1"].transpose(1, 0, 2).reshape(P, EXPERTS * FF),
                a["L3_ffn_fw2"].reshape(EXPERTS, 2, P, P).transpose(2, 0, 1, 3).reshape(P, EXPERTS * FF)]
    col["eps5"], col["eps6"], col["eps8"], col["zero"] = (np.full(P, e) for e in (1e-5, 1e-6, 1e-8, 0.0))
    c = constants()
    headrow = np.zeros((16, 8, P))
    for j in range(8):
        headrow[2 * j, j, 0:64] = headrow[2 * j + 1, j, 64:P] = 1.0
    out = {
        "x": a["L0_attn_x"].reshape(TOKENS, P).T,
        "const": np.concatenate([c[n] for n in CONST], 1),
        "cols": np.stack([col[n] for n in COLUMNS], 1),
        "headrow": headrow.reshape(16, HEADROW_N),
        "rows": np.concatenate([np.ones((1, P)), a["L3_ffn_mha_bv"].reshape(1, -1), bq[None, 2 * P:]], 1),
        "low": low,
    }
    for n, parts in g.items():
        out[n] = np.concatenate(parts, 1)
    return {n: np.ascontiguousarray(v, dtype=f) for n, v in out.items()}


def kernel(**inputs):
    import concourse.bacc as bacc
    from concourse.bass_utils import run_bass_kernel_spmd

    nc = bacc.Bacc("TRN2", target_bir_lowering=False, num_devices=1)
    arrays = layout(inputs)
    ins = {n: nc.dram_tensor(f"in_{n}", v.shape, F32, kind="ExternalInput").ap() for n, v in arrays.items()}
    out = nc.dram_tensor("out", (P, TOKENS), F32, kind="ExternalOutput").ap()
    program(nc, ins, out)
    r = run_bass_kernel_spmd(nc, [{f"in_{n}": v for n, v in arrays.items()}], core_ids=[0])
    return r.results[0]["out"].T.reshape(BATCH, SEQ, P)
```

```python
from contextlib import ExitStack

import numpy as np
import concourse.bass as bass
from concourse import mybir

F32 = mybir.dt.float32
BF16 = mybir.dt.bfloat16
ALU = mybir.AluOpType
ACT = mybir.ActivationFunctionType
AXX = mybir.AxisListType.X

P = 128
BATCH, SEQ = 8, 256
TOKENS = BATCH * SEQ
CHUNK = 512
NCHUNK = TOKENS // CHUNK
PER = CHUNK // SEQ
BANK = 512
BANKS = 8
MASKED = -3.0e38

DEPTH, L0_HEADS, L0_DIM, WINDOW = 2, 8, 64, 64
INNER = L0_HEADS * L0_DIM
HID = int(P * 4 * 2 / 3)
HID_BLOCKS = [(i, min(P, HID - i)) for i in range(0, HID, P)]
SPIKE_HID, SPIKE_STEPS, BETA = 4 * P, 5, 0.9
HEADS, KD = 16, P // 16
M_EXPERTS, EXPERTS, TOP_K, FF = 2, 8, 2, 2 * P
RANK = 32


class Token:

    def __init__(self, stage):
        self.stage, self.waited_for, self.sem, self.value = stage, False, None, None


class Queue:

    def __init__(self, program, name):
        self.program, self.name, self.items, self.last, self.held = program, name, [], None, []

    def __call__(self, method, *args, w=(), **kw):
        token = Token(self.program.stage)
        waits = [t for t in list(w) + self.held if t is not None]
        self.held = []
        for t in waits:
            t.waited_for = True
        self.items.append((method, args, kw, waits, token))
        self.last = token
        return token

    def dma(self, out, in_, sem, w=()):
        token = Token(None)
        sem.value += 16
        token.waited_for, token.sem, token.value = True, sem.sem, sem.value
        waits = [t for t in w if t is not None]
        for t in waits:
            t.waited_for = True
        self.items.append((None, (out, in_), {}, waits, token))
        return token

    def count(self, sems):
        reached = {}
        for _, _, _, _, t in self.items:
            if t.waited_for and t.sem is None:
                key = (self.name, t.stage)
                if key not in sems:
                    sems[key] = self.program.sem(f"{self.name}_stage{t.stage}")
                reached[key] = reached.get(key, 0) + 1
                t.sem, t.value = sems[key], reached[key]

    def emit(self, eng):
        passed = {}
        for method, args, kw, waits, token in self.items:
            for t in waits:
                if passed.get(t.sem.name, 0) < t.value:
                    eng.wait_ge(t.sem, t.value)
                    passed[t.sem.name] = t.value
            if method is None:
                eng.dma_start(*args).then_inc(token.sem, 16)
            else:
                done = method(*args, **kw)
                if token.waited_for:
                    done.then_inc(token.sem, 1)


class Counter:

    def __init__(self, sem):
        self.sem, self.value = sem, 0


class Program:
    def __init__(self, nc, ctx):
        self.nc, self.ctx, self.stage = nc, ctx, 0
        self.pe, self.act, self.dve, self.pool, self.sp = (
            Queue(self, n) for n in ("tensor", "scalar", "vector", "gpsimd", "sync"))
        self.engines = [self.pe, self.act, self.dve, self.pool]

    def sem(self, name):
        return self.ctx.enter_context(self.nc.semaphore(name))

    def counter(self, name):
        return Counter(self.sem(name))

    def sbuf(self, name, shape, dtype=F32):
        return self.ctx.enter_context(self.nc.sbuf_tensor(name, shape, dtype))

    def next_stage(self):
        last = [q.last for q in self.engines if q.last is not None]
        for q in self.engines:
            q.held = q.held + last
        self.stage += 1


class Arena:

    def __init__(self, whole, columns):
        self.whole, self.columns, self.used = whole, columns, 0

    def reset(self):
        self.used = 0

    def take(self, columns, rows=P):
        at = self.used
        self.used += columns
        assert self.used <= self.columns, (self.used, self.columns)
        return self.whole[0:rows, at:at + columns]

    def take_bf16(self, columns, rows=P):
        return self.take((columns + 1) // 2, rows).bitcast(BF16)


def packed(parts):
    at, out = 0, {}
    for name, columns in parts:
        out[name] = (at, columns)
        at += columns
    return out, at


COLUMNS = ([f"L0_{n}{l}" for l in range(DEPTH) for n in ("qs", "qsr", "ks", "ksr", "lg", "lb", "b2")]
           + [f"L0_b1{l}_{i}" for l in range(DEPTH) for i in range(2 * len(HID_BLOCKS))]
           + ["L1_bo"]
           + ["L2_b", "ph", "bmag", "bq"] + [f"L2_lg{i}" for i in range(4)] + [f"L2_lb{i}" for i in range(4)]
           + ["L2_b1_0", "L2_b1_1", "L2_b2", "gamma", "ln1_g", "ln1_b", "ln2_g", "ln2_b"]
           + ["bo0", "bo1", "eps5", "eps6", "eps8", "zero"])
COL = {n: i for i, n in enumerate(COLUMNS)}
ROUTE = M_EXPERTS + EXPERTS

CONST, CONST_N = packed([("ident", P), ("center", P), ("mean", P), ("causal_q", P), ("causal_k", P),
                         ("local_q1", 3 * WINDOW), ("local_k0", 3 * WINDOW), ("negsel", 32),
                         ("cos_q", SEQ), ("sin_q", SEQ), ("cos_k", SEQ), ("sin_k", SEQ),
                         ("pos", SEQ), ("headsum", 8 * 16), ("meanrow", 16), ("dft_k1", P), ("dft_k2", P), ("dft_v1", P), ("dft_v2", P),
                         ("idft1", P), ("idft2", P), ("earlier", EXPERTS * EXPERTS)])
HEADROW_N = 8 * P + 4 * P
ROWS, ROWS_N = packed([("ones", SEQ)] + [(f"{x}{a}", P) for a in ("L1_0", "L3_0", "L3_1") for x in "qkv"])
PARTS = 3
SLOTS = ((0, 0), (1, 0), (2, 0), (0, 1), (1, 1), (0, 2))
STACK = 96
W, W_N = {}, {}
for _l in range(DEPTH):
    W[f"L0f{_l}"], W_N[f"L0f{_l}"] = packed([("qkv", 3 * INNER), ("rot", 2 * INNER), ("wo", INNER),
                                             ("w1", 2 * HID), ("w2", len(HID_BLOCKS) * P)])
W["L0a"], W_N["L0a"] = packed([("qT", P), ("kT", P), ("vT", P), ("out", P)])
W["L1f"], W_N["L1f"] = packed([("fcT", SPIKE_HID), ("projT", SPIKE_HID)])
W["L1a"], W_N["L1a"] = packed([("wq", P), ("wk", P), ("wv", P), ("wo", P)])
W["L2"], W_N["L2"] = packed([("fT", P), ("magT", P), ("qT", P), ("w1T", 4 * 2 * P), ("w2T", 2 * P)])
W["L3a"], W_N["L3a"] = packed([("qkvaT", 3 * P)])
W["L3m"], W_N["L3m"] = packed([("wq", M_EXPERTS * P), ("wk", M_EXPERTS * P),
                               ("wv", M_EXPERTS * P), ("wo", M_EXPERTS * P), ("rw", ROUTE), ("rb", ROUTE)])
W["L3e"], W_N["L3e"] = packed([("fw1", EXPERTS * FF), ("fw2", EXPERTS * FF)])


def program(nc, ins, out, stages=tuple(range(12))):
    with ExitStack() as ctx:
        pr = Program(nc, ctx)
        pe, act, dve, pool, sp = pr.pe, pr.act, pr.dve, pr.pool, pr.sp
        T, V, S, G = nc.tensor, nc.vector, nc.scalar, nc.gpsimd
        pool_queue = pool

        def pool(method, *args, w=(), **kw):
            return pool_queue(method, *args, w=list(w) + [pool_queue.last], **kw)

        X = pr.sbuf("residual", [P, TOKENS])
        X0 = pr.sbuf("stream", [P, TOKENS])
        const = pr.sbuf("const", [P, CONST_N])
        cols = pr.sbuf("cols", [P, len(COLUMNS)])
        headrow = pr.sbuf("headrow", [16, HEADROW_N])
        rows = pr.sbuf("rows", [1, ROWS_N])
        low = pr.sbuf("low_rank", [RANK, 2 * P])
        wt = {n: pr.sbuf(f"w_{n}", [P, k]) for n, k in W_N.items()}
        ident_b = pr.sbuf("ident_b", [P, P], BF16)
        masks_b = pr.sbuf("masks_b", [P, 2 * P + 6 * WINDOW], BF16)
        negsel = pr.sbuf("negsel", [96, 32, P], BF16)
        fold = pr.sbuf("folded", [P, 10 * P])
        probs = pr.sbuf("probs", [P, 16 * BATCH])
        ARENA = 21150
        arena = Arena(pr.sbuf("arena", [P, ARENA]), ARENA)
        ps = ctx.enter_context(nc.psum_tensor("ps", [P, BANKS, BANK], F32))
        bank_free = [None] * BANKS

        def K(name):
            at, n = CONST[name]
            return const[:, at:at + n]

        def C(name):
            return cols[:, COL[name]:COL[name] + 1]

        def R(name):
            at, n = ROWS[name]
            return rows[0:1, at:at + n]

        def wp(group, name):
            at, n = W[group][name]
            return wt[group][:, at:at + n]

        def mm(o, lhsT, rhs, start=True, stop=True, w=()):
            return pe(T.matmul, o, lhsT, rhs, start=start, stop=stop, skip_group_check=True, w=w)

        def seqs(ap, n=PER):
            return ap.rearrange("p (b s) -> p b s", b=n)

        def table(ap, n=PER):
            return ap.unsqueeze(1).to_broadcast([ap.shape[0], n, SEQ])

        loads = {}

        def load(name, dst, src):
            loads[name] = sp.dma(dst, src, pr.counter(f"loaded_{name}"))

        load("x", X[:], ins["x"])
        load("const", const[:], ins["const"])
        load("cols", cols[:], ins["cols"])
        load("headrow", headrow[:], ins["headrow"])
        load("rows", rows[:], ins["rows"])
        load("low", low[:], ins["low"])
        for n in ("L0f0", "L0f1", "L0a", "L1f", "L1a", "L2", "L3a", "L3m", "L3e"):
            load(n, wt[n][:], ins[n])

        t = dve(V.tensor_copy, ident_b[:], K("ident"), w=[loads["const"]])
        dve(V.tensor_copy, masks_b[:, 0:2 * P + 6 * WINDOW],
            const[:, CONST["causal_q"][0]:CONST["causal_q"][0] + 2 * P + 6 * WINDOW])
        dve(V.tensor_copy, negsel[:], K("negsel")[0:96, :].unsqueeze(2).to_broadcast([96, 32, P]))
        causal_q, causal_k = masks_b[:, 0:P], masks_b[:, P:2 * P]
        local_q1 = masks_b[:, 2 * P:2 * P + 3 * WINDOW]
        local_k0 = masks_b[:, 2 * P + 3 * WINDOW:2 * P + 6 * WINDOW]

        def layernorm(src, dst, eps, ready, scale=None, shift=None, work=None):
            sq, sd = work
            xc = dst
            squared, centred, inverse, done = [], [], [], []
            for c in range(NCHUNK):
                cs = slice(c * CHUNK, (c + 1) * CHUNK)
                a = 2 * c
                m = mm(ps[:, a, :], K("center"), src[:, cs], w=[bank_free[a], ready[c], loads["const"]])
                squared.append(act(S.activation, sq[:, cs], ps[:, a, :], ACT.Square, w=[m]))
                centred.append(act(S.activation, xc[:, cs], ps[:, a, :], ACT.Copy))
                bank_free[a] = centred[-1]
            for c in range(NCHUNK):
                b = 2 * c + 1
                for t in range(4):
                    var = mm(ps[0:4, b, 0:P], K("meanrow")[:, 4 * t:4 * t + 4], sq[:, c * CHUNK + t * P:c * CHUNK + (t + 1) * P],
                             start=t == 0, stop=t == 3, w=[bank_free[b], squared[c]])
                r4 = sd[0:4, c * P:(c + 1) * P]
                root = act(S.activation, r4, ps[0:4, b, 0:P], ACT.Sqrt, bias=C(eps)[0:4, :], w=[var, loads["cols"]])
                bank_free[b] = root
                inverse.append(dve(V.reciprocal, r4, r4, w=[root]))
            for c in range(NCHUNK):
                cs, b = slice(c * CHUNK, (c + 1) * CHUNK), 2 * c + 1
                for t in range(4):
                    m = mm(ps[:, b, t * P:(t + 1) * P], headrow[0:4, (8 + t) * P:(9 + t) * P], sd[0:4, c * P:(c + 1) * P],
                           w=[bank_free[b], inverse[c], loads["headrow"]])
                h = dve(V.tensor_tensor, dst[:, cs], xc[:, cs], ps[:, b, :], ALU.mult, w=[m, centred[c]])
                bank_free[b] = h
                if scale is not None:
                    h = dve(V.tensor_scalar, dst[:, cs], dst[:, cs], C(scale), C(shift), ALU.mult, ALU.add, w=[h])
                done.append(h)
            return done

        def start_stage():
            pr.next_stage()
            arena.reset()

        x_ready = [loads["x"]] * NCHUNK

        class Attention:

            def __init__(self, heads, dim, scale, q1, k1, masks_q, masks_k, o_heads, banks2):
                self.heads, self.dim, self.scale = heads, dim, scale
                self.q1, self.k1 = q1, k1
                self.masks_q, self.masks_k, self.o_heads = masks_q, masks_k, o_heads
                self.banks2 = banks2
                self.at_once = len(banks2[0])
                self.mx = [arena.take(2 * heads) for _ in range(2)]
                self.split = [arena.take_bf16(SEQ, 96) for _ in range(2)]
                self.rest = arena.take(SEQ, 32)
                self.mid = arena.take_bf16(SEQ, 32)
                self.pt = [arena.take(self.at_once * BANK) for _ in range(2)]
                self.rinv = [arena.take(2 * o_heads) for _ in range(2)]
                self.ctx = [arena.take(2 * P) for _ in range(2)]
                self.max_read, self.split_done, self.split_read = [None] * 2, [None] * 2, [None] * 2
                self.lo_done = None
                self.pt_read, self.ctx_read = [None] * 2, [None] * 2
                self.zeroed = [dve(V.memset, s, 0.0) for s in self.split]
                self.turn, self.outs, self.later = 0, 0, []

            def after(self, steps, fn):
                self.later.append([steps, fn])

            def tick(self):
                for x in self.later:
                    x[0] -= 1
                due = [x[1] for x in self.later if x[0] <= 0]
                self.later = [x for x in self.later if x[0] > 0]
                for fn in due:
                    fn()

            def flush(self):
                while self.later:
                    self.tick()

            def pass1(self, n, q, k, ready):
                i, H = n % 2, self.heads
                mx = self.mx[i].rearrange("p (t h) -> p t h", t=2)
                ks, nk = self.q1
                n0 = SEQ if not self.masks_q else P
                found = []

                def scores(h):
                    bank = h % 2
                    m = mm(ps[:, bank, 0:n0], q(h)[:, 0:P], k(h)[:, 0:n0], stop=not self.masks_q,
                           w=[bank_free[bank]] + ready)
                    if self.masks_q:
                        mm(ps[:, bank, 0:P], ident_b[:], self.masks_q[0], start=False)
                    m = mm(ps[:, bank, n0:n0 + nk], q(h)[:, P:SEQ], k(h)[:, ks:ks + nk], stop=not self.masks_q)
                    if self.masks_q:
                        mk = self.masks_q[1]
                        m = mm(ps[:, bank, n0 + nk - mk.shape[1]:n0 + nk], ident_b[:], mk, start=False)
                    free = self.max_read[i] if h == 0 else None
                    if n0 == nk:
                        m = dve(V.tensor_reduce, mx[:, :, h:h + 1], ps[:, bank, 0:2 * nk].rearrange("p (t s) -> p t s", t=2),
                                AXX, ALU.max, w=[m, free])
                    else:
                        dve(V.tensor_reduce, mx[:, 0, h:h + 1], ps[:, bank, 0:n0], AXX, ALU.max, w=[m, free])
                        m = dve(V.tensor_reduce, mx[:, 1, h:h + 1], ps[:, bank, n0:n0 + nk], AXX, ALU.max)
                    bank_free[bank] = m
                    found.append(m)
                    self.tick()

                def split():
                    for t in range(2):
                        tr = pe(T.transpose, ps[0:H, 7, t * P:(t + 1) * P], mx[:, t, :], K("ident"),
                                w=[bank_free[7]] + found[-1:])
                    self.max_read[i] = tr
                    src, s, r1 = ps[0:H, 7, 0:SEQ], self.split[i], self.rest[0:H, :]
                    hi = dve(V.tensor_copy, s[0:H, :], src, w=[tr, self.split_read[i], self.zeroed[i]])
                    a = dve(V.tensor_tensor, r1, src, s[0:H, :], ALU.subtract, w=[hi, self.lo_done])
                    bank_free[7] = a
                    mid = dve(V.tensor_copy, self.mid[0:H, :], r1, w=[a])
                    dve(V.tensor_copy, s[32:32 + H, :], self.mid[0:H, :], w=[mid])
                    self.lo_done = dve(V.tensor_tensor, s[64:64 + H, :], r1, self.mid[0:H, :], ALU.subtract)
                    self.split_done[i] = self.lo_done

                return [lambda h=h: scores(h) for h in range(H)] + [lambda: self.after(1, split)]

            def pass2(self, n, q, k, v, ready, finish):
                i, H, G = n % 2, self.heads, self.at_once
                (i0, n0), (i1, n1) = self.k1

                def group(h0):
                    if h0 == 0:
                        self.tick()
                    u = self.turn % 2
                    banks = self.banks2[u]
                    self.turn += 1
                    for h in range(h0, h0 + G):
                        bank = banks[h - h0]
                        for t, (st, cnt, at) in enumerate(((i0, n0, 0), (i1, n1, n0))):
                            o = ps[:, bank, at:at + cnt]
                            mm(o, k(h)[:, t * P:(t + 1) * P], q(h)[:, st:st + cnt], stop=False,
                               w=[bank_free[bank]] + ready)
                            if self.masks_k:
                                mk = self.masks_k[t]
                                mm(ps[:, bank, at:at + mk.shape[1]], ident_b[:], mk, start=False, stop=False)
                            m = mm(o, negsel[:, h, :], self.split[i][:, st:st + cnt], start=False,
                                   w=[self.split_done[i]])
                    self.split_read[i] = m
                    both = n0 + n1
                    pt = self.pt[u].rearrange("p (h c) -> p h c", h=G)
                    e = act(S.activation, pt[:, :, 0:both], ps[:, banks[0]:banks[-1] + 1, 0:both], ACT.Exp,
                            scale=self.scale, w=[m, self.pt_read[u]])
                    for bank in banks:
                        bank_free[bank] = e
                    self.after(2, lambda: self.weigh(n, h0, u, pt, e, v, finish))
                    self.tick()

                return [lambda h=h: group(h) for h in range(0, H, G)]

            def weigh(self, n, h0, u, pt, e, v, finish):
                D, G = self.dim + 1, self.at_once
                n0, i1 = self.k1[0][1], self.k1[1][0]
                for h in range(h0, h0 + G):
                    slot = h % self.o_heads
                    pth = pt[:, h - h0, :]
                    for t in range(2):
                        at = (t * self.o_heads + slot) * D
                        if t == 0:
                            parts = [(0, P, pth[:, 0:P])] + ([(1, P, pth[:, n0:n0 + P])] if i1 == 0 else [])
                        else:
                            m1, at1 = n0 - P, n0 + P - i1
                            parts = [(1, P, pth[:, at1:at1 + P]), (0, m1, pth[:, P:P + m1])]
                        for j, (kt, cnt, lhsT) in enumerate(parts):
                            o = mm(ps[0:cnt, 6, at:at + D], lhsT, v(kt, h), start=j == 0, stop=j == len(parts) - 1,
                                   w=[e, bank_free[6]])
                self.pt_read[u] = o
                if slot == self.o_heads - 1:
                    finish(h0 + G - 1, o)

            def normalise(self, o, factor, then):
                oh, D = self.o_heads, self.dim + 1
                k = self.outs % 2
                self.outs += 1
                ov = ps[:, 6, 0:2 * oh * D].rearrange("p (a d) -> p a d", d=D)
                rinv = self.rinv[k][:, 0:2 * oh]
                r = dve(V.reciprocal, rinv, ov[:, :, self.dim:D].rearrange("p a d -> p (a d)"), w=[o])
                if factor is not None:
                    r = dve(V.tensor_scalar, rinv, rinv, factor, None, ALU.mult, w=[r])
                ctxv = self.ctx[k].rearrange("p (a d) -> p a d", d=self.dim)
                c = dve(V.tensor_tensor, ctxv, ov[:, :, 0:self.dim],
                        rinv.unsqueeze(2).to_broadcast([P, 2 * oh, self.dim]), ALU.mult, w=[r, self.ctx_read[k]])
                bank_free[6] = c

                def turn():
                    for t in range(2):
                        tr = pe(T.transpose, ps[:, 7, t * P:(t + 1) * P], self.ctx[k][:, t * P:(t + 1) * P], K("ident"),
                                w=[c, bank_free[7]])
                    self.ctx_read[k] = tr
                    then(tr)

                self.after(2, turn)

        class FeatureMajor(Attention):

            def __init__(self, *args):
                super().__init__(*args)
                self.raw = [arena.take(BANK)] * 2
                self.raw_read = None
                bank_free[6] = dve(V.memset, ps[:, 6, :], 0.0, w=[bank_free[6]])

            def weigh(self, n, h0, u, pt, e, v, finish):
                (i0, n0), (i1, n1) = self.k1
                for h in range(h0, h0 + self.at_once):
                    g, c, pth = h % 4, h // 4 % 2, pt[:, h - h0, :]
                    for t, (st, cnt, at) in enumerate(((i0, n0, 0), (i1, n1, n0))):
                        o = mm(ps[32 * g:32 * g + self.dim + 1, 6, c * SEQ + st:c * SEQ + st + cnt], v(t, h), pth[:, at:at + cnt],
                               start=t == 0, stop=t == 1, w=[e, bank_free[6]])
                self.pt_read[u] = o
                if h % 8 == 7:
                    r = h // 8
                    self.unit_read(n, o)
                    copied = act(S.activation, self.raw[r], ps[:, 6, :], ACT.Copy, w=[o, self.raw_read])
                    bank_free[6] = copied
                    self.after(2, lambda: self.turn_back(n, r, copied, finish))

            def turn_back(self, n, r, copied, finish):
                for a in range(4):
                    at = (a % 2 * 2 + a // 2) * P
                    tr = pe(T.transpose, ps[:, 7, a * P:(a + 1) * P], self.raw[r][:, at:at + P], K("ident"),
                            w=[copied, bank_free[7]])
                self.raw_read = tr
                rows32 = ps[:, 7, :].rearrange("p (a d) -> p a d", d=32)
                k = n % 2
                rinv = self.rinv[r][:, 0:16]
                inv = dve(V.reciprocal, rinv, rows32[:, :, self.dim:self.dim + 1].rearrange("p a d -> p (a d)"), w=[tr])
                factor = self.factor(n)
                if factor is not None:
                    inv = dve(V.tensor_scalar, rinv, rinv, factor, None, ALU.mult, w=[inv])
                ctxv = self.ctx[k].rearrange("p (t q) -> p t q", t=2)[:, :, r * 64:(r + 1) * 64]
                c = dve(V.tensor_tensor, ctxv.rearrange("p t (a d) -> p t a d", d=self.dim),
                        rows32[:, :, 0:self.dim].rearrange("p (t a) d -> p t a d", t=2),
                        rinv.rearrange("p (t a) -> p t a", t=2).unsqueeze(3).to_broadcast([P, 2, 8, self.dim]),
                        ALU.mult, w=[inv, self.ctx_read[k]])
                bank_free[7] = c
                if r == 1:
                    self.after(2, lambda: self.turn_again(n, k, c, finish))

            def turn_again(self, n, k, c, finish):
                for t in range(2):
                    tr = pe(T.transpose, ps[:, 7, t * P:(t + 1) * P], self.ctx[k][:, t * P:(t + 1) * P], K("ident"), w=[c, bank_free[7]])
                self.ctx_read[k] = tr
                finish(tr)

        def interleave(*lists):
            total = max(len(x) for x in lists)
            at = [0] * len(lists)
            for i in range(total):
                for j, x in enumerate(lists):
                    while at[j] < len(x) and at[j] * total < (i + 1) * len(x):
                        x[at[j]]()
                        at[j] += 1

        def run_units(count, prepare, first, second, att):
            for n in range(count + 2):
                interleave(prepare(n) if n < count else [],
                           first(n - 1) if 0 <= n - 1 < count else [],
                           second(n - 2) if 0 <= n - 2 < count else [])
            att.flush()

        def l0_layer(l, last, x_in):
            start_stage()
            w0 = f"L0f{l}"
            ready = [loads[w0], loads["cols"], loads["const"], loads["headrow"]]
            H = arena.take(TOKENS)
            oT = [arena.take(4 * SEQ).rearrange("p (j s) -> p j s", j=4) for _ in range(2)]
            tabs = [arena.take(2 * SEQ) for _ in range(2)]
            qk = [arena.take(8 * SEQ).rearrange("p (j s) -> p j s", j=8) for _ in range(3)]
            prod = [arena.take(2 * SEQ) for _ in range(2)]
            sqs = arena.take(8 * SEQ).rearrange("p (j s) -> p j s", j=8)
            rn = arena.take(SEQ, 16)
            va = [arena.take(2 * L0_HEADS * 65).rearrange("p (t h d) -> p t h d", t=2, h=L0_HEADS) for _ in range(3)]
            att = Attention(L0_HEADS, L0_DIM, 1.0, (WINDOW, 3 * WINDOW), ((0, 3 * WINDOW), (P, P)),
                            (local_q1[:, WINDOW:], local_q1), (local_k0, local_k0[:, 0:P]), 2, ((2,), (3,)))
            for v in va:
                ones = dve(V.memset, v[:, :, :, L0_DIM:L0_DIM + 1], 1.0)
            for tab, at, tname, cname in ((0, 0, "cos_q", "qs"), (0, 1, "sin_q", "qsr"), (1, 0, "cos_k", "ks"), (1, 1, "sin_k", "ksr")):
                tab_ready = dve(V.tensor_scalar, tabs[tab][:, at * SEQ:(at + 1) * SEQ], K(tname), C(f"L0_{cname}{l}"), None,
                                ALU.mult, w=[loads["cols"], loads["const"]])

            def shifted(src, dst, ready_c, cs):
                pool(G.tensor_copy, dst[0:64, cs], src[0:64, cs], w=[ready_c])
                dv, sv = seqs(dst[64:P, cs]), seqs(src[64:P, cs])
                pool(G.memset, dv[:, :, 0:1], 0.0)
                return pool(G.tensor_copy, dv[:, :, 1:SEQ], sv[:, :, 0:SEQ - 1])

            h_done = [shifted(X0, H, x_in[c], slice(c * CHUNK, (c + 1) * CHUNK)) for c in range(NCHUNK)]
            normed, v_done = [None] * BATCH, [None] * BATCH
            qk_read, va_read, sq_read, prod_read, rn_read = [None] * 3, [None] * 3, [None], [None] * 2, [None]
            o_read, x1 = [None] * 2, [None] * BATCH

            def prepare(b):
                i, bs = b % 3, slice(b * SEQ, (b + 1) * SEQ)
                Q, squares, placed = qk[i], [], []

                def block(j):
                    bank, k = 4 + j % 2, j % 2
                    mm(ps[:, bank, 0:SEQ], wp(w0, "qkv")[:, j * P:(j + 1) * P], H[:, bs],
                       w=[bank_free[bank], h_done[b // PER]] + ready)
                    m = mm(ps[:, bank, SEQ:2 * SEQ], wp(w0, "rot")[:, j * P:(j + 1) * P], H[:, bs])
                    sq = act(S.activation, sqs[:, j, :], ps[:, bank, 0:SEQ], ACT.Square, w=[m, sq_read[0]])
                    squares.append(sq)
                    pd = dve(V.tensor_tensor, prod[k], ps[:, bank, :], tabs[j // 4], ALU.mult,
                             w=[sq, prod_read[k], tab_ready])
                    bank_free[bank] = pd
                    prod_read[k] = pool(G.tensor_tensor, Q[:, j, :], prod[k][:, 0:SEQ], prod[k][:, SEQ:2 * SEQ], ALU.add,
                                        w=[pd, qk_read[i]])
                    placed.append(prod_read[k])

                def norms():
                    for j in range(8):
                        m = mm(ps[0:16, 7, 0:SEQ], K("headsum")[:, j * 16:(j + 1) * 16], sqs[:, j, :], start=j == 0, stop=j == 7,
                               w=[squares[-1], bank_free[7]])
                    sq_read[0] = m
                    root = act(S.activation, rn, ps[0:16, 7, 0:SEQ], ACT.Sqrt, bias=C("zero")[0:16, :], w=[m, rn_read[0]])
                    bank_free[7] = root
                    clipped = dve(V.tensor_scalar, rn, rn, 1e-12, None, ALU.max, w=[root])
                    inverse.append(dve(V.reciprocal, rn, rn, w=[clipped]))

                inverse = []

                def spread(j):
                    for x in range(2):
                        m = mm(ps[:, 7, x * SEQ:(x + 1) * SEQ], headrow[:, (j + x) * P:(j + x + 1) * P], rn,
                               w=[bank_free[7], inverse[0]])
                    rn_read[0] = m
                    normed[b] = dve(V.tensor_tensor, Q[:, j:j + 2, :], Q[:, j:j + 2, :],
                                    ps[:, 7, :].rearrange("p (x s) -> p x s", x=2), ALU.mult, w=[m, placed[j + 1]])
                    bank_free[7] = normed[b]

                def values(t):
                    tok = slice(b * SEQ + t * P, b * SEQ + (t + 1) * P)
                    bank = 4 + t
                    m = mm(ps[:, bank, :], H[:, tok], wp(w0, "qkv")[:, 2 * INNER:3 * INNER], w=[bank_free[bank]])
                    v_done[b] = act(S.activation, va[i][:, t, :, 0:L0_DIM], ps[:, bank, :].rearrange("p (h d) -> p h d", h=L0_HEADS),
                                    ACT.Copy, w=[m, va_read[i], ones])
                    bank_free[bank] = v_done[b]

                return ([lambda j=j: block(j) for j in range(8)] + [norms] + [lambda t=t: values(t) for t in range(2)]
                        + [lambda j=j: spread(j) for j in range(0, 8, 2)])

            def head(b, first):
                def f(h):
                    base = L0_DIM * (h % 2)
                    return qk[b % 3][base:base + L0_DIM, first + h // 2, :]
                return f

            def finish(b, h, o):
                k, j = b % 2, h // 2

                def then(tr):
                    cp = act(S.activation, oT[k][:, j, :], ps[:, 7, 0:SEQ], ACT.Copy, w=[tr, o_read[k]])
                    bank_free[7] = cp
                    if j == 3:
                        att.after(2, lambda: project(cp))

                def project(cp):
                    for jj in range(4):
                        y = mm(ps[:, 7, 0:SEQ], wp(w0, "wo")[:, jj * P:(jj + 1) * P], oT[k][:, jj, :], start=jj == 0,
                               stop=jj == 3, w=[bank_free[7], cp])
                    o_read[k] = y
                    bs = slice(b * SEQ, (b + 1) * SEQ)
                    x1[b] = dve(V.tensor_tensor, X0[:, bs], X0[:, bs], ps[:, 7, 0:SEQ], ALU.add, w=[y])
                    bank_free[7] = x1[b]

                att.normalise(o, None, then)
                if j == 3:
                    qk_read[b % 3] = va_read[b % 3] = o

            run_units(BATCH, prepare,
                      lambda b: att.pass1(b, head(b, 0), head(b, 4), [normed[b]]),
                      lambda b: att.pass2(b, head(b, 0), head(b, 4), lambda kt, h: va[b % 3][:, kt, h, :], [v_done[b]],
                                          lambda h, o: finish(b, h, o)), att)
            x1 = [x1[PER * c + PER - 1] for c in range(NCHUNK)]

            start_stage()
            H2 = arena.take(TOKENS)
            N2 = arena.take(TOKENS)
            work = (arena.take(TOKENS), arena.take(TOKENS))
            g = [arena.take(CHUNK) for _ in range(2)]
            hh = [arena.take(3 * CHUNK) for _ in range(2)]
            h_done = [shifted(X0, H2, x1[c], slice(c * CHUNK, (c + 1) * CHUNK)) for c in range(NCHUNK)]
            n_done = layernorm(H2, N2, "eps5", h_done, f"L0_lg{l}", f"L0_lb{l}", work)
            out_done = []
            g_read, hh_read = [None, None], [None, None]
            for c in range(NCHUNK):
                cs = slice(c * CHUNK, (c + 1) * CHUNK)
                k = c % 2
                for j, (at, n) in enumerate(HID_BLOCKS):
                    a, gb = 2 * (j % 2), 2 * (j % 2) + 1
                    u = j % 2
                    pa = mm(ps[0:n, a, :], wp(w0, "w1")[:, at:at + n], N2[:, cs], w=[bank_free[a], n_done[c], loads[w0]])
                    pg = mm(ps[0:n, gb, :], wp(w0, "w1")[:, HID + at:HID + at + n], N2[:, cs], w=[bank_free[gb]])
                    ge = act(S.activation, g[u][0:n, :], ps[0:n, gb, :], ACT.Gelu,
                             bias=C(f"L0_b1{l}_{3 + j}")[0:n, :], w=[pg, g_read[u]])
                    bank_free[gb] = ge
                    pr_ = dve(V.scalar_tensor_tensor, hh[k][0:n, j * CHUNK:(j + 1) * CHUNK], ps[0:n, a, :],
                              C(f"L0_b1{l}_{j}")[0:n, :], g[u][0:n, :], ALU.add, ALU.mult, w=[ge, pa, hh_read[k]])
                    bank_free[a] = pr_
                    g_read[u] = pr_
                ob = 4 + c % 2
                for j, (at, n) in enumerate(HID_BLOCKS):
                    y = mm(ps[:, ob, :], wp(w0, "w2")[0:n, j * P:(j + 1) * P], hh[k][0:n, j * CHUNK:(j + 1) * CHUNK],
                           start=j == 0, stop=j == 2, w=[bank_free[ob], pr_])
                hh_read[k] = y
                xx = dve(V.scalar_tensor_tensor, X0[:, cs], ps[:, ob, :], C(f"L0_b2{l}"), X0[:, cs], ALU.add, ALU.add, w=[y])
                bank_free[ob] = xx
                if last:
                    xx = dve(V.scalar_tensor_tensor, X[:, cs], X0[:, cs], 0.5, X[:, cs], ALU.mult, ALU.add, w=[xx])
                out_done.append(xx)
            return out_done

        def l0_ffn(x_ready):
            start_stage()
            done = layernorm(X, X0, "eps5", x_ready, work=(arena.take(TOKENS), arena.take(TOKENS)))
            for l in range(DEPTH):
                done = l0_layer(l, l == DEPTH - 1, done)
            return done

        def l0_attn(x_ready):
            start_stage()
            h = arena.take(TOKENS)
            done = layernorm(X, h, "eps5", x_ready, work=(arena.take(TOKENS), arena.take(TOKENS)))
            spec = [("kT", "dft_k1"), ("kT", "dft_k2"), ("vT", "dft_v1"), ("vT", "dft_v2"), ("qT", "dft_v1"), ("qT", "dft_v2")]
            for i, (wn, dn) in enumerate(spec):
                bk = 0 if i < 4 else 1
                m = mm(ps[:, bk, (i % 4) * P:(i % 4 + 1) * P], wp("L0a", wn), DFT[dn],
                       w=[bank_free[bk], loads["L0a"], loads["const"]])
            for i, dn in enumerate(("idft1", "idft2")):
                m = mm(ps[:, 1, (2 + i) * P:(3 + i) * P], K(dn), wp("L0a", "out"))
            e0 = act(S.activation, fold[:, 0:BANK], ps[:, 0, :], ACT.Copy, w=[m])
            folded = act(S.activation, fold[:, BANK:2 * BANK], ps[:, 1, :], ACT.Copy)
            bank_free[0] = bank_free[1] = folded
            k1, kv, cum, t2 = (arena.take(TOKENS) for _ in range(4))
            keep = arena.take(TOKENS)
            kp = dve(V.memset, keep, 1.0)
            kp = dve(V.memset, seqs(keep, BATCH)[:, :, 0:1], 0.0, w=[kp])
            out = []
            for c in range(NCHUNK):
                cs = slice(c * CHUNK, (c + 1) * CHUNK)
                prj = []
                for i in range(6):
                    b = i if i < 4 else i + 0
                    prj.append(mm(ps[:, b, :], fold[:, i * P:(i + 1) * P], h[:, cs],
                                  w=[bank_free[b], done[c], folded]))
                c1 = act(S.activation, k1[:, cs], ps[:, 0, :], ACT.Copy, w=[prj[0]])
                c2 = act(S.activation, t2[:, cs], ps[:, 1, :], ACT.Copy, w=[prj[1]])
                bank_free[0], bank_free[1] = c1, c2
                a1 = dve(V.tensor_tensor, k1[:, cs], k1[:, cs], ps[:, 2, :], ALU.mult, w=[c1, prj[2]])
                a2 = dve(V.tensor_tensor, t2[:, cs], t2[:, cs], ps[:, 3, :], ALU.mult, w=[c2, prj[3]])
                bank_free[2], bank_free[3] = a1, a2
                s_ = pool(G.tensor_tensor, kv[:, cs], k1[:, cs], t2[:, cs], ALU.add, w=[a1, a2])
                cu = dve(V.tensor_tensor_scan, cum[:, cs], keep[:, cs], kv[:, cs], 0.0, ALU.mult, ALU.add, w=[s_, kp])
                b1 = dve(V.tensor_tensor, k1[:, cs], cum[:, cs], ps[:, 4, :], ALU.mult, w=[cu, prj[4]])
                b2 = dve(V.tensor_tensor, t2[:, cs], cum[:, cs], ps[:, 5, :], ALU.mult, w=[prj[5]])
                bank_free[4], bank_free[5] = b1, b2
                ob = 6 + c % 2
                mm(ps[:, ob, :], fold[:, 6 * P:7 * P], k1[:, cs], stop=False, w=[bank_free[ob], b1])
                y = mm(ps[:, ob, :], fold[:, 7 * P:8 * P], t2[:, cs], start=False, w=[b2])
                xx = dve(V.tensor_tensor, X[:, cs], X[:, cs], ps[:, ob, :], ALU.add, w=[y])
                bank_free[ob] = xx
                out.append(xx)
            return out

        DFT = {"dft_k1": K("dft_k1"), "dft_k2": K("dft_k2"), "dft_v2": K("dft_v2"), "dft_v1": K("dft_v1")}

        def l1_ffn(x_ready):
            start_stage()
            h = arena.take(TOKENS)
            done = layernorm(X, h, "eps5", x_ready, work=(arena.take(TOKENS), arena.take(TOKENS)))
            relu = [arena.take(4 * CHUNK) for _ in range(2)]
            y, mem, u, acc = (arena.take(TOKENS) for _ in range(4))
            out = []
            rl_read = [None, None]
            for c in range(NCHUNK):
                cs = slice(c * CHUNK, (c + 1) * CHUNK)
                k = c % 2
                sq = []
                for j in range(4):
                    p1 = mm(ps[:, j, :], wp("L1f", "fcT")[:, j * P:(j + 1) * P], h[:, cs],
                            w=[bank_free[j], done[c], loads["L1f"]])
                    js = slice(j * CHUNK, (j + 1) * CHUNK)
                    r = act(S.activation, relu[k][:, js], ps[:, j, :], ACT.Relu, w=[p1, rl_read[k]])
                    bank_free[j] = r
                    sq.append(act(S.activation, relu[k][:, js], relu[k][:, js], ACT.Square, w=[r]))
                ob = 4 + c % 2
                for j in range(4):
                    yy = mm(ps[:, ob, :], wp("L1f", "projT")[:, j * P:(j + 1) * P], relu[k][:, j * CHUNK:(j + 1) * CHUNK],
                            start=j == 0, stop=j == 3, w=[sq[j], bank_free[ob]])
                rl_read[k] = yy
                d = act(S.activation, y[:, cs], ps[:, ob, :], ACT.Copy, w=[yy])
                bank_free[ob] = d
                d = dve(V.tensor_scalar, mem[:, cs], y[:, cs], -1.0, None, ALU.mult, w=[d])
                a = dve(V.tensor_scalar, acc[:, cs], mem[:, cs], -1.0, None, ALU.is_lt, w=[d])
                for s_ in range(SPIKE_STEPS - 1):
                    d = dve(V.scalar_tensor_tensor, u[:, cs], mem[:, cs], BETA, y[:, cs], ALU.mult, ALU.subtract, w=[d])
                    d = dve(V.scalar_tensor_tensor, mem[:, cs], mem[:, cs], -1.0, u[:, cs], ALU.is_lt, ALU.add, w=[d])
                    a = dve(V.scalar_tensor_tensor, acc[:, cs], mem[:, cs], -1.0, acc[:, cs], ALU.is_lt, ALU.add, w=[d, a])
                out.append(dve(V.scalar_tensor_tensor, X[:, cs], acc[:, cs], 0.5 / SPIKE_STEPS, X[:, cs], ALU.mult, ALU.add, w=[a]))
            return out

        scratch = nc.dram_tensor("scratch", (3, 2, PARTS, P, SEQ), BF16, kind="Internal").ap()
        written = [pr.counter(f"parts_written{i}") for i in range(3)]
        stacked = [pr.counter(f"stack_loaded{i}") for i in range(3)]

        class SmallHeads:

            def __init__(self, group, name, members, h, h_ready, masks_q, masks_k, finish, free_after, buffer2, factor):
                self.group, self.name, self.members, self.h, self.h_ready = group, name, members, h, h_ready
                self.finish = finish
                whole = [arena.take(2 * HEADS * SEQ // 2) for _ in range(2)] + [buffer2]
                stacks = [t.bitcast(BF16).rearrange("p (x h s) -> p x h s", x=2, h=HEADS) for t in whole]
                self.q, self.k = [t[0:STACK, 0] for t in stacks], [t[0:STACK, 1] for t in stacks]
                self.cleared = [pool(G.memset, whole[i][0:STACK, :], 0.0, w=free_after if i == 2 else []) for i in range(3)]
                self.parts = [arena.take_bf16(2 * PARTS * SEQ).rearrange("p (x a s) -> p x a s", x=2, a=PARTS) for _ in range(1)]
                self.rest = arena.take(2 * SEQ)
                self.va = [arena.take(2 * HEADS * (KD + 1)).rearrange("p (t h d) -> p t h d", t=2, h=HEADS) for _ in range(3)]
                for v in self.va:
                    self.ones = dve(V.memset, v[:, :, :, KD:KD + 1], 1.0)
                self.att = FeatureMajor(HEADS, KD, float(1.0 / np.sqrt(np.float32(KD))), (0, SEQ),
                                     ((0, SEQ), (P, P) if masks_q else (0, SEQ)), masks_q, masks_k, 8, ((2, 3), (4, 5)))
                self.att.factor, self.att.unit_read = factor, self.unit_read
                self.loaded, self.v_done = [None] * 3, [None] * 3
                self.stack_read, self.parts_written, self.rest_read = [None] * 3, [None] * 2, None

            def unit_read(self, n, o):
                self.stack_read[n % 3] = o

            def prepare(self, n):
                b, m, i, k = n // self.members, n % self.members, n % 3, 0
                bs, ms = slice(b * SEQ, (b + 1) * SEQ), slice(m * P, (m + 1) * P)
                g, tag, ready = self.group, f"{self.name}_{m}", [self.h_ready[b // PER], loads[self.group], loads["rows"]]
                parts, rest = self.parts[k], self.rest
                both = lambda ap: ap.rearrange("p (x s) -> p x s", x=2)

                def qk():
                    for x, xn in enumerate("qk"):
                        o = ps[:, 7, x * SEQ:(x + 1) * SEQ]
                        mm(o, wp(g, "w" + xn)[:, ms], self.h[:, bs], stop=False, w=[bank_free[7]] + ready)
                        mp_ = mm(o, R(xn + tag), R("ones"), start=False)
                    hi = act(S.activation, parts[:, :, 0, :], both(ps[:, 7, :]), ACT.Copy, w=[mp_, self.parts_written[k]])
                    r1 = dve(V.tensor_tensor, both(rest), both(ps[:, 7, :]), parts[:, :, 0, :], ALU.subtract,
                             w=[hi, self.rest_read])
                    bank_free[7] = r1
                    mid = act(S.activation, parts[:, :, 1, :], both(rest), ACT.Copy, w=[r1])
                    lo = pool(G.tensor_tensor, parts[:, :, 2, :], both(rest), parts[:, :, 1, :], ALU.subtract, w=[mid])
                    self.rest_read = lo
                    out_ = sp.dma(scratch[i].rearrange("x a p s -> p (x a) s"), parts.rearrange("p x a s -> p (x a) s"),
                                  written[i], w=[lo, self.loaded[i]])
                    self.parts_written[k] = out_
                    rows_ = scratch[i].rearrange("x a (r h) s -> x (a r) h s", h=HEADS)
                    for x, st in enumerate((self.q[i], self.k[i])):
                        s0 = 0
                        while s0 < len(SLOTS):
                            a0, s1 = SLOTS[s0][x], s0 + 1
                            while s1 < len(SLOTS) and SLOTS[s1][x] == a0 + s1 - s0:
                                s1 += 1
                            self.loaded[i] = sp.dma(st[KD * s0:KD * s1], rows_[x, KD * a0:KD * (a0 + s1 - s0)], stacked[i],
                                                    w=[out_, self.stack_read[i], self.cleared[i]])
                            s0 = s1

                def values():
                    for t in range(2):
                        o = ps[:, 7, t * P:(t + 1) * P]
                        mm(o, self.h[:, b * SEQ + t * P:b * SEQ + (t + 1) * P], wp(g, "wv")[:, ms], stop=False, w=[bank_free[7]])
                        mv = mm(o, R("ones")[:, 0:P], R("v" + tag), start=False)
                    self.v_done[i] = act(S.activation, self.va[i][:, :, :, 0:KD],
                                         ps[:, 7, 0:2 * P].rearrange("p (t h d) -> p t h d", t=2, d=KD), ACT.Copy,
                                         w=[mv, self.stack_read[i], self.ones])
                    bank_free[7] = self.v_done[i]

                return [qk, values]

            def run(self):
                at = self.att

                run_units(BATCH * self.members, self.prepare,
                          lambda n: at.pass1(n, lambda h: self.q[n % 3][:, h, :], lambda h: self.k[n % 3][:, h, :],
                                             [self.loaded[n % 3]]),
                          lambda n: at.pass2(n, lambda h: self.q[n % 3][:, h, :], lambda h: self.k[n % 3][:, h, :],
                                             lambda kt, h: self.va[n % 3][:, kt, h, :], [self.v_done[n % 3]],
                                             lambda tr: self.finish(n, tr)), at)

        def l1_attn(x_ready):
            start_stage()
            h = arena.take(TOKENS)
            buffer2 = arena.take(2 * TOKENS)
            done = layernorm(X, h, "eps5", x_ready, work=(buffer2[:, 0:TOKENS], buffer2[:, TOKENS:]))
            ctxT = [arena.take(SEQ) for _ in range(2)]
            out, ct_read = [None] * BATCH, [None, None]

            def finish(b, tr):
                k = b % 2
                cp = act(S.activation, ctxT[k], ps[:, 7, 0:SEQ], ACT.Copy, w=[tr, ct_read[k]])
                bank_free[7] = cp

                def project(cp):
                    y = mm(ps[:, 7, 0:SEQ], wp("L1a", "wo"), ctxT[k], w=[cp, bank_free[7]])
                    ct_read[k] = y
                    bs = slice(b * SEQ, (b + 1) * SEQ)
                    out[b] = dve(V.scalar_tensor_tensor, X[:, bs], ps[:, 7, 0:SEQ], C("L1_bo"), X[:, bs],
                                 ALU.add, ALU.add, w=[y])
                    bank_free[7] = out[b]

                small.att.after(2, lambda: project(cp))

            small = SmallHeads("L1a", "L1", 1, h, done, (causal_q, causal_q), (causal_k, causal_k), finish, done, buffer2,
                               lambda n: None)
            small.run()
            return [out[PER * c + PER - 1] for c in range(NCHUNK)]

        def l2_ffn(x_ready):
            start_stage()
            mm(ps[:, 7, 0:P], K("ident"), wp("L2", "fT"), stop=False, w=[bank_free[7], loads["L2"]])
            m = mm(ps[:, 7, 0:P], low[:, 0:P], low[:, P:2 * P], start=False, w=[loads["low"]])
            wf = fold[:, 8 * P:9 * P]
            f = act(S.activation, wf, ps[:, 7, 0:P], ACT.Copy, w=[m])
            half_b = arena.take(1)
            hb = act(S.mul, half_b, C("L2_b"), 0.5, w=[loads["cols"]])
            bank_free[7] = f
            h = arena.take(TOKENS)
            done = layernorm(X, h, "eps5", x_ready, work=(arena.take(TOKENS), arena.take(TOKENS)))
            y = arena.take(TOKENS)
            out = []
            for c in range(NCHUNK):
                cs = slice(c * CHUNK, (c + 1) * CHUNK)
                b = 2 * c
                m = mm(ps[:, b, :], wf, h[:, cs], w=[bank_free[b], done[c], f])
                e = act(S.activation, y[:, cs], ps[:, b, :], ACT.Identity, bias=half_b, scale=0.5, w=[m, hb])
                bank_free[b] = e
                out.append(dve(V.tensor_tensor, X[:, cs], X[:, cs], y[:, cs], ALU.add, w=[e]))
            return out

        TWO_PI = 6.283185307179586
        HI = float(np.float32(6.28125))
        MIDP = float(np.float32(TWO_PI - HI))
        LOP = float(np.float32(TWO_PI - HI - MIDP))
        MAGIC = 12582912.0
        PI = float(np.nextafter(np.float32(np.pi), np.float32(0)))

        def sines(src, sin_out, cos_out, k, r, ready):
            last = []
            for o, quarter in ((sin_out, 0.0), (cos_out, 0.25)):
                a = dve(V.tensor_scalar, k, src, 1.0 / TWO_PI, quarter, ALU.mult, ALU.add, w=ready + last)
                a = dve(V.tensor_scalar, k, k, MAGIC, -MAGIC, ALU.add, ALU.add, w=[a])
                a = dve(V.scalar_tensor_tensor, r, k, -HI, src, ALU.mult, ALU.add, w=[a] + last)
                a = dve(V.scalar_tensor_tensor, r, k, -MIDP, r, ALU.mult, ALU.add, w=[a])
                a = dve(V.scalar_tensor_tensor, r, k, -LOP, r, ALU.mult, ALU.add, w=[a])
                if quarter:
                    a = dve(V.tensor_scalar, r, r, TWO_PI / 4, None, ALU.add, w=[a])
                a = dve(V.tensor_scalar, r, r, PI, -PI, ALU.min, ALU.max, w=[a])
                last = [act(S.activation, o, r, ACT.Sin, w=[a])]
            return last[0]

        def l2_attn(x_ready):
            start_stage()
            h = arena.take(TOKENS)
            work = (arena.take(TOKENS), arena.take(TOKENS))
            done = layernorm(X, h, "eps5", x_ready, work=work)
            phi, cphi, sphi, kq, rq = (arena.take(SEQ) for _ in range(5))
            keep = arena.take(CHUNK)
            kp = dve(V.memset, keep, 1.0)
            kp = dve(V.memset, seqs(keep)[:, :, 0:1], 0.0, w=[kp])
            a = dve(V.tensor_scalar, phi, K("pos"), C("ph"), None, ALU.mult, w=[loads["const"], loads["cols"]])
            phi_done = dve(V.tensor_scalar, phi, phi, 0.01, None, ALU.mult, w=[a])
            trig = sines(phi, sphi, cphi, kq, rq, [phi_done])
            w1 = arena.take(4 * FF).rearrange("p (i f) -> p i f", i=4)
            bias1 = arena.take(2)
            for i in range(4):
                g_ = dve(V.tensor_scalar, w1[:, i, :], wp("L2", "w1T")[:, i * FF:(i + 1) * FF], C(f"L2_lg{i}"), None, ALU.mult,
                         w=[loads["L2"], loads["cols"]])
            for o in range(2):
                for i in range(4):
                    m = mm(ps[:, 7, o:o + 1], wp("L2", "w1T")[:, i * FF + o * P:i * FF + (o + 1) * P], C(f"L2_lb{i}"),
                           start=i == 0, stop=i == 3, w=[bank_free[7], loads["L2"], loads["cols"]])
            for o in range(2):
                bb = dve(V.tensor_tensor, bias1[:, o:o + 1], ps[:, 7, o:o + 1], C(f"L2_b1_{o}"), ALU.add, w=[m])
            bank_free[7] = bb
            n = CHUNK
            mag, wx, tr, ti, mr, mi, am, pq, sq_, cq, k_, r_ = (arena.take(n) for _ in range(12))
            ctxb = arena.take(4 * n).rearrange("p (i s) -> p i s", i=4)
            sqb = work[0].rearrange("p (i s) -> p i s", i=4)
            hb = arena.take(2 * n).rearrange("p (i s) -> p i s", i=2)
            five = arena.take(1)
            out = []
            TT = V.tensor_tensor
            prev = []
            for c in range(NCHUNK):
                cs = slice(c * CHUNK, (c + 1) * CHUNK)
                hc = h[:, cs]
                pm = mm(ps[:, 0, :], wp("L2", "magT"), hc, w=[bank_free[0], done[c], loads["L2"]])
                pq_ = mm(ps[:, 1, :], wp("L2", "qT"), hc, w=[bank_free[1]])
                sg = act(S.activation, mag, ps[:, 0, :], ACT.Sigmoid, bias=C("bmag"), w=[pm] + prev)
                bank_free[0] = sg
                mg = dve(V.tensor_scalar, mag, mag, 5.0, None, ALU.mult, w=[sg])
                wxd = dve(TT, wx, mag, hc, ALU.mult, w=[mg])
                trd = dve(TT, seqs(tr), seqs(wx), table(cphi), ALU.mult, w=[wxd, trig])
                tid = dve(TT, seqs(ti), seqs(wx), table(sphi), ALU.mult)
                a1 = dve(V.tensor_tensor_scan, mr, keep, tr, 0.0, ALU.mult, ALU.add, w=[trd, kp])
                a2 = dve(V.tensor_tensor_scan, mi, keep, ti, 0.0, ALU.mult, ALU.add, w=[tid])
                a3 = dve(V.tensor_tensor_scan, am, keep, mag, 0.0, ALU.mult, ALU.add)
                rt = act(S.activation, am, am, ACT.Sqrt, bias=C("eps8"), w=[a3])
                iv = dve(V.reciprocal, am, am, w=[rt])
                a1 = dve(TT, mr, mr, am, ALU.mult, w=[iv, a1])
                a2 = dve(TT, mi, mi, am, ALU.mult, w=[a2])
                q1 = dve(V.tensor_scalar, pq, ps[:, 1, :], C("bq"), None, ALU.add, w=[pq_] + prev)
                bank_free[1] = q1
                q2 = dve(TT, seqs(pq), seqs(pq), table(phi), ALU.add, w=[q1])
                sc = sines(pq, sq_, cq, k_, r_, [q2])
                b1 = dve(TT, ctxb[:, 2, :], mr, cq, ALU.mult, w=[sc, a1] + prev)
                b2 = dve(TT, k_, mi, sq_, ALU.mult, w=[a2])
                b3 = dve(TT, ctxb[:, 3, :], mi, cq, ALU.mult)
                b4 = dve(TT, r_, mr, sq_, ALU.mult)
                b1 = dve(TT, ctxb[:, 2, :], ctxb[:, 2, :], k_, ALU.add, w=[b1, b2])
                b3 = dve(TT, ctxb[:, 3, :], ctxb[:, 3, :], r_, ALU.subtract, w=[b3, b4])
                b5 = pool(G.tensor_tensor, seqs(ctxb[:, 0, :]), seqs(hc), table(cphi), ALU.mult, w=[trig, done[c]] + prev)
                b6 = pool(G.tensor_tensor, seqs(ctxb[:, 1, :]), seqs(hc), table(sphi), ALU.mult)
                cd = [b6, b6, b1, b3]
                for i in range(4):
                    m = mm(ps[:, 2, :], K("mean"), ctxb[:, i, :], start=i == 0, stop=i == 3, w=[bank_free[2], cd[i], cd[0]])
                mean = act(S.mul, wx, ps[:, 2, :], 0.25, w=[m, tid])
                bank_free[2] = mean
                for i in range(4):
                    cdi = dve(TT, ctxb[:, i, :], ctxb[:, i, :], wx, ALU.subtract, w=[mean])
                    s = act(S.activation, sqb[:, i, :], ctxb[:, i, :], ACT.Square, w=[cdi, done[-1]] + prev)
                    m = mm(ps[:, 3, :], K("mean"), sqb[:, i, :], start=i == 0, stop=i == 3, w=[bank_free[3], s])
                rt = act(S.activation, am, ps[:, 3, :], ACT.Sqrt, bias=C("eps5"), scale=0.25, w=[m, a2, b1])
                bank_free[3] = rt
                iv = dve(V.reciprocal, am, am, w=[rt])
                for i in range(4):
                    cdi = dve(TT, ctxb[:, i, :], ctxb[:, i, :], am, ALU.mult, w=[iv])
                for o in range(2):
                    for i in range(4):
                        m = mm(ps[:, 4 + o, :], w1[:, i, o * P:(o + 1) * P], ctxb[:, i, :], start=i == 0, stop=i == 3,
                               w=[bank_free[4 + o], cdi, g_])
                    ge = act(S.activation, hb[:, o, :], ps[:, 4 + o, :], ACT.Gelu, bias=bias1[:, o:o + 1], w=[m, bb])
                    bank_free[4 + o] = ge
                for o in range(2):
                    m = mm(ps[:, 6, :], wp("L2", "w2T")[:, o * P:(o + 1) * P], hb[:, o, :], start=o == 0, stop=o == 1,
                           w=[bank_free[6], ge])
                a = dve(V.scalar_tensor_tensor, mag, ps[:, 6, :], C("L2_b2"), hc, ALU.add, ALU.add, w=[m])
                bank_free[6] = a
                a = dve(TT, X[:, cs], X[:, cs], mag, ALU.add, w=[a])
                prev = [a, m]
                out.append(a)
            return out

        def l3_attn(x_ready):
            start_stage()
            h = arena.take(TOKENS)
            work = (arena.take(TOKENS), arena.take(TOKENS))
            wg = fold[:, 0:3 * P]
            g = dve(V.tensor_scalar, wg, wp("L3a", "qkvaT"), C("gamma"), float(np.float32(np.sqrt(P))), ALU.mult, ALU.mult,
                    w=[loads["L3a"], loads["cols"]])
            done = layernorm(X, h, "eps5", x_ready, work=work)
            sq, sd = work
            a_, kv, q, cum = (arena.take(TOKENS) for _ in range(4))
            out = []
            for c in range(NCHUNK):
                cs = slice(c * CHUNK, (c + 1) * CHUNK)
                s = act(S.activation, sq[:, cs], h[:, cs], ACT.Square, w=[done[c]])
                m = mm(ps[:, 7, :], K("mean"), sq[:, cs], w=[s, bank_free[7]])
                rt = act(S.activation, sd[:, cs], ps[:, 7, :], ACT.Sqrt, scale=float(P), bias=C("zero"), w=[m])
                bank_free[7] = rt
                cl = dve(V.tensor_scalar, sd[:, cs], sd[:, cs], 1e-12, None, ALU.max, w=[rt])
                iv = dve(V.reciprocal, sd[:, cs], sd[:, cs], w=[cl])
                xn = dve(V.tensor_tensor, h[:, cs], h[:, cs], sd[:, cs], ALU.mult, w=[iv])
                k = 3 * (c % 2)
                for j in range(3):
                    m = mm(ps[:, k + j, :], wg[:, j * P:(j + 1) * P], h[:, cs], w=[bank_free[k + j], xn, g])
                sg = act(S.activation, a_[:, cs], ps[:, k + 2, :], ACT.Sigmoid, w=[m])
                e1 = act(S.activation, kv[:, cs], ps[:, k + 1, :], ACT.Copy)
                bank_free[k + 2] = bank_free[k + 1] = e1
                z = pool(G.memset, seqs(a_[:, cs])[:, :, 0:1], 0.0, w=[sg])
                cu = dve(V.tensor_tensor_scan, cum[:, cs], a_[:, cs], kv[:, cs], 0.0, ALU.mult, ALU.add, w=[z, e1])
                pq = dve(V.tensor_tensor, q[:, cs], cum[:, cs], ps[:, k, :], ALU.mult, w=[cu])
                bank_free[k] = pq
                out.append(dve(V.tensor_tensor, X[:, cs], X[:, cs], q[:, cs], ALU.add, w=[pq]))
            return out

        def softmax_small(lg, e, ready, small):
            v = lg.rearrange("p (b e) -> p b e", e=e)
            mx, = (small,)
            a = dve(V.tensor_reduce, mx, v, AXX, ALU.max, w=ready)
            a = dve(V.tensor_tensor, v, v, mx.unsqueeze(2).to_broadcast([P, BATCH, e]), ALU.subtract, w=[a])
            a = act(S.activation, lg, lg, ACT.Exp, w=[a])
            a = dve(V.tensor_reduce, mx, v, AXX, ALU.add, w=[a])
            a = dve(V.reciprocal, mx, mx, w=[a])
            return dve(V.tensor_tensor, v, v, mx.unsqueeze(2).to_broadcast([P, BATCH, e]), ALU.mult, w=[a])

        def route(n_, lo, e, lg, ready, rep, mean, small):
            a = dve(V.tensor_reduce, mean, seqs(n_, BATCH), AXX, ALU.add, w=ready)
            a = dve(V.tensor_scalar, mean, mean, 1.0 / SEQ, None, ALU.mult, w=[a])
            r = dve(V.tensor_copy, rep[:, 0:e, :], wp("L3m", "rw")[:, lo:lo + e].unsqueeze(2).to_broadcast([P, e, P]),
                    w=ready + [loads["L3m"]])
            for i in range(e):
                m = mm(ps[:, 7, i * BATCH:(i + 1) * BATCH], rep[:, i, :], mean, w=[bank_free[7], a, r])
            v = lg.rearrange("p (b e) -> p b e", e=e)
            d = dve(V.tensor_tensor, v, ps[:, 7, 0:e * BATCH].rearrange("p (e b) -> p b e", e=e),
                    wp("L3m", "rb")[:, lo:lo + e].unsqueeze(1).to_broadcast([P, BATCH, e]), ALU.add, w=[m])
            bank_free[7] = d
            return softmax_small(lg, e, [d], small)

        def l3_ffn(x_ready):
            start_stage()
            buffer2 = arena.take(2 * TOKENS)
            work = (buffer2[:, 0:TOKENS], buffer2[:, TOKENS:])
            n1 = arena.take(TOKENS)
            done = layernorm(X, X0, "eps5", x_ready, work=work)
            done = layernorm(X0, n1, "eps6", done, "ln1_g", "ln1_b", work)
            ctxT = [arena.take(SEQ) for _ in range(M_EXPERTS)]
            rep = buffer2[:, 0:EXPERTS * P].rearrange("p (e c) -> p e c", e=EXPERTS)
            mean, small, bop = (arena.take(BATCH) for _ in range(3))
            mp = probs[:, 0:M_EXPERTS * BATCH]
            mp_done = route(n1, 0, M_EXPERTS, mp, done, rep, mean, small)
            mpv = mp.rearrange("p (b e) -> p b e", e=M_EXPERTS)
            a = dve(V.tensor_scalar, bop, mpv[:, :, 0:1].rearrange("p b e -> p (b e)"), C("bo0"), None, ALU.mult, w=[mp_done])
            bop_done = dve(V.scalar_tensor_tensor, bop, mpv[:, :, 1:2].rearrange("p b e -> p (b e)"), C("bo1"), bop,
                           ALU.mult, ALU.add, w=[a])
            out, ct_read, ct_done = [None] * BATCH, [None], [None, None]

            def finish(n, tr):
                b, m = n // M_EXPERTS, n % M_EXPERTS
                cp = act(S.activation, ctxT[m], ps[:, 7, 0:SEQ], ACT.Copy, w=[tr, ct_read[0]])
                ct_done[m] = bank_free[7] = cp

                def project():
                    for j in range(M_EXPERTS):
                        y = mm(ps[:, 7, 0:SEQ], wp("L3m", "wo")[:, j * P:(j + 1) * P], ctxT[j], start=j == 0,
                               stop=j == M_EXPERTS - 1, w=[bank_free[7]] + ct_done)
                    ct_read[0] = y
                    bs = slice(b * SEQ, (b + 1) * SEQ)
                    out[b] = dve(V.scalar_tensor_tensor, X0[:, bs], ps[:, 7, 0:SEQ], bop[:, b:b + 1], X0[:, bs],
                                 ALU.add, ALU.add, w=[y, bop_done])
                    bank_free[7] = out[b]

                if m == M_EXPERTS - 1:
                    heads.att.after(2, project)

            heads = SmallHeads("L3m", "L3", M_EXPERTS, n1, done, (), (), finish, done + [mp_done], buffer2,
                               lambda n: mp[:, n:n + 1])
            heads.run()
            x1 = [out[PER * c + PER - 1] for c in range(NCHUNK)]

            start_stage()
            work = (arena.take(TOKENS), arena.take(TOKENS))
            n2 = arena.take(TOKENS)
            rep = work[0][:, 0:EXPERTS * P].rearrange("p (e c) -> p e c", e=EXPERTS)
            mean, small = (arena.take(BATCH) for _ in range(2))
            done = layernorm(X0, n2, "eps6", x1, "ln2_g", "ln2_b", work)
            ep = probs[:, 0:EXPERTS * BATCH]
            pv_ = ep.rearrange("p (b e) -> p b e", e=EXPERTS)
            epd = route(n2, M_EXPERTS, EXPERTS, ep, done, rep, mean, small)
            gt = arena.take(BATCH * EXPERTS * EXPERTS).rearrange("p (b e f) -> p b e f", b=BATCH, e=EXPERTS)
            eq = arena.take(BATCH * EXPERTS * EXPERTS).rearrange("p (b e f) -> p b e f", b=BATCH, e=EXPERTS)
            rank = arena.take(BATCH * EXPERTS)
            rv = rank.rearrange("p (b e) -> p b e", e=EXPERTS)
            for b in range(BATCH):
                mine = pv_[:, b, :].unsqueeze(2).to_broadcast([P, EXPERTS, EXPERTS])
                other = pv_[:, b, :].unsqueeze(1).to_broadcast([P, EXPERTS, EXPERTS])
                g1 = dve(V.tensor_tensor, gt[:, b], other, mine, ALU.is_gt, w=[epd])
                g2 = dve(V.tensor_tensor, eq[:, b], other, mine, ALU.is_equal)
                g2 = dve(V.tensor_tensor, eq[:, b], eq[:, b], K("earlier").rearrange("p (e f) -> p e f", e=EXPERTS), ALU.mult, w=[g2])
                g1 = dve(V.tensor_tensor, gt[:, b], gt[:, b], eq[:, b], ALU.add, w=[g1, g2])
                g1 = dve(V.tensor_reduce, rv[:, b, :], gt[:, b], AXX, ALU.add, w=[g1])
            g1 = dve(V.scalar_tensor_tensor, ep, rank, float(TOP_K), ep, ALU.is_lt, ALU.mult, w=[g1])
            g1 = dve(V.tensor_reduce, small, pv_, AXX, ALU.add, w=[g1])
            g1 = dve(V.reciprocal, small, small, w=[g1])
            gate = dve(V.tensor_tensor, pv_, pv_, small.unsqueeze(2).to_broadcast([P, BATCH, EXPERTS]), ALU.mult, w=[g1])
            hb = [arena.take(2 * CHUNK).rearrange("p (f s) -> p f s", f=2) for _ in range(2)]
            hb_read = [None, None]
            out = []
            for c in range(NCHUNK):
                cs = slice(c * CHUNK, (c + 1) * CHUNK)
                ob = 6 + c % 2

                def up(e):
                    u = e % 2
                    w_ = []
                    for f in range(2):
                        bk = 2 * u + f
                        m = mm(ps[:, bk, :], wp("L3e", "fw1")[:, e * FF + f * P:e * FF + (f + 1) * P], n2[:, cs],
                               w=[bank_free[bk], done[c], loads["L3e"]])
                    ge = act(S.activation, hb[u], ps[:, 2 * u:2 * u + 2, :], ACT.Gelu, w=[m, hb_read[u]])
                    bank_free[2 * u] = bank_free[2 * u + 1] = ge
                    for bb in range(PER):
                        b = c * PER + bb
                        s = hb[u][:, :, bb * SEQ:(bb + 1) * SEQ]
                        g = dve(V.tensor_scalar, s, s, ep[:, b * EXPERTS + e:b * EXPERTS + e + 1], None, ALU.mult, w=[ge, gate])
                    return g

                def down(e, g):
                    u = e % 2
                    for f in range(2):
                        m = mm(ps[:, ob, :], wp("L3e", "fw2")[:, (2 * e + f) * P:(2 * e + f + 1) * P], hb[u][:, f, :],
                               start=(e == 0 and f == 0), stop=(e == EXPERTS - 1 and f == 1), w=[g, bank_free[ob]])
                    hb_read[u] = m
                    return m

                g = up(0)
                for e in range(EXPERTS):
                    g2 = up(e + 1) if e + 1 < EXPERTS else None
                    m = down(e, g)
                    g = g2
                a = dve(V.tensor_tensor, X0[:, cs], X0[:, cs], ps[:, ob, :], ALU.add, w=[m])
                bank_free[ob] = a
                out.append(dve(V.scalar_tensor_tensor, X[:, cs], X0[:, cs], 0.5, X[:, cs], ALU.mult, ALU.add, w=[a]))
            return out

        order = [l0_ffn, l0_attn, l0_ffn, l1_ffn, l1_attn, l1_ffn, l2_ffn, l2_attn, l2_ffn, l3_ffn, l3_attn, l3_ffn]
        for s in stages:
            x_ready = order[s](x_ready)

        stored = pr.sem("stored")
        for c in range(NCHUNK):
            x_ready[c].waited_for = True
        sems = {}
        for q in pr.engines:
            q.count(sems)

        with nc.Block() as block:
            @block.sync
            def _(eng):
                sp.emit(eng)
                for c in range(NCHUNK):
                    cs = slice(c * CHUNK, (c + 1) * CHUNK)
                    eng.wait_ge(x_ready[c].sem, x_ready[c].value)
                    eng.dma_start(out[:, cs], X[:, cs]).then_inc(stored, 16)
                eng.wait_ge(stored, 16 * NCHUNK)
                for t in loads.values():
                    eng.wait_ge(t.sem, t.value)

            @block.tensor
            def _(eng):
                pe.emit(eng)

            @block.scalar
            def _(eng):
                act.emit(eng)

            @block.vector
            def _(eng):
                dve.emit(eng)

            @block.gpsimd
            def _(eng):
                pool_queue.emit(eng)


def constants():
    c = {}
    eye = np.eye(P)
    c["ident"], c["mean"] = eye, np.full((P, P), 1.0 / P)
    c["center"] = eye - 1.0 / P
    i, j = np.arange(P)[:, None], np.arange(P)[None, :]
    c["causal_q"] = np.where(j > i, MASKED, 0.0)
    c["causal_k"] = c["causal_q"].T
    q, k = P + i, WINDOW + np.arange(3 * WINDOW)[None, :]
    c["local_q1"] = np.where((q < k) | (q > k + WINDOW), MASKED, 0.0)
    q, k = np.arange(3 * WINDOW)[None, :], i
    c["local_k0"] = np.where((q < k) | (q > k + WINDOW), MASKED, 0.0)
    c["negsel"] = np.where(i % 32 == np.arange(32)[None, :], -1.0, 0.0)
    f4 = np.float32
    half = np.arange(0, L0_DIM, 2, dtype=f4)
    inv_freq = (f4(1.0) / f4(10000.0) ** (half / f4(L0_DIM))).astype(f4)
    t = np.arange(SEQ, dtype=f4)
    fr = (t[:, None] * inv_freq[None, :]).astype(f4)
    fr = np.concatenate([fr, fr], -1).astype(np.float64)
    base = (half + f4(0.4 * L0_DIM)) / f4(1.4 * L0_DIM)
    power = (t - SEQ // 2) / f4(WINDOW // 2)
    sc = base.astype(np.float64)[None, :] ** power.astype(np.float64)[:, None]
    sc = np.concatenate([sc, sc], -1)
    sign = np.where(np.arange(L0_DIM) < L0_DIM // 2, -1.0, 1.0)
    two = lambda a: np.concatenate([a.T, a.T], 0)
    c["cos_q"], c["sin_q"] = two(8.0 * np.cos(fr) * sc), two(8.0 * np.sin(fr) * sc * sign)
    c["cos_k"], c["sin_k"] = two(np.cos(fr) / sc), two(np.sin(fr) / sc * sign)
    c["pos"] = np.broadcast_to(t, (P, SEQ))
    hs = np.zeros((P, 8, 16))
    for b in range(8):
        for hh in range(2):
            hs[64 * hh:64 * hh + 64, b, 2 * b + hh] = 1.0
    c["headsum"] = hs.reshape(P, P)
    c["meanrow"] = np.broadcast_to(np.eye(4).reshape(1, 16) / P, (P, 16))
    n = np.arange(16)
    re = np.array([np.cos(2 * np.pi * f * n / 16) for f in range(9)])
    im = np.array([-np.sin(2 * np.pi * f * n / 16) for f in range(9)])
    d = {x: np.zeros((P, P)) for x in ("dft_k1", "dft_k2", "dft_v1", "dft_v2", "idft1", "idft2")}
    for h in range(8):
        r = slice(16 * h, 16 * h + 16)
        for f in range(8):
            a, b = 8 * h + f, 64 + 8 * h + f
            d["dft_k1"][r, a], d["dft_k1"][r, b] = re[f], (re[8] if f == 0 else im[f])
            if f:
                d["dft_k2"][r, a], d["dft_k2"][r, b] = -im[f], re[f]
                d["dft_v1"][r, a], d["dft_v1"][r, b] = re[f], re[f]
                d["dft_v2"][r, a], d["dft_v2"][r, b] = im[f], im[f]
                cr, ci = 2 * np.cos(2 * np.pi * f * n / 16) / 16, -2 * np.sin(2 * np.pi * f * n / 16) / 16
                d["idft1"][r, a], d["idft1"][r, b] = cr, ci
                d["idft2"][r, a], d["idft2"][r, b] = -ci, cr
            else:
                d["dft_v1"][r, a], d["dft_v1"][r, b] = re[0], re[8]
                d["idft1"][r, a], d["idft1"][r, b] = 1.0 / 16, re[8] / 16
    c.update(d)
    c["earlier"] = np.broadcast_to((np.arange(8)[None, :] < np.arange(8)[:, None]).astype(float).reshape(1, 64), (P, 64))
    return c


def layout(a):
    f = np.float32
    a = {k: np.asarray(v) for k, v in a.items()}
    col = {}
    g = {}
    rot = np.concatenate([np.arange(32, 64), np.arange(0, 32)])
    for l in range(DEPTH):
        qs, ks = a["L0_ffn_q_scale"][l], a["L0_ffn_k_scale"][l]
        col[f"L0_qs{l}"], col[f"L0_qsr{l}"] = np.tile(qs, 2), np.tile(qs[rot], 2)
        col[f"L0_ks{l}"], col[f"L0_ksr{l}"] = np.tile(ks, 2), np.tile(ks[rot], 2)
        col[f"L0_lg{l}"], col[f"L0_lb{l}"], col[f"L0_b2{l}"] = a["L0_ffn_ln_g"][l], a["L0_ffn_ln_b"][l], a["L0_ffn_b2"][l]
        for half in range(2):
            for j, (at, n) in enumerate(HID_BLOCKS):
                v = np.zeros(P, f)
                v[:n] = a["L0_ffn_b1"][l][half * HID + at:half * HID + at + n]
                col[f"L0_b1{l}_{3 * half + j}"] = v
        wq = a["L0_ffn_wqkv"][l]
        wr = wq[:, :2 * INNER].reshape(P, 16, 64)[:, :, rot].reshape(P, 2 * INNER)
        wo = a["L0_ffn_wo"][l].reshape(4, P, P).transpose(1, 0, 2).reshape(P, INNER)
        w2 = np.zeros((3 * P, P), f)
        w2[:HID] = a["L0_ffn_w2"][l]
        w2 = w2.reshape(3, P, P).transpose(1, 0, 2).reshape(P, 3 * P)
        g[f"L0f{l}"] = [wq, wr, wo, a["L0_ffn_w1"][l], w2]
    w = a["L0_attn_w_qkv"]
    g["L0a"] = [w[:, :P].T, w[:, P:2 * P].T, w[:, 2 * P:].T, a["L0_attn_w_out"]]
    g["L1f"] = [a["L1_ffn_W_fc"].T, a["L1_ffn_W_proj"].T.reshape(4, P, P).transpose(1, 0, 2).reshape(P, 4 * P)]

    def by_feature(w_):
        return w_.reshape(-1, HEADS, KD).transpose(0, 2, 1).reshape(-1, P)

    w, bq = a["L1_attn_w_qkv"], a["L1_attn_b_qkv"]
    g["L1a"] = [by_feature(w[:, :P]), by_feature(w[:, P:2 * P]), w[:, 2 * P:], a["L1_attn_w_out"]]
    row = [np.ones((1, SEQ)), by_feature(bq[None, :P]), by_feature(bq[None, P:2 * P]), bq[None, 2 * P:]]
    col["L1_bo"] = a["L1_attn_b_out"]
    col["L2_b"], col["ph"], col["bmag"], col["bq"] = a["L2_ffn_b"], a["L2_attn_random_phases"], a["L2_attn_b_mag"], a["L2_attn_b_q"]
    for i in range(4):
        col[f"L2_lg{i}"], col[f"L2_lb{i}"] = a["L2_attn_ln_g"][i * P:(i + 1) * P], a["L2_attn_ln_b"][i * P:(i + 1) * P]
    col["L2_b1_0"], col["L2_b1_1"], col["L2_b2"] = a["L2_attn_b1"][:P], a["L2_attn_b1"][P:], a["L2_attn_b2"]
    w1T = a["L2_attn_W1"].T.reshape(4, P, FF).transpose(1, 0, 2).reshape(P, 4 * FF)
    w2T = a["L2_attn_W2"].T.reshape(2, P, P).transpose(1, 0, 2).reshape(P, 2 * P)
    g["L2"] = [a["L2_ffn_W"].T, a["L2_attn_W_mag"].T, a["L2_attn_W_q"].T, w1T, w2T]
    low = np.concatenate([a["L2_ffn_V_r"].T, a["L2_ffn_C"].T], 1)
    col["gamma"] = a["L3_attn_gamma"]
    g["L3a"] = [a["L3_attn_w_qkva"].T]
    for n in ("ln1_g", "ln1_b", "ln2_g", "ln2_b"):
        col[n] = a[f"L3_ffn_{n}"]
    for m in range(M_EXPERTS):
        row += [by_feature(a["L3_ffn_mha_bq"][m][None]), by_feature(a["L3_ffn_mha_bk"][m][None]),
                a["L3_ffn_mha_bv"][m].reshape(1, P)]
    col["bo0"], col["bo1"] = a["L3_ffn_mha_bo"]
    perm = lambda w_: w_.reshape(M_EXPERTS, P, P)
    g["L3m"] = [np.concatenate([by_feature(m) for m in perm(a["L3_ffn_mha_wq"])], 1),
                np.concatenate([by_feature(m) for m in perm(a["L3_ffn_mha_wk"])], 1),
                np.concatenate(list(perm(a["L3_ffn_mha_wv"])), 1), np.concatenate(list(perm(a["L3_ffn_mha_wo"])), 1),
                a["L3_ffn_mha_rw"], a["L3_ffn_ffn_rw"],
                np.broadcast_to(a["L3_ffn_mha_rb"], (P, M_EXPERTS)), np.broadcast_to(a["L3_ffn_ffn_rb"], (P, EXPERTS))]
    g["L3e"] = [a["L3_ffn_fw1"].transpose(1, 0, 2).reshape(P, EXPERTS * FF),
                a["L3_ffn_fw2"].reshape(EXPERTS, 2, P, P).transpose(2, 0, 1, 3).reshape(P, EXPERTS * FF)]
    col["eps5"], col["eps6"], col["eps8"], col["zero"] = (np.full(P, e) for e in (1e-5, 1e-6, 1e-8, 0.0))
    c = constants()
    headrow = np.zeros((16, 12, P))
    for t in range(4):
        headrow[t, 8 + t] = 1.0
    for j in range(8):
        headrow[2 * j, j, 0:64] = headrow[2 * j + 1, j, 64:P] = 1.0
    out = {
        "x": a["L0_attn_x"].reshape(TOKENS, P).T,
        "const": np.concatenate([c[n] for n in CONST], 1),
        "cols": np.stack([col[n] for n in COLUMNS], 1),
        "headrow": headrow.reshape(16, HEADROW_N),
        "rows": np.concatenate(row, 1),
        "low": low,
    }
    for n, parts in g.items():
        out[n] = np.concatenate(parts, 1)
    return {n: np.ascontiguousarray(v, dtype=f) for n, v in out.items()}


def kernel(**inputs):
    import concourse.bacc as bacc
    from concourse.bass_utils import run_bass_kernel_spmd

    nc = bacc.Bacc("TRN2", target_bir_lowering=False, num_devices=1)
    arrays = layout(inputs)
    ins = {n: nc.dram_tensor(f"in_{n}", v.shape, F32, kind="ExternalInput").ap() for n, v in arrays.items()}
    out = nc.dram_tensor("out", (P, TOKENS), F32, kind="ExternalOutput").ap()
    program(nc, ins, out)
    r = run_bass_kernel_spmd(nc, [{f"in_{n}": v for n, v in arrays.items()}], core_ids=[0])
    return r.results[0]["out"].T.reshape(BATCH, SEQ, P)
```

```python
from contextlib import ExitStack

import numpy as np
import concourse.bass as bass
from concourse import mybir

F32 = mybir.dt.float32
BF16 = mybir.dt.bfloat16
U32 = mybir.dt.uint32
ALU = mybir.AluOpType
ACT = mybir.ActivationFunctionType
AXX = mybir.AxisListType.X

P = 128
BATCH, SEQ = 8, 256
TOKENS = BATCH * SEQ
CHUNK = 512
NCHUNK = TOKENS // CHUNK
PER = CHUNK // SEQ
BANK = 512
BANKS = 8
MASKED = -3.0e38

DEPTH, L0_HEADS, L0_DIM, WINDOW = 2, 8, 64, 64
INNER = L0_HEADS * L0_DIM
HID = int(P * 4 * 2 / 3)
HID_BLOCKS = [(i, min(P, HID - i)) for i in range(0, HID, P)]
SPIKE_HID, SPIKE_STEPS, BETA = 4 * P, 5, 0.9
HEADS, KD = 16, P // 16
M_EXPERTS, EXPERTS, TOP_K, FF = 2, 8, 2, 2 * P
RANK = 32


class Token:

    def __init__(self, stage):
        self.stage, self.waited_for, self.sem, self.value = stage, False, None, None


class Queue:

    def __init__(self, program, name):
        self.program, self.name, self.items, self.last, self.held = program, name, [], None, []

    def __call__(self, method, *args, w=(), **kw):
        token = Token(self.program.stage)
        waits = [t for t in list(w) + self.held if t is not None]
        self.held = []
        for t in waits:
            t.waited_for = True
        self.items.append((method, args, kw, waits, token))
        self.last = token
        return token

    def dma(self, out, in_, sem, w=(), rows=None):
        token = Token(None)
        sem.value += 16
        token.waited_for, token.sem, token.value = True, sem.sem, sem.value
        waits = [t for t in w if t is not None]
        for t in waits:
            t.waited_for = True
        self.items.append((None, (out, in_, rows), {}, waits, token))
        return token

    def count(self, sems):
        reached = {}
        for _, _, _, _, t in self.items:
            if t.waited_for and t.sem is None:
                key = (self.name, t.stage)
                if key not in sems:
                    sems[key] = self.program.sem(f"{self.name}_stage{t.stage}")
                reached[key] = reached.get(key, 0) + 1
                t.sem, t.value = sems[key], reached[key]

    def emit(self, eng):
        passed = {}
        for method, args, kw, waits, token in self.items:
            for t in waits:
                if passed.get(t.sem.name, 0) < t.value:
                    eng.wait_ge(t.sem, t.value)
                    passed[t.sem.name] = t.value
            if method is None:
                out, in_, rows = args
                if rows is None:
                    done = eng.dma_start(out, in_)
                else:
                    done = eng.indirect_dma_start(out, None, in_, bass.IndirectOffsetOnAxis(ap=rows, axis=0))
                done.then_inc(token.sem, 16)
            else:
                done = method(*args, **kw)
                if token.waited_for:
                    done.then_inc(token.sem, 1)


class Counter:

    def __init__(self, sem):
        self.sem, self.value = sem, 0


class Program:
    def __init__(self, nc, ctx):
        self.nc, self.ctx, self.stage = nc, ctx, 0
        self.pe, self.act, self.dve, self.pool, self.sp = (
            Queue(self, n) for n in ("tensor", "scalar", "vector", "gpsimd", "sync"))
        self.engines = [self.pe, self.act, self.dve, self.pool]

    def sem(self, name):
        return self.ctx.enter_context(self.nc.semaphore(name))

    def counter(self, name):
        return Counter(self.sem(name))

    def sbuf(self, name, shape, dtype=F32):
        return self.ctx.enter_context(self.nc.sbuf_tensor(name, shape, dtype))

    def next_stage(self):
        last = [q.last for q in self.engines if q.last is not None]
        for q in self.engines:
            q.held = q.held + last
        self.stage += 1


class Arena:

    def __init__(self, whole, columns):
        self.whole, self.columns, self.used = whole, columns, 0

    def reset(self):
        self.used = 0

    def take(self, columns, rows=P):
        at = self.used
        self.used += columns
        assert self.used <= self.columns, (self.used, self.columns)
        return self.whole[0:rows, at:at + columns]

    def take_bf16(self, columns, rows=P):
        return self.take((columns + 1) // 2, rows).bitcast(BF16)


def packed(parts):
    at, out = 0, {}
    for name, columns in parts:
        out[name] = (at, columns)
        at += columns
    return out, at


COLUMNS = ([f"L0_{n}{l}" for l in range(DEPTH) for n in ("qs", "qsr", "ks", "ksr", "lg", "lb", "b2")]
           + [f"L0_b1{l}_{i}" for l in range(DEPTH) for i in range(2 * len(HID_BLOCKS))]
           + ["L1_bo"]
           + ["L2_b", "ph", "bmag", "bq"] + [f"L2_lg{i}" for i in range(4)] + [f"L2_lb{i}" for i in range(4)]
           + ["L2_b1_0", "L2_b1_1", "L2_b2", "gamma", "ln1_g", "ln1_b", "ln2_g", "ln2_b"]
           + ["bo0", "bo1", "partition"] + [f"{x}{a}" for a in ("L1_0", "L3_0", "L3_1") for x in "qkv"] + [ "past_hi", "past_mid", "eps5", "eps6", "eps8", "zero"])
COL = {n: i for i, n in enumerate(COLUMNS)}
ROUTE = M_EXPERTS + EXPERTS

CONST, CONST_N = packed([("ident", P), ("center", P), ("mean", P), ("causal_q", P), ("causal_k", P),
                         ("local_q1", 3 * WINDOW), ("negsel", 32),
                         ("cos_q", SEQ), ("sin_q", SEQ), ("cos_k", SEQ), ("sin_k", SEQ),
                         ("pos", SEQ), ("normsel", 8 * 32), ("headsel", 4 * P), ("meanrow", 16), ("dft_k1", P), ("dft_k2", P), ("dft_v1", P), ("dft_v2", P),
                         ("idft1", P), ("idft2", P), ("earlier", EXPERTS * EXPERTS), ("expert_row", EXPERTS)])
TILEROW_N = 4 * P
PARTS = 3
SLOTS = ((0, 0), (1, 0), (2, 0), (0, 1), (1, 1), (0, 2))
STACK = 96
W, W_N = {}, {}
for _l in range(DEPTH):
    W[f"L0f{_l}"], W_N[f"L0f{_l}"] = packed([("qkv", 3 * INNER), ("rot", 2 * INNER), ("wo", INNER),
                                             ("w1", 2 * HID), ("w2", len(HID_BLOCKS) * P)])
W["L0a"], W_N["L0a"] = packed([("qT", P), ("kT", P), ("vT", P), ("out", P)])
W["L1f"], W_N["L1f"] = packed([("fcT", SPIKE_HID), ("projT", SPIKE_HID)])
W["L1a"], W_N["L1a"] = packed([("wq", P), ("wk", P), ("wv", P), ("wo", P)])
W["L2"], W_N["L2"] = packed([("fT", P), ("magT", P), ("qT", P), ("w1T", 4 * 2 * P), ("w2T", 2 * P)])
W["L3a"], W_N["L3a"] = packed([("qkvaT", 3 * P)])
W["L3m"], W_N["L3m"] = packed([("wq", M_EXPERTS * P), ("wk", M_EXPERTS * P),
                               ("wv", M_EXPERTS * P), ("wo", M_EXPERTS * P), ("rw", ROUTE), ("rb", ROUTE)])
EXPERT_N = 2 * FF


def program(nc, ins, out, stages=tuple(range(12))):
    with ExitStack() as ctx:
        pr = Program(nc, ctx)
        pe, act, dve, pool, sp = pr.pe, pr.act, pr.dve, pr.pool, pr.sp
        T, V, S, G = nc.tensor, nc.vector, nc.scalar, nc.gpsimd
        pool_queue = pool

        def pool(method, *args, w=(), **kw):
            return pool_queue(method, *args, w=list(w) + [pool_queue.last], **kw)

        X = pr.sbuf("residual", [P, TOKENS])
        X0 = pr.sbuf("stream", [P, TOKENS])
        const = pr.sbuf("const", [P, CONST_N])
        cols = pr.sbuf("cols", [P, len(COLUMNS)])
        tilerow = pr.sbuf("tilerow", [4, TILEROW_N])
        low = pr.sbuf("low_rank", [RANK, 2 * P])
        wt = {n: pr.sbuf(f"w_{n}", [P, k]) for n, k in W_N.items()}
        ident_b = pr.sbuf("ident_b", [P, P], BF16)
        masks_b = pr.sbuf("masks_b", [P, 2 * P + 3 * WINDOW], BF16)
        headsel = pr.sbuf("headsel", [P, 4, P], BF16)
        negsel = pr.sbuf("negsel", [96, 32, P], BF16)
        fold = pr.sbuf("folded", [P, 10 * P])
        probs = pr.sbuf("probs", [P, 16 * BATCH])
        ARENA = 21592
        arena = Arena(pr.sbuf("arena", [P, ARENA]), ARENA)
        ps = ctx.enter_context(nc.psum_tensor("ps", [P, BANKS, BANK], F32))
        bank_free = [None] * BANKS

        def K(name):
            at, n = CONST[name]
            return const[:, at:at + n]

        def C(name):
            return cols[:, COL[name]:COL[name] + 1]

        def wp(group, name):
            at, n = W[group][name]
            return wt[group][:, at:at + n]

        def mm(o, lhsT, rhs, start=True, stop=True, w=()):
            return pe(T.matmul, o, lhsT, rhs, start=start, stop=stop, skip_group_check=True, w=w)

        def seqs(ap, n=PER):
            return ap.rearrange("p (b s) -> p b s", b=n)

        def table(ap, n=PER):
            return ap.unsqueeze(1).to_broadcast([ap.shape[0], n, SEQ])

        loads = {}

        def load(name, dst, src):
            loads[name] = sp.dma(dst, src, pr.counter(f"loaded_{name}"))

        load("x", X[:], ins["x"])
        load("const", const[:], ins["const"])
        load("cols", cols[:], ins["cols"])
        load("tilerow", tilerow[:], ins["tilerow"])
        load("low", low[:], ins["low"])
        for n in ("L0f0", "L0f1", "L0a", "L1f", "L1a", "L2", "L3a", "L3m"):
            load(n, wt[n][:], ins[n])

        t = dve(V.tensor_copy, ident_b[:], K("ident"), w=[loads["const"]])
        dve(V.tensor_copy, masks_b[:],
            const[:, CONST["causal_q"][0]:CONST["causal_q"][0] + 2 * P + 3 * WINDOW])
        headsel_done = dve(V.tensor_copy, headsel[:].rearrange("p j c -> p (j c)"), K("headsel"))
        dve(V.tensor_copy, negsel[:], K("negsel")[0:96, :].unsqueeze(2).to_broadcast([96, 32, P]))
        causal_q, causal_k = masks_b[:, 0:P], masks_b[:, P:2 * P]
        local_q1 = masks_b[:, 2 * P:2 * P + 3 * WINDOW]

        def layernorm(src, dst, eps, ready, scale=None, shift=None, work=None):
            sq, sd = work
            xc = dst
            squared, centred, inverse, done = [], [], [], []
            for c in range(NCHUNK):
                cs = slice(c * CHUNK, (c + 1) * CHUNK)
                a = 2 * c
                before = ready[c] if isinstance(ready[c], list) else [ready[c]]
                m = mm(ps[:, a, :], K("center"), src[:, cs], w=[bank_free[a], loads["const"]] + before)
                squared.append(act(S.activation, sq[:, cs], ps[:, a, :], ACT.Square, w=[m]))
                centred.append(act(S.activation, xc[:, cs], ps[:, a, :], ACT.Copy))
                bank_free[a] = centred[-1]
            for c in range(NCHUNK):
                b = 2 * c + 1
                for t in range(4):
                    var = mm(ps[0:4, b, 0:P], K("meanrow")[:, 4 * t:4 * t + 4], sq[:, c * CHUNK + t * P:c * CHUNK + (t + 1) * P],
                             start=t == 0, stop=t == 3, w=[bank_free[b], squared[c]])
                r4 = sd[0:4, c * P:(c + 1) * P]
                root = act(S.activation, r4, ps[0:4, b, 0:P], ACT.Sqrt, bias=C(eps)[0:4, :], w=[var, loads["cols"]])
                bank_free[b] = root
                inverse.append(dve(V.reciprocal, r4, r4, w=[root]))
            for c in range(NCHUNK):
                cs, b = slice(c * CHUNK, (c + 1) * CHUNK), 2 * c + 1
                for t in range(4):
                    m = mm(ps[:, b, t * P:(t + 1) * P], tilerow[:, t * P:(t + 1) * P], sd[0:4, c * P:(c + 1) * P],
                           w=[bank_free[b], inverse[c], loads["tilerow"]])
                h = dve(V.tensor_tensor, dst[:, cs], xc[:, cs], ps[:, b, :], ALU.mult, w=[m, centred[c]])
                bank_free[b] = h
                if scale is not None:
                    h = dve(V.tensor_scalar, dst[:, cs], dst[:, cs], C(scale), C(shift), ALU.mult, ALU.add, w=[h])
                done.append(h)
            return done

        def start_stage():
            pr.next_stage()
            arena.reset()

        x_ready = [loads["x"]] * NCHUNK

        class Steps:

            def __init__(self):
                self.later = []

            def after(self, steps, fn):
                self.later.append([steps, fn])

            def tick(self):
                for x in self.later:
                    x[0] -= 1
                due = [x[1] for x in self.later if x[0] <= 0]
                self.later = [x for x in self.later if x[0] > 0]
                for fn in due:
                    fn()

            def flush(self):
                while self.later:
                    self.tick()

        class Attention(Steps):

            def __init__(self, heads, dim, scale, q1, k1, masks_q, masks_k, o_heads, banks2):
                self.heads, self.dim, self.scale = heads, dim, scale
                self.q1, self.k1 = q1, k1
                self.masks_q, self.masks_k, self.o_heads = masks_q, masks_k, o_heads
                self.banks2 = banks2
                self.at_once = len(banks2[0])
                self.mx = [arena.take(2 * heads) for _ in range(2)]
                self.split = [arena.take_bf16(SEQ, 96) for _ in range(2)]
                self.rest = arena.take(SEQ, 32)
                self.mid = arena.take_bf16(SEQ, 32)
                self.pt = [arena.take(self.at_once * BANK) for _ in range(2)]
                self.rinv = [arena.take(2 * o_heads) for _ in range(2)]
                self.ctx = [arena.take(2 * P) for _ in range(2)]
                self.max_read, self.split_done, self.split_read = [None] * 2, [None] * 2, [None] * 2
                self.lo_done = None
                self.pt_read, self.ctx_read = [None] * 2, [None] * 2
                self.zeroed = [dve(V.memset, s, 0.0) for s in self.split]
                self.turn, self.later, self.unweighed = 0, [], [False] * 2
                self.raw, self.raw_read = [arena.take(BANK)] * 2, None
                bank_free[6] = dve(V.memset, ps[:, 6, :], 0.0, w=[bank_free[6]])

            def pass1(self, n, q, k, ready):
                i, H = n % 2, self.heads
                mx = self.mx[i].rearrange("p (t h) -> p t h", t=2)
                ks, nk = self.q1
                n0 = SEQ if not self.masks_q else P
                found = []

                def scores(h):
                    bank = h % 2
                    m = mm(ps[:, bank, 0:n0], q(h)[:, 0:P], k(h)[:, 0:n0], stop=not self.masks_q,
                           w=[bank_free[bank]] + ready)
                    if self.masks_q:
                        mm(ps[:, bank, 0:P], ident_b[:], self.masks_q[0], start=False)
                    m = mm(ps[:, bank, n0:n0 + nk], q(h)[:, P:SEQ], k(h)[:, ks:ks + nk], stop=not self.masks_q)
                    if self.masks_q:
                        mk = self.masks_q[1]
                        m = mm(ps[:, bank, n0 + nk - mk.shape[1]:n0 + nk], ident_b[:], mk, start=False)
                    free = self.max_read[i] if h == 0 else None
                    if n0 == nk:
                        m = dve(V.tensor_reduce, mx[:, :, h:h + 1], ps[:, bank, 0:2 * nk].rearrange("p (t s) -> p t s", t=2),
                                AXX, ALU.max, w=[m, free])
                    else:
                        dve(V.tensor_reduce, mx[:, 0, h:h + 1], ps[:, bank, 0:n0], AXX, ALU.max, w=[m, free])
                        m = dve(V.tensor_reduce, mx[:, 1, h:h + 1], ps[:, bank, n0:n0 + nk], AXX, ALU.max)
                    bank_free[bank] = m
                    found.append(m)
                    self.tick()

                def split():
                    for t in range(2):
                        tr = pe(T.transpose, ps[0:H, 7, t * P:(t + 1) * P], mx[:, t, :], K("ident"),
                                w=[bank_free[7]] + found[-1:])
                    self.max_read[i] = tr
                    src, s, r1 = ps[0:H, 7, 0:SEQ], self.split[i], self.rest[0:H, :]
                    hi = dve(V.tensor_copy, s[0:H, :], src, w=[tr, self.split_read[i], self.zeroed[i]])
                    a = dve(V.tensor_tensor, r1, src, s[0:H, :], ALU.subtract, w=[hi, self.lo_done])
                    bank_free[7] = a
                    mid = dve(V.tensor_copy, self.mid[0:H, :], r1, w=[a])
                    dve(V.tensor_copy, s[32:32 + H, :], self.mid[0:H, :], w=[mid])
                    self.lo_done = dve(V.tensor_tensor, s[64:64 + H, :], r1, self.mid[0:H, :], ALU.subtract)
                    self.split_done[i] = self.lo_done

                return [lambda h=h: scores(h) for h in range(H)] + [split]

            def pass2(self, n, q, k, v, ready, finish):
                i, H, G = n % 2, self.heads, self.at_once
                (i0, n0), (i1, n1) = self.k1

                def group(h0):
                    if h0 == 0:
                        self.tick()
                    u = self.turn % 2
                    while self.unweighed[u]:
                        self.tick()
                    banks = self.banks2[u]
                    self.turn += 1
                    for h in range(h0, h0 + G):
                        bank = banks[h - h0]
                        for t, (st, cnt, at) in enumerate(((i0, n0, 0), (i1, n1, n0))):
                            o = ps[:, bank, at:at + cnt]
                            mm(o, k(h)[:, t * P:(t + 1) * P], q(h)[:, st:st + cnt], stop=False,
                               w=[bank_free[bank]] + ready)
                            if self.masks_k:
                                mk = self.masks_k[t]
                                mm(ps[:, bank, at:at + mk.shape[1]], ident_b[:], mk, start=False, stop=False)
                            m = mm(o, negsel[:, h, :], self.split[i][:, st:st + cnt], start=False,
                                   w=[self.split_done[i]])
                    self.split_read[i] = m
                    both = n0 + n1
                    pt = self.pt[u].rearrange("p (h c) -> p h c", h=G)
                    e = act(S.activation, pt[:, :, 0:both], ps[:, banks[0]:banks[-1] + 1, 0:both], ACT.Exp,
                            scale=self.scale, w=[m, self.pt_read[u]])
                    for bank in banks:
                        bank_free[bank] = e
                    self.unweighed[u] = True
                    self.after(4, lambda: self.weigh(n, h0, u, pt, e, v, finish))
                    self.tick()

                return [lambda h=h: group(h) for h in range(0, H, G)]

            def weigh(self, n, h0, u, pt, e, v, finish):
                (i0, n0), (i1, n1) = self.k1
                self.unweighed[u] = False
                for h in range(h0, h0 + self.at_once):
                    g, c, pth = h % 4, h // 4 % 2, pt[:, h - h0, :]
                    for t, (st, cnt, at) in enumerate(((i0, n0, 0), (i1, n1, n0))):
                        o = mm(ps[32 * g:32 * g + self.dim + 1, 6, c * SEQ + st:c * SEQ + st + cnt], v(t, h), pth[:, at:at + cnt],
                               start=t == 0, stop=t == 1, w=[e, bank_free[6]])
                self.pt_read[u] = o
                if h % 8 == 7:
                    r = h // 8
                    self.unit_read(n, o)
                    copied = act(S.activation, self.raw[r], ps[:, 6, :], ACT.Copy, w=[o, self.raw_read])
                    bank_free[6] = copied
                    self.after(3, lambda: self.turn_back(n, r, copied, finish))

            def turn_back(self, n, r, copied, finish):
                for a in range(4):
                    at = (a % 2 * 2 + a // 2) * P
                    tr = pe(T.transpose, ps[:, 7, a * P:(a + 1) * P], self.raw[r][:, at:at + P], K("ident"),
                            w=[copied, bank_free[7]])
                self.raw_read = tr
                rows32 = ps[:, 7, :].rearrange("p (a d) -> p a d", d=32)
                k = n % 2
                rinv = self.rinv[r][:, 0:16]
                inv = dve(V.reciprocal, rinv, rows32[:, :, self.dim:self.dim + 1].rearrange("p a d -> p (a d)"), w=[tr])
                factor = self.factor(n)
                if factor is not None:
                    inv = dve(V.tensor_scalar, rinv, rinv, factor, None, ALU.mult, w=[inv])
                ctxv = self.ctx[k].rearrange("p (t q) -> p t q", t=2)[:, :, r * 64:(r + 1) * 64]
                c = dve(V.tensor_tensor, ctxv.rearrange("p t (a d) -> p t a d", d=self.dim),
                        rows32[:, :, 0:self.dim].rearrange("p (t a) d -> p t a d", t=2),
                        rinv.rearrange("p (t a) -> p t a", t=2).unsqueeze(3).to_broadcast([P, 2, 8, self.dim]),
                        ALU.mult, w=[inv, self.ctx_read[k]])
                bank_free[7] = c
                if r == 1:
                    self.after(3, lambda: self.turn_again(n, k, c, finish))

            def turn_again(self, n, k, c, finish):
                for t in range(2):
                    tr = pe(T.transpose, ps[:, 7, t * P:(t + 1) * P], self.ctx[k][:, t * P:(t + 1) * P], K("ident"), w=[c, bank_free[7]])
                self.ctx_read[k] = tr
                finish(tr)

        def interleave(*lists):
            total = max(len(x) for x in lists)
            at = [0] * len(lists)
            for i in range(total):
                for j, x in enumerate(lists):
                    while at[j] < len(x) and at[j] * total < (i + 1) * len(x):
                        x[at[j]]()
                        at[j] += 1

        def run_units(count, prepare, first, second, att):
            for n in range(count + 2):
                interleave(prepare(n) if n < count else [],
                           first(n - 1) if 0 <= n - 1 < count else [],
                           second(n - 2) if 0 <= n - 2 < count else [])
            att.flush()

        def l0_layer(l, last, x_in):
            start_stage()
            w0 = f"L0f{l}"
            ready = [loads[w0], loads["cols"], loads["const"], loads["tilerow"]]
            H = arena.take(TOKENS)
            oT = [arena.take(4 * SEQ).rearrange("p (j s) -> p j s", j=4) for _ in range(2)]
            tabs = [arena.take(2 * SEQ) for _ in range(2)]
            qk = [arena.take(8 * SEQ).rearrange("p (j s) -> p j s", j=8) for _ in range(3)]
            prod = [arena.take(2 * SEQ) for _ in range(2)]
            sqs = arena.take(8 * SEQ).rearrange("p (j s) -> p j s", j=8)
            rn, rn_rest = arena.take(SEQ), arena.take(SEQ)
            rn_part = [arena.take_bf16(SEQ) for _ in range(3)]
            rq = [arena.take(2 * L0_HEADS).rearrange("p (t h) -> p t h", t=2) for _ in range(2)]
            va = [arena.take(2 * INNER).rearrange("p (t c) -> p t c", t=2) for _ in range(3)]
            S0, S1 = P, 3 * WINDOW
            prob = [arena.take(S0 + S1) for _ in range(3)]
            diag = [arena.take(2 * P) for _ in range(3)]
            probT = [arena.take(S0 + S1) for _ in range(4)]
            stat = [arena.take(6) for _ in range(4)]
            prob_sum = [arena.take(2) for _ in range(4)]
            steps = Steps()
            for bank in (2, 3):
                bank_free[bank] = dve(V.memset, ps[:, bank, :], 0.0, w=[bank_free[bank]])
            for tab, at, tname, cname in ((0, 0, "cos_q", "qs"), (0, 1, "sin_q", "qsr"), (1, 0, "cos_k", "ks"), (1, 1, "sin_k", "ksr")):
                tab_ready = dve(V.tensor_scalar, tabs[tab][:, at * SEQ:(at + 1) * SEQ], K(tname), C(f"L0_{cname}{l}"), None,
                                ALU.mult, w=[loads["cols"], loads["const"]])

            def shifted(src, dst, ready_c, cs):
                lower = act(S.activation, dst[0:64, cs], src[0:64, cs], ACT.Copy, w=[ready_c])
                dv, sv = seqs(dst[64:P, cs]), seqs(src[64:P, cs])
                dve(V.memset, dv[:, :, 0:1], 0.0)
                return [lower, dve(V.tensor_copy, dv[:, :, 1:SEQ], sv[:, :, 0:SEQ - 1], w=[ready_c])]

            h_done = [shifted(X0, H, x_in[c], slice(c * CHUNK, (c + 1) * CHUNK)) for c in range(NCHUNK)]
            normed, v_done = [None] * BATCH, [None] * BATCH
            qk_read, va_read, sq_read, prod_read, rn_read = [None] * 3, [None] * 3, [None], [None] * 2, [None]
            rq_done, rq_read, rn_split, rn_part_read = [None] * 2, [None] * 2, [None], [None]
            o_read, x1 = [None] * 2, [None] * BATCH
            prob_read, diag_read, probT_read = [None] * 3, [None] * 3, [None] * 4

            def prepare(b):
                i, bs = b % 2, slice(b * SEQ, (b + 1) * SEQ)
                Q, squares, placed = qk[b % 3], [], []

                def block(j):
                    bank, k = 4 + j % 2, j % 2
                    mm(ps[:, bank, 0:SEQ], wp(w0, "qkv")[:, j * P:(j + 1) * P], H[:, bs],
                       w=[bank_free[bank]] + h_done[b // PER] + ready)
                    m = mm(ps[:, bank, SEQ:2 * SEQ], wp(w0, "rot")[:, j * P:(j + 1) * P], H[:, bs])
                    sq = act(S.activation, sqs[:, j, :], ps[:, bank, 0:SEQ], ACT.Square, w=[m, sq_read[0]])
                    squares.append(sq)
                    pd = dve(V.tensor_tensor, prod[k], ps[:, bank, :], tabs[j // 4], ALU.mult,
                             w=[sq, prod_read[k], tab_ready])
                    bank_free[bank] = pd
                    prod_read[k] = pool(G.tensor_tensor, Q[:, j, :], prod[k][:, 0:SEQ], prod[k][:, SEQ:2 * SEQ], ALU.add,
                                        w=[pd, qk_read[b % 3]])
                    placed.append(prod_read[k])

                def norms():
                    for j in range(8):
                        g = j % 4
                        m = mm(ps[32 * g:32 * g + 32, 7, 0:SEQ], K("normsel")[:, j * 32:(j + 1) * 32], sqs[:, j, :], start=j < 4, stop=j >= 4,
                               w=[squares[-1], bank_free[7]])
                    sq_read[0] = m
                    root = act(S.activation, rn, ps[:, 7, 0:SEQ], ACT.Sqrt, bias=C("zero"), w=[m, rn_read[0], rn_split[0]])
                    bank_free[7] = root
                    clipped = dve(V.tensor_scalar, rn, rn, 1e-12, None, ALU.max, w=[root])
                    inverse.append(dve(V.reciprocal, rn, rn, w=[clipped]))
                    hi = dve(V.tensor_copy, rn_part[0], rn, w=[inverse[0]])
                    rest = dve(V.scalar_tensor_tensor, rn_rest, rn_part[0], C("past_hi"), rn, ALU.mult, ALU.add, w=[hi])
                    mid = dve(V.tensor_copy, rn_part[1], rn_rest, w=[rest])
                    rn_split[0] = dve(V.scalar_tensor_tensor, rn_part[2], rn_part[1], C("past_mid"), rn_rest, ALU.mult, ALU.add,
                                      w=[mid, rn_part_read[0]])
                    splits.append(rn_split[0])

                inverse, splits = [], []

                def columns():
                    for t in range(2):
                        tr = pe(T.transpose, ps[:, 7, t * P:(t + 1) * P], rn[:, t * P:(t + 1) * P], K("ident"), w=[inverse[0], bank_free[7]])
                    rn_read[0] = tr
                    rq_done[i] = dve(V.tensor_copy, rq[i].rearrange("p t (g e) -> p t g e", g=4),
                                     ps[:, 7, 0:SEQ].rearrange("p (t g r) -> p t g r", t=2, g=4)[:, :, :, 0:2], w=[tr, rq_read[i]])
                    bank_free[7] = rq_done[i]

                def spread(j):
                    for x in range(2):
                        m = mm(ps[:, 7, x * SEQ:(x + 1) * SEQ], headsel[:, j - 4 + x, :], rn_part[2],
                               w=[bank_free[7], splits[0], headsel_done])
                    rn_part_read[0] = m
                    normed[b] = dve(V.tensor_tensor, Q[:, j:j + 2, :], Q[:, j:j + 2, :],
                                    ps[:, 7, :].rearrange("p (x s) -> p x s", x=2), ALU.mult, w=[m, placed[j + 1]])
                    bank_free[7] = normed[b]

                def values(t):
                    tok = slice(b * SEQ + t * P, b * SEQ + (t + 1) * P)
                    bank = 4 + t
                    m = mm(ps[:, bank, :], H[:, tok], wp(w0, "qkv")[:, 2 * INNER:3 * INNER], w=[bank_free[bank]])
                    v_done[b] = act(S.activation, va[b % 3][:, t, :], ps[:, bank, :], ACT.Copy, w=[m, va_read[b % 3]])
                    bank_free[bank] = v_done[b]

                return ([lambda j=j: block(j) for j in range(8)] + [norms],
                        [lambda t=t: values(t) for t in range(2)] + [columns] + [lambda j=j: spread(j) for j in (4, 6)])

            def attend(b):
                i = b % 2

                def scores(h):
                    bank, r, c, u, d, st = h % 2, L0_DIM * (h % 2), h // 2, (8 * b + h) % 3, (8 * b + h) % 3, stat[h % 4]
                    q, k = qk[b % 3][r:r + L0_DIM, c, :], qk[b % 3][r:r + L0_DIM, 4 + c, :]
                    mm(ps[:, bank, 0:S0], q[:, 0:P], k[:, 0:P], stop=False, w=[bank_free[bank], normed[b]])
                    m0 = mm(ps[:, bank, 0:S0], ident_b[:], local_q1[:, WINDOW:], start=False)
                    mm(ps[:, bank, S0:S0 + S1], q[:, P:SEQ], k[:, WINDOW:SEQ], stop=False)
                    m1 = mm(ps[:, bank, S0:S0 + S1], ident_b[:], local_q1, start=False)
                    top, bias, total, inv = st[:, 0:2], st[:, 2:4], prob_sum[h % 4], st[:, 4:6]
                    dve(V.tensor_reduce, top[:, 0:1], ps[:, bank, 0:S0], AXX, ALU.max, w=[m1])
                    t1 = dve(V.tensor_reduce, top[:, 1:2], ps[:, bank, S0:S0 + S1], AXX, ALU.max)
                    shift = dve(V.scalar_tensor_tensor, bias, top, -1.0, rq[i][:, :, h], ALU.mult, ALU.mult, w=[t1, rq_done[i]])
                    for t, (at, n) in enumerate(((0, S0), (S0, S1))):
                        e = act(S.activation, prob[u][:, at:at + n], ps[:, bank, at:at + n], ACT.Exp, bias=bias[:, t:t + 1],
                                scale=rq[i][:, t, h:h + 1], accum_out=total[:, t:t + 1], w=[shift, prob_read[u]])
                    bank_free[bank] = e
                    rv = dve(V.reciprocal, inv, total, w=[e])
                    for t in range(2):
                        dg = dve(V.tensor_scalar, diag[d][:, t * P:(t + 1) * P], K("ident"), inv[:, t:t + 1], None, ALU.mult,
                                 w=[rv, diag_read[d]])
                    if h == L0_HEADS - 1:
                        rq_read[i], qk_read[b % 3] = e, m1
                    steps.after(3, lambda: turn(h, u, d, dg))
                    steps.tick()

                def turn(h, u, d, dg):
                    bank, w_ = 2 + h % 2, h % 4
                    mm(ps[:, bank, 0:P], prob[u][:, 0:P], diag[d][:, 0:P], w=[bank_free[bank], dg])
                    mm(ps[:, bank, P:2 * P], prob[u][:, S0 + WINDOW:S0 + S1], diag[d][:, P:2 * P])
                    m = mm(ps[WINDOW:P, bank, 2 * P:2 * P + WINDOW], prob[u][:, S0:S0 + WINDOW], diag[d][:, P:P + WINDOW])
                    prob_read[u] = diag_read[d] = m
                    cp = act(S.activation, probT[w_], ps[:, bank, 0:S0 + S1], ACT.Copy, w=[m, probT_read[w_]])
                    bank_free[bank] = cp
                    if h % 2 == 1:
                        steps.after(2, lambda: weigh(h - 1, cp))

                def weigh(h0, cp):
                    for part in range(3):
                        for h in (h0, h0 + 1):
                            r, pt = L0_DIM * (h % 2), probT[h % 4]
                            out_ = ps[r:r + L0_DIM, 6, :]
                            v0, v1 = (va[b % 3][:, t, h * L0_DIM:(h + 1) * L0_DIM] for t in range(2))
                            if part == 0:
                                mm(out_[:, 0:P], v0, pt[:, 0:P], w=[bank_free[6], cp, v_done[b]])
                            elif part == 1:
                                mm(out_[:, P:2 * P], v1, pt[:, P:2 * P], stop=False)
                            else:
                                o = mm(out_[:, P:P + WINDOW], v0[WINDOW:P], pt[WINDOW:P, 2 * P:2 * P + WINDOW], start=False)
                            probT_read[h % 4] = o if part == 2 else None
                    k, j = b % 2, h0 // 2
                    copied = act(S.activation, oT[k][:, j, :], ps[:, 6, 0:SEQ], ACT.Copy, w=[o, o_read[k]])
                    bank_free[6] = copied
                    if j == 3:
                        va_read[b % 3] = o
                        steps.after(2, lambda: project(copied))

                def project(copied):
                    k = b % 2
                    for jj in range(4):
                        y = mm(ps[:, 7, 0:SEQ], wp(w0, "wo")[:, jj * P:(jj + 1) * P], oT[k][:, jj, :], start=jj == 0,
                               stop=jj == 3, w=[bank_free[7], copied])
                    o_read[k] = y
                    bs = slice(b * SEQ, (b + 1) * SEQ)
                    x1[b] = dve(V.tensor_tensor, X0[:, bs], X0[:, bs], ps[:, 7, 0:SEQ], ALU.add, w=[y])
                    bank_free[7] = x1[b]

                return [lambda h=h: scores(h) for h in range(L0_HEADS)]

            rest = []
            for n in range(BATCH + 2):
                blocks, later = prepare(n) if n < BATCH else ([], [])
                interleave(rest, blocks, attend(n - 2) if n >= 2 else [])
                rest = later
            steps.flush()
            x1 = [x1[PER * c + PER - 1] for c in range(NCHUNK)]

            start_stage()
            H2 = arena.take(TOKENS)
            N2 = arena.take(TOKENS)
            work = (arena.take(TOKENS), arena.take(TOKENS))
            g = [arena.take(CHUNK) for _ in range(2)]
            hh = [arena.take(3 * CHUNK) for _ in range(2)]
            h_done = [shifted(X0, H2, x1[c], slice(c * CHUNK, (c + 1) * CHUNK)) for c in range(NCHUNK)]
            n_done = layernorm(H2, N2, "eps5", h_done, f"L0_lg{l}", f"L0_lb{l}", work)
            out_done = []
            g_read, hh_read = [None, None], [None, None]
            for c in range(NCHUNK):
                cs = slice(c * CHUNK, (c + 1) * CHUNK)
                k = c % 2
                for j, (at, n) in enumerate(HID_BLOCKS):
                    a, gb = 2 * (j % 2), 2 * (j % 2) + 1
                    u = j % 2
                    pa = mm(ps[0:n, a, :], wp(w0, "w1")[:, at:at + n], N2[:, cs], w=[bank_free[a], n_done[c], loads[w0]])
                    pg = mm(ps[0:n, gb, :], wp(w0, "w1")[:, HID + at:HID + at + n], N2[:, cs], w=[bank_free[gb]])
                    ge = act(S.activation, g[u][0:n, :], ps[0:n, gb, :], ACT.Gelu,
                             bias=C(f"L0_b1{l}_{3 + j}")[0:n, :], w=[pg, g_read[u]])
                    bank_free[gb] = ge
                    pr_ = dve(V.scalar_tensor_tensor, hh[k][0:n, j * CHUNK:(j + 1) * CHUNK], ps[0:n, a, :],
                              C(f"L0_b1{l}_{j}")[0:n, :], g[u][0:n, :], ALU.add, ALU.mult, w=[ge, pa, hh_read[k]])
                    bank_free[a] = pr_
                    g_read[u] = pr_
                ob = 4 + c % 2
                for j, (at, n) in enumerate(HID_BLOCKS):
                    y = mm(ps[:, ob, :], wp(w0, "w2")[0:n, j * P:(j + 1) * P], hh[k][0:n, j * CHUNK:(j + 1) * CHUNK],
                           start=j == 0, stop=j == 2, w=[bank_free[ob], pr_])
                hh_read[k] = y
                xx = dve(V.scalar_tensor_tensor, X0[:, cs], ps[:, ob, :], C(f"L0_b2{l}"), X0[:, cs], ALU.add, ALU.add, w=[y])
                bank_free[ob] = xx
                if last:
                    xx = dve(V.scalar_tensor_tensor, X[:, cs], X0[:, cs], 0.5, X[:, cs], ALU.mult, ALU.add, w=[xx])
                out_done.append(xx)
            return out_done

        def l0_ffn(x_ready):
            start_stage()
            done = layernorm(X, X0, "eps5", x_ready, work=(arena.take(TOKENS), arena.take(TOKENS)))
            for l in range(DEPTH):
                done = l0_layer(l, l == DEPTH - 1, done)
            return done

        def l0_attn(x_ready):
            start_stage()
            h = arena.take(TOKENS)
            done = layernorm(X, h, "eps5", x_ready, work=(arena.take(TOKENS), arena.take(TOKENS)))
            spec = [("kT", "dft_k1"), ("kT", "dft_k2"), ("vT", "dft_v1"), ("vT", "dft_v2"), ("qT", "dft_v1"), ("qT", "dft_v2")]
            for i, (wn, dn) in enumerate(spec):
                bk = 0 if i < 4 else 1
                m = mm(ps[:, bk, (i % 4) * P:(i % 4 + 1) * P], wp("L0a", wn), DFT[dn],
                       w=[bank_free[bk], loads["L0a"], loads["const"]])
            for i, dn in enumerate(("idft1", "idft2")):
                m = mm(ps[:, 1, (2 + i) * P:(3 + i) * P], K(dn), wp("L0a", "out"))
            e0 = act(S.activation, fold[:, 0:BANK], ps[:, 0, :], ACT.Copy, w=[m])
            folded = act(S.activation, fold[:, BANK:2 * BANK], ps[:, 1, :], ACT.Copy)
            bank_free[0] = bank_free[1] = folded
            k1, kv, cum, t2 = (arena.take(TOKENS) for _ in range(4))
            keep = arena.take(TOKENS)
            kp = dve(V.memset, keep, 1.0)
            kp = dve(V.memset, seqs(keep, BATCH)[:, :, 0:1], 0.0, w=[kp])
            out = []
            for c in range(NCHUNK):
                cs = slice(c * CHUNK, (c + 1) * CHUNK)
                prj = []
                for i in range(6):
                    prj.append(mm(ps[:, i, :], fold[:, i * P:(i + 1) * P], h[:, cs],
                                  w=[bank_free[i], done[c], folded]))
                c1 = act(S.activation, k1[:, cs], ps[:, 0, :], ACT.Copy, w=[prj[0]])
                c2 = act(S.activation, t2[:, cs], ps[:, 1, :], ACT.Copy, w=[prj[1]])
                bank_free[0], bank_free[1] = c1, c2
                a1 = dve(V.tensor_tensor, k1[:, cs], k1[:, cs], ps[:, 2, :], ALU.mult, w=[c1, prj[2]])
                a2 = dve(V.tensor_tensor, t2[:, cs], t2[:, cs], ps[:, 3, :], ALU.mult, w=[c2, prj[3]])
                bank_free[2], bank_free[3] = a1, a2
                s_ = pool(G.tensor_tensor, kv[:, cs], k1[:, cs], t2[:, cs], ALU.add, w=[a1, a2])
                cu = dve(V.tensor_tensor_scan, cum[:, cs], keep[:, cs], kv[:, cs], 0.0, ALU.mult, ALU.add, w=[s_, kp])
                b1 = dve(V.tensor_tensor, k1[:, cs], cum[:, cs], ps[:, 4, :], ALU.mult, w=[cu, prj[4]])
                b2 = dve(V.tensor_tensor, t2[:, cs], cum[:, cs], ps[:, 5, :], ALU.mult, w=[prj[5]])
                bank_free[4], bank_free[5] = b1, b2
                ob = 6 + c % 2
                mm(ps[:, ob, :], fold[:, 6 * P:7 * P], k1[:, cs], stop=False, w=[bank_free[ob], b1])
                y = mm(ps[:, ob, :], fold[:, 7 * P:8 * P], t2[:, cs], start=False, w=[b2])
                xx = dve(V.tensor_tensor, X[:, cs], X[:, cs], ps[:, ob, :], ALU.add, w=[y])
                bank_free[ob] = xx
                out.append(xx)
            return out

        DFT = {"dft_k1": K("dft_k1"), "dft_k2": K("dft_k2"), "dft_v2": K("dft_v2"), "dft_v1": K("dft_v1")}

        def l1_ffn(x_ready):
            start_stage()
            h = arena.take(TOKENS)
            done = layernorm(X, h, "eps5", x_ready, work=(arena.take(TOKENS), arena.take(TOKENS)))
            relu = [arena.take(4 * CHUNK) for _ in range(2)]
            y, mem, u, acc = (arena.take(TOKENS) for _ in range(4))
            out = []
            rl_read = [None, None]
            for c in range(NCHUNK):
                cs = slice(c * CHUNK, (c + 1) * CHUNK)
                k = c % 2
                sq = []
                for j in range(4):
                    p1 = mm(ps[:, j, :], wp("L1f", "fcT")[:, j * P:(j + 1) * P], h[:, cs],
                            w=[bank_free[j], done[c], loads["L1f"]])
                    js = slice(j * CHUNK, (j + 1) * CHUNK)
                    r = act(S.activation, relu[k][:, js], ps[:, j, :], ACT.Relu, w=[p1, rl_read[k]])
                    bank_free[j] = r
                    sq.append(act(S.activation, relu[k][:, js], relu[k][:, js], ACT.Square, w=[r]))
                ob = 4 + c % 2
                for j in range(4):
                    yy = mm(ps[:, ob, :], wp("L1f", "projT")[:, j * P:(j + 1) * P], relu[k][:, j * CHUNK:(j + 1) * CHUNK],
                            start=j == 0, stop=j == 3, w=[sq[j], bank_free[ob]])
                rl_read[k] = yy
                d = act(S.activation, y[:, cs], ps[:, ob, :], ACT.Copy, w=[yy])
                bank_free[ob] = d
                d = dve(V.tensor_scalar, mem[:, cs], y[:, cs], -1.0, None, ALU.mult, w=[d])
                a = dve(V.tensor_scalar, acc[:, cs], mem[:, cs], -1.0, None, ALU.is_lt, w=[d])
                for s_ in range(SPIKE_STEPS - 1):
                    d = dve(V.scalar_tensor_tensor, u[:, cs], mem[:, cs], BETA, y[:, cs], ALU.mult, ALU.subtract, w=[d])
                    d = dve(V.scalar_tensor_tensor, mem[:, cs], mem[:, cs], -1.0, u[:, cs], ALU.is_lt, ALU.add, w=[d])
                    a = dve(V.scalar_tensor_tensor, acc[:, cs], mem[:, cs], -1.0, acc[:, cs], ALU.is_lt, ALU.add, w=[d, a])
                out.append(dve(V.scalar_tensor_tensor, X[:, cs], acc[:, cs], 0.5 / SPIKE_STEPS, X[:, cs], ALU.mult, ALU.add, w=[a]))
            return out

        scratch = nc.dram_tensor("scratch", (3, 2, PARTS, P, SEQ), BF16, kind="Internal").ap()
        written = [pr.counter(f"parts_written{i}") for i in range(3)]
        stacked = [pr.counter(f"stack_loaded{i}") for i in range(3)]

        class SmallHeads:

            def __init__(self, group, name, members, h, h_ready, masks_q, masks_k, finish, free_after, buffer2, factor):
                self.group, self.name, self.members, self.h, self.h_ready = group, name, members, h, h_ready
                self.finish = finish
                whole = [arena.take(2 * HEADS * SEQ // 2) for _ in range(2)] + [buffer2]
                stacks = [t.bitcast(BF16).rearrange("p (x h s) -> p x h s", x=2, h=HEADS) for t in whole]
                self.q, self.k = [t[0:STACK, 0] for t in stacks], [t[0:STACK, 1] for t in stacks]
                self.cleared = [pool(G.memset, whole[i][0:STACK, :], 0.0, w=free_after if i == 2 else []) for i in range(3)]
                self.parts = [arena.take_bf16(2 * PARTS * SEQ).rearrange("p (x a s) -> p x a s", x=2, a=PARTS) for _ in range(1)]
                self.rest = arena.take(2 * SEQ)
                self.va = [arena.take(2 * HEADS * (KD + 1)).rearrange("p (t h d) -> p t h d", t=2, h=HEADS) for _ in range(3)]
                for v in self.va:
                    self.ones = dve(V.memset, v[:, :, :, KD:KD + 1], 1.0)
                self.att = Attention(HEADS, KD, float(1.0 / np.sqrt(np.float32(KD))), (0, SEQ),
                                     ((0, SEQ), (P, P) if masks_q else (0, SEQ)), masks_q, masks_k, 8, ((2, 3), (4, 5)))
                self.att.factor, self.att.unit_read = factor, self.unit_read
                self.loaded, self.v_done = [None] * 3, [None] * 3
                self.stack_read, self.parts_written, self.rest_read = [None] * 3, [None] * 2, None

            def unit_read(self, n, o):
                self.stack_read[n % 3] = o

            def prepare(self, n):
                b, m, i, k = n // self.members, n % self.members, n % 3, 0
                bs, ms = slice(b * SEQ, (b + 1) * SEQ), slice(m * P, (m + 1) * P)
                g, tag, ready = self.group, f"{self.name}_{m}", [self.h_ready[b // PER], loads[self.group], loads["cols"]]
                parts, rest = self.parts[k], self.rest
                both = lambda ap: ap.rearrange("p (x s) -> p x s", x=2)

                def qk():
                    for x, xn in enumerate("qk"):
                        o = ps[:, 7, x * SEQ:(x + 1) * SEQ]
                        mp_ = mm(o, wp(g, "w" + xn)[:, ms], self.h[:, bs], w=[bank_free[7]] + ready)
                    for x, xn in enumerate("qk"):
                        hi = act(S.activation, parts[:, x, 0, :], ps[:, 7, x * SEQ:(x + 1) * SEQ], ACT.Identity,
                                 bias=C(xn + tag), w=[mp_, self.parts_written[k]])
                    for x, xn in enumerate("qk"):
                        r1 = dve(V.scalar_tensor_tensor, both(rest)[:, x, :], ps[:, 7, x * SEQ:(x + 1) * SEQ], C(xn + tag),
                                 parts[:, x, 0, :], ALU.add, ALU.subtract, w=[hi, self.rest_read])
                    bank_free[7] = r1
                    mid = act(S.activation, parts[:, :, 1, :], both(rest), ACT.Copy, w=[r1])
                    lo = pool(G.tensor_tensor, parts[:, :, 2, :], both(rest), parts[:, :, 1, :], ALU.subtract, w=[mid])
                    self.rest_read = lo
                    out_ = sp.dma(scratch[i].rearrange("x a p s -> p (x a) s"), parts.rearrange("p x a s -> p (x a) s"),
                                  written[i], w=[lo, self.loaded[i]])
                    self.parts_written[k] = out_
                    rows_ = scratch[i].rearrange("x a (r h) s -> x (a r) h s", h=HEADS)
                    for x, st in enumerate((self.q[i], self.k[i])):
                        s0 = 0
                        while s0 < len(SLOTS):
                            a0, s1 = SLOTS[s0][x], s0 + 1
                            while s1 < len(SLOTS) and SLOTS[s1][x] == a0 + s1 - s0:
                                s1 += 1
                            self.loaded[i] = sp.dma(st[KD * s0:KD * s1], rows_[x, KD * a0:KD * (a0 + s1 - s0)], stacked[i],
                                                    w=[out_, self.stack_read[i], self.cleared[i]])
                            s0 = s1

                def values():
                    for t in range(2):
                        o = ps[:, 7, t * P:(t + 1) * P]
                        mv = mm(o, self.h[:, b * SEQ + t * P:b * SEQ + (t + 1) * P], wp(g, "wv")[:, ms], w=[bank_free[7]])
                    self.v_done[i] = act(S.activation, self.va[i][:, :, :, 0:KD],
                                         ps[:, 7, 0:2 * P].rearrange("p (t h d) -> p t h d", t=2, d=KD), ACT.Copy,
                                         w=[mv, self.stack_read[i], self.ones])
                    bank_free[7] = self.v_done[i]

                return [qk, values]

            def run(self):
                at = self.att

                run_units(BATCH * self.members, self.prepare,
                          lambda n: at.pass1(n, lambda h: self.q[n % 3][:, h, :], lambda h: self.k[n % 3][:, h, :],
                                             [self.loaded[n % 3]]),
                          lambda n: at.pass2(n, lambda h: self.q[n % 3][:, h, :], lambda h: self.k[n % 3][:, h, :],
                                             lambda kt, h: self.va[n % 3][:, kt, h, :], [self.v_done[n % 3]],
                                             lambda tr: self.finish(n, tr)), at)

        def l1_attn(x_ready):
            start_stage()
            h = arena.take(TOKENS)
            buffer2 = arena.take(2 * TOKENS)
            done = layernorm(X, h, "eps5", x_ready, work=(buffer2[:, 0:TOKENS], buffer2[:, TOKENS:]))
            ctxT = [arena.take(SEQ) for _ in range(2)]
            out, ct_read = [None] * BATCH, [None, None]

            def finish(b, tr):
                k = b % 2
                cp = act(S.activation, ctxT[k], ps[:, 7, 0:SEQ], ACT.Identity, bias=C("vL1_0"), w=[tr, ct_read[k]])
                bank_free[7] = cp

                def project(cp):
                    y = mm(ps[:, 7, 0:SEQ], wp("L1a", "wo"), ctxT[k], w=[cp, bank_free[7]])
                    ct_read[k] = y
                    bs = slice(b * SEQ, (b + 1) * SEQ)
                    out[b] = dve(V.scalar_tensor_tensor, X[:, bs], ps[:, 7, 0:SEQ], C("L1_bo"), X[:, bs],
                                 ALU.add, ALU.add, w=[y])
                    bank_free[7] = out[b]

                small.att.after(2, lambda: project(cp))

            small = SmallHeads("L1a", "L1", 1, h, done, (causal_q, causal_q), (causal_k, causal_k), finish, done, buffer2,
                               lambda n: None)
            small.run()
            return [out[PER * c + PER - 1] for c in range(NCHUNK)]

        def l2_ffn(x_ready):
            start_stage()
            mm(ps[:, 7, 0:P], K("ident"), wp("L2", "fT"), stop=False, w=[bank_free[7], loads["L2"]])
            m = mm(ps[:, 7, 0:P], low[:, 0:P], low[:, P:2 * P], start=False, w=[loads["low"]])
            wf = fold[:, 8 * P:9 * P]
            f = act(S.activation, wf, ps[:, 7, 0:P], ACT.Copy, w=[m])
            half_b = arena.take(1)
            hb = act(S.mul, half_b, C("L2_b"), 0.5, w=[loads["cols"]])
            bank_free[7] = f
            h = arena.take(TOKENS)
            done = layernorm(X, h, "eps5", x_ready, work=(arena.take(TOKENS), arena.take(TOKENS)))
            y = arena.take(TOKENS)
            out = []
            for c in range(NCHUNK):
                cs = slice(c * CHUNK, (c + 1) * CHUNK)
                b = 2 * c
                m = mm(ps[:, b, :], wf, h[:, cs], w=[bank_free[b], done[c], f])
                e = act(S.activation, y[:, cs], ps[:, b, :], ACT.Identity, bias=half_b, scale=0.5, w=[m, hb])
                bank_free[b] = e
                out.append(dve(V.tensor_tensor, X[:, cs], X[:, cs], y[:, cs], ALU.add, w=[e]))
            return out

        TWO_PI = 6.283185307179586
        HI = float(np.float32(6.28125))
        MIDP = float(np.float32(TWO_PI - HI))
        LOP = float(np.float32(TWO_PI - HI - MIDP))
        MAGIC = 12582912.0
        PI = float(np.nextafter(np.float32(np.pi), np.float32(0)))

        def sines(src, sin_out, cos_out, k, r, ready):
            last = []
            for o, quarter in ((sin_out, 0.0), (cos_out, 0.25)):
                a = dve(V.tensor_scalar, k, src, 1.0 / TWO_PI, quarter, ALU.mult, ALU.add, w=ready + last)
                a = dve(V.tensor_scalar, k, k, MAGIC, -MAGIC, ALU.add, ALU.add, w=[a])
                a = dve(V.scalar_tensor_tensor, r, k, -HI, src, ALU.mult, ALU.add, w=[a] + last)
                a = dve(V.scalar_tensor_tensor, r, k, -MIDP, r, ALU.mult, ALU.add, w=[a])
                a = dve(V.scalar_tensor_tensor, r, k, -LOP, r, ALU.mult, ALU.add, w=[a])
                if quarter:
                    a = dve(V.tensor_scalar, r, r, TWO_PI / 4, None, ALU.add, w=[a])
                a = dve(V.tensor_scalar, r, r, PI, -PI, ALU.min, ALU.max, w=[a])
                last = [act(S.activation, o, r, ACT.Sin, w=[a])]
            return last[0]

        def l2_attn(x_ready):
            start_stage()
            h = arena.take(TOKENS)
            work = (arena.take(TOKENS), arena.take(TOKENS))
            done = layernorm(X, h, "eps5", x_ready, work=work)
            phi, cphi, sphi, kq, rq = (arena.take(SEQ) for _ in range(5))
            keep = arena.take(CHUNK)
            kp = dve(V.memset, keep, 1.0)
            kp = dve(V.memset, seqs(keep)[:, :, 0:1], 0.0, w=[kp])
            a = dve(V.tensor_scalar, phi, K("pos"), C("ph"), None, ALU.mult, w=[loads["const"], loads["cols"]])
            phi_done = dve(V.tensor_scalar, phi, phi, 0.01, None, ALU.mult, w=[a])
            trig = sines(phi, sphi, cphi, kq, rq, [phi_done])
            w1 = arena.take(4 * FF).rearrange("p (i f) -> p i f", i=4)
            bias1 = arena.take(2)
            for i in range(4):
                g_ = dve(V.tensor_scalar, w1[:, i, :], wp("L2", "w1T")[:, i * FF:(i + 1) * FF], C(f"L2_lg{i}"), None, ALU.mult,
                         w=[loads["L2"], loads["cols"]])
            for o in range(2):
                for i in range(4):
                    m = mm(ps[:, 7, o:o + 1], wp("L2", "w1T")[:, i * FF + o * P:i * FF + (o + 1) * P], C(f"L2_lb{i}"),
                           start=i == 0, stop=i == 3, w=[bank_free[7], loads["L2"], loads["cols"]])
            for o in range(2):
                bb = dve(V.tensor_tensor, bias1[:, o:o + 1], ps[:, 7, o:o + 1], C(f"L2_b1_{o}"), ALU.add, w=[m])
            bank_free[7] = bb
            n = CHUNK
            mag, wx, tr, ti, mr, mi, am, pq, sq_, cq, k_, r_, mean_, total = (arena.take(n) for _ in range(14))
            four = lambda t: t.rearrange("p (i s) -> p i s", i=4)
            ctxb = [four(arena.take(4 * n)), four(work[1])]
            sqb = four(work[0])
            hb = arena.take(2 * n).rearrange("p (i s) -> p i s", i=2)
            dev = arena.take(P)
            TT = V.tensor_tensor
            blocks = [None] * NCHUNK
            mag_read, mean_read, sq_read, dev_read, hb_read = None, None, None, None, None
            ctx_read, out = [done[-1]] * 2, [None] * NCHUNK

            projected = [None] * NCHUNK

            def project(c):
                hc = h[:, c * CHUNK:(c + 1) * CHUNK]
                projected[c] = (mm(ps[:, 0, :], wp("L2", "magT"), hc, w=[bank_free[0], done[c], loads["L2"]]),
                                mm(ps[:, 1, :], wp("L2", "qT"), hc, w=[bank_free[1]]))

            def retrieve(c):
                nonlocal mag_read
                cs, ctx_ = slice(c * CHUNK, (c + 1) * CHUNK), ctxb[c % 2]
                hc = h[:, cs]
                pm, pq_ = projected[c]
                sg = act(S.activation, mag, ps[:, 0, :], ACT.Sigmoid, bias=C("bmag"), w=[pm, mag_read])
                bank_free[0] = sg
                b5 = pool(G.tensor_tensor, seqs(ctx_[:, 0, :]), seqs(hc), table(cphi), ALU.mult, w=[trig, done[c], ctx_read[c % 2]])
                b6 = pool(G.tensor_tensor, seqs(ctx_[:, 1, :]), seqs(hc), table(sphi), ALU.mult)
                q1 = dve(V.tensor_scalar, pq, ps[:, 1, :], C("bq"), None, ALU.add, w=[pq_])
                bank_free[1] = q1
                if c + 1 < NCHUNK:
                    project(c + 1)
                q2 = dve(TT, seqs(pq), seqs(pq), table(phi), ALU.add, w=[q1])
                yield
                mg = dve(V.tensor_scalar, mag, mag, 5.0, None, ALU.mult, w=[sg])
                wxd = dve(TT, wx, mag, hc, ALU.mult, w=[mg])
                mag_read = a3 = dve(V.tensor_tensor_scan, am, keep, mag, 0.0, ALU.mult, ALU.add, w=[kp])
                rt = act(S.activation, am, am, ACT.Sqrt, bias=C("eps8"), w=[a3])
                trd = dve(TT, seqs(tr), seqs(wx), table(cphi), ALU.mult, w=[wxd, trig])
                tid = dve(TT, seqs(ti), seqs(wx), table(sphi), ALU.mult)
                yield
                a1 = dve(V.tensor_tensor_scan, mr, keep, tr, 0.0, ALU.mult, ALU.add, w=[trd])
                a2 = dve(V.tensor_tensor_scan, mi, keep, ti, 0.0, ALU.mult, ALU.add, w=[tid])
                yield
                iv = dve(V.reciprocal, am, am, w=[rt])
                a1 = dve(TT, mr, mr, am, ALU.mult, w=[iv, a1])
                a2 = dve(TT, mi, mi, am, ALU.mult, w=[a2])
                yield
                sc = sines(pq, sq_, cq, k_, r_, [q2])
                yield
                b1 = dve(TT, ctx_[:, 2, :], mr, cq, ALU.mult, w=[sc, a1, ctx_read[c % 2]])
                b2 = dve(TT, k_, mi, sq_, ALU.mult, w=[a2])
                b3 = dve(TT, ctx_[:, 3, :], mi, cq, ALU.mult)
                b4 = dve(TT, r_, mr, sq_, ALU.mult)
                yield
                b1 = dve(TT, ctx_[:, 2, :], ctx_[:, 2, :], k_, ALU.add, w=[b1, b2])
                b3 = dve(TT, ctx_[:, 3, :], ctx_[:, 3, :], r_, ALU.subtract, w=[b3, b4])
                blocks[c] = [b6, b6, b1, b3]

            def merge(c):
                nonlocal mean_read, sq_read, dev_read, hb_read
                cs, ctx_, cd = slice(c * CHUNK, (c + 1) * CHUNK), ctxb[c % 2], blocks[c]
                for i in range(4):
                    m = mm(ps[:, 2, :], K("mean"), ctx_[:, i, :], start=i == 0, stop=i == 3, w=[bank_free[2]] + cd)
                mean = act(S.mul, mean_, ps[:, 2, :], 0.25, w=[m, mean_read])
                bank_free[2] = mean
                yield
                for i in range(4):
                    mean_read = dve(TT, ctx_[:, i, :], ctx_[:, i, :], mean_, ALU.subtract, w=[mean])
                    s = act(S.activation, sqb[:, i, :], ctx_[:, i, :], ACT.Square, w=[mean_read, done[-1], sq_read])
                yield
                for t in range(4):
                    for i in range(4):
                        m = mm(ps[0:4, 3, 0:P], K("meanrow")[:, 4 * t:4 * t + 4], sqb[:, i, t * P:(t + 1) * P],
                               start=t == 0 and i == 0, stop=t == 3 and i == 3, w=[bank_free[3], s])
                sq_read = m
                rt = act(S.activation, dev[0:4, :], ps[0:4, 3, 0:P], ACT.Sqrt, bias=C("eps5")[0:4, :], scale=0.25,
                         w=[m, loads["cols"], dev_read])
                bank_free[3] = rt
                yield
                iv = dve(V.reciprocal, dev[0:4, :], dev[0:4, :], w=[rt])
                for t in range(4):
                    m = mm(ps[:, 7, t * P:(t + 1) * P], tilerow[:, t * P:(t + 1) * P], dev[0:4, :],
                           w=[bank_free[7], iv, loads["tilerow"]])
                dev_read = m
                yield
                for i in range(4):
                    nd = dve(TT, ctx_[:, i, :], ctx_[:, i, :], ps[:, 7, :], ALU.mult, w=[m])
                bank_free[7] = nd
                yield
                for o in range(2):
                    for i in range(4):
                        m = mm(ps[:, 4 + o, :], w1[:, i, o * P:(o + 1) * P], ctx_[:, i, :], start=i == 0, stop=i == 3,
                               w=[bank_free[4 + o], nd, g_])
                    ge = act(S.activation, hb[:, o, :], ps[:, 4 + o, :], ACT.Gelu, bias=bias1[:, o:o + 1], w=[m, bb, hb_read])
                    bank_free[4 + o] = ge
                ctx_read[c % 2] = m
                for o in range(2):
                    m = mm(ps[:, 6, :], wp("L2", "w2T")[:, o * P:(o + 1) * P], hb[:, o, :], start=o == 0, stop=o == 1,
                           w=[bank_free[6], ge])
                hb_read = m
                yield
                a = dve(V.scalar_tensor_tensor, total, ps[:, 6, :], C("L2_b2"), h[:, cs], ALU.add, ALU.add, w=[m])
                bank_free[6] = a
                out[c] = dve(TT, X[:, cs], X[:, cs], total, ALU.add, w=[a])

            project(0)
            for c in range(NCHUNK + 1):
                going = ([retrieve(c)] if c < NCHUNK else []) + ([merge(c - 1)] if c else [])
                while going:
                    going = [g for g in going if next(g, going) is None]
            return out

        def l3_attn(x_ready):
            start_stage()
            h = arena.take(TOKENS)
            work = (arena.take(TOKENS), arena.take(TOKENS))
            wg = fold[:, 0:3 * P]
            g = dve(V.tensor_scalar, wg, wp("L3a", "qkvaT"), C("gamma"), float(np.float32(np.sqrt(P))), ALU.mult, ALU.mult,
                    w=[loads["L3a"], loads["cols"]])
            done = layernorm(X, h, "eps5", x_ready, work=work)
            sq, sd = work
            a_, kv, q, cum = (arena.take(TOKENS) for _ in range(4))
            out = []
            for c in range(NCHUNK):
                cs = slice(c * CHUNK, (c + 1) * CHUNK)
                s = act(S.activation, sq[:, cs], h[:, cs], ACT.Square, w=[done[c]])
                m = mm(ps[:, 7, :], K("mean"), sq[:, cs], w=[s, bank_free[7]])
                rt = act(S.activation, sd[:, cs], ps[:, 7, :], ACT.Sqrt, scale=float(P), bias=C("zero"), w=[m])
                bank_free[7] = rt
                cl = dve(V.tensor_scalar, sd[:, cs], sd[:, cs], 1e-12, None, ALU.max, w=[rt])
                iv = dve(V.reciprocal, sd[:, cs], sd[:, cs], w=[cl])
                xn = dve(V.tensor_tensor, h[:, cs], h[:, cs], sd[:, cs], ALU.mult, w=[iv])
                k = 3 * (c % 2)
                for j in range(3):
                    m = mm(ps[:, k + j, :], wg[:, j * P:(j + 1) * P], h[:, cs], w=[bank_free[k + j], xn, g])
                sg = act(S.activation, a_[:, cs], ps[:, k + 2, :], ACT.Sigmoid, w=[m])
                e1 = act(S.activation, kv[:, cs], ps[:, k + 1, :], ACT.Copy)
                bank_free[k + 2] = bank_free[k + 1] = e1
                z = pool(G.memset, seqs(a_[:, cs])[:, :, 0:1], 0.0, w=[sg])
                cu = dve(V.tensor_tensor_scan, cum[:, cs], a_[:, cs], kv[:, cs], 0.0, ALU.mult, ALU.add, w=[z, e1])
                pq = dve(V.tensor_tensor, q[:, cs], cum[:, cs], ps[:, k, :], ALU.mult, w=[cu])
                bank_free[k] = pq
                out.append(dve(V.tensor_tensor, X[:, cs], X[:, cs], q[:, cs], ALU.add, w=[pq]))
            return out

        def softmax_small(lg, e, ready, small):
            v = lg.rearrange("p (b e) -> p b e", e=e)
            mx, = (small,)
            a = dve(V.tensor_reduce, mx, v, AXX, ALU.max, w=ready)
            a = dve(V.tensor_tensor, v, v, mx.unsqueeze(2).to_broadcast([P, BATCH, e]), ALU.subtract, w=[a])
            a = act(S.activation, lg, lg, ACT.Exp, w=[a])
            a = dve(V.tensor_reduce, mx, v, AXX, ALU.add, w=[a])
            a = dve(V.reciprocal, mx, mx, w=[a])
            return dve(V.tensor_tensor, v, v, mx.unsqueeze(2).to_broadcast([P, BATCH, e]), ALU.mult, w=[a])

        def route(n_, lo, e, lg, ready, rep, mean, small):
            a = dve(V.tensor_reduce, mean, seqs(n_, BATCH), AXX, ALU.add, w=ready)
            a = dve(V.tensor_scalar, mean, mean, 1.0 / SEQ, None, ALU.mult, w=[a])
            r = dve(V.tensor_copy, rep[:, 0:e, :], wp("L3m", "rw")[:, lo:lo + e].unsqueeze(2).to_broadcast([P, e, P]),
                    w=ready + [loads["L3m"]])
            for i in range(e):
                m = mm(ps[:, 7, i * BATCH:(i + 1) * BATCH], rep[:, i, :], mean, w=[bank_free[7], a, r])
            v = lg.rearrange("p (b e) -> p b e", e=e)
            d = dve(V.tensor_tensor, v, ps[:, 7, 0:e * BATCH].rearrange("p (e b) -> p b e", e=e),
                    wp("L3m", "rb")[:, lo:lo + e].unsqueeze(1).to_broadcast([P, BATCH, e]), ALU.add, w=[m])
            bank_free[7] = d
            return softmax_small(lg, e, [d], small)

        experts_loaded = [pr.counter(f"expert_loaded{n}") for n in range(BATCH * TOP_K)]

        def l3_ffn(x_ready):
            start_stage()
            buffer2 = arena.take(2 * TOKENS)
            work = (buffer2[:, 0:TOKENS], buffer2[:, TOKENS:])
            n1 = arena.take(TOKENS)
            done = layernorm(X, X0, "eps5", x_ready, work=work)
            done = layernorm(X0, n1, "eps6", done, "ln1_g", "ln1_b", work)
            ctxT = [arena.take(SEQ) for _ in range(M_EXPERTS)]
            rep = buffer2[:, 0:EXPERTS * P].rearrange("p (e c) -> p e c", e=EXPERTS)
            mean, small, bop = (arena.take(BATCH) for _ in range(3))
            bvp = arena.take(M_EXPERTS * BATCH)
            mp = probs[:, 0:M_EXPERTS * BATCH]
            mp_done = route(n1, 0, M_EXPERTS, mp, done, rep, mean, small)
            mpv = mp.rearrange("p (b e) -> p b e", e=M_EXPERTS)
            a = dve(V.tensor_scalar, bop, mpv[:, :, 0:1].rearrange("p b e -> p (b e)"), C("bo0"), None, ALU.mult, w=[mp_done])
            bop_done = dve(V.scalar_tensor_tensor, bop, mpv[:, :, 1:2].rearrange("p b e -> p (b e)"), C("bo1"), bop,
                           ALU.mult, ALU.add, w=[a])
            for m in range(M_EXPERTS):
                bvp_done = dve(V.tensor_scalar, bvp.rearrange("p (b e) -> p b e", e=M_EXPERTS)[:, :, m:m + 1], mpv[:, :, m:m + 1],
                               C(f"vL3_{m}"), None, ALU.mult, w=[mp_done])
            out, ct_read, ct_done = [None] * BATCH, [None], [None, None]

            def finish(n, tr):
                b, m = n // M_EXPERTS, n % M_EXPERTS
                cp = act(S.activation, ctxT[m], ps[:, 7, 0:SEQ], ACT.Identity, bias=bvp[:, n:n + 1], w=[tr, ct_read[0], bvp_done])
                ct_done[m] = bank_free[7] = cp

                def project():
                    for j in range(M_EXPERTS):
                        y = mm(ps[:, 7, 0:SEQ], wp("L3m", "wo")[:, j * P:(j + 1) * P], ctxT[j], start=j == 0,
                               stop=j == M_EXPERTS - 1, w=[bank_free[7]] + ct_done)
                    ct_read[0] = y
                    bs = slice(b * SEQ, (b + 1) * SEQ)
                    out[b] = dve(V.scalar_tensor_tensor, X0[:, bs], ps[:, 7, 0:SEQ], bop[:, b:b + 1], X0[:, bs],
                                 ALU.add, ALU.add, w=[y, bop_done])
                    bank_free[7] = out[b]

                if m == M_EXPERTS - 1:
                    heads.att.after(2, project)

            heads = SmallHeads("L3m", "L3", M_EXPERTS, n1, done, (), (), finish, done + [mp_done], buffer2,
                               lambda n: mp[:, n:n + 1])
            heads.run()
            x1 = [out[PER * c + PER - 1] for c in range(NCHUNK)]

            start_stage()
            work = (arena.take(TOKENS), arena.take(TOKENS))
            n2 = arena.take(TOKENS)
            rep = work[0][:, 0:EXPERTS * P].rearrange("p (e c) -> p e c", e=EXPERTS)
            mean, small = (arena.take(BATCH) for _ in range(2))
            done = layernorm(X0, n2, "eps6", x1, "ln2_g", "ln2_b", work)
            ep = probs[:, 0:EXPERTS * BATCH]
            pv_ = ep.rearrange("p (b e) -> p b e", e=EXPERTS)
            epd = route(n2, M_EXPERTS, EXPERTS, ep, done, rep, mean, small)
            gt = arena.take(BATCH * EXPERTS * EXPERTS).rearrange("p (b e f) -> p b e f", b=BATCH, e=EXPERTS)
            eq = arena.take(BATCH * EXPERTS * EXPERTS).rearrange("p (b e f) -> p b e f", b=BATCH, e=EXPERTS)
            rank = arena.take(BATCH * EXPERTS)
            rv = rank.rearrange("p (b e) -> p b e", e=EXPERTS)
            for b in range(BATCH):
                mine = pv_[:, b, :].unsqueeze(2).to_broadcast([P, EXPERTS, EXPERTS])
                other = pv_[:, b, :].unsqueeze(1).to_broadcast([P, EXPERTS, EXPERTS])
                g1 = dve(V.tensor_tensor, gt[:, b], other, mine, ALU.is_gt, w=[epd])
                g2 = dve(V.tensor_tensor, eq[:, b], other, mine, ALU.is_equal)
                g2 = dve(V.tensor_tensor, eq[:, b], eq[:, b], K("earlier").rearrange("p (e f) -> p e f", e=EXPERTS), ALU.mult, w=[g2])
                g1 = dve(V.tensor_tensor, gt[:, b], gt[:, b], eq[:, b], ALU.add, w=[g1, g2])
                g1 = dve(V.tensor_reduce, rv[:, b, :], gt[:, b], AXX, ALU.add, w=[g1])
            g1 = dve(V.scalar_tensor_tensor, ep, rank, float(TOP_K), ep, ALU.is_lt, ALU.mult, w=[g1])
            g1 = dve(V.tensor_reduce, small, pv_, AXX, ALU.add, w=[g1])
            g1 = dve(V.reciprocal, small, small, w=[g1])
            gate = dve(V.tensor_tensor, pv_, pv_, small.unsqueeze(2).to_broadcast([P, BATCH, EXPERTS]), ALU.mult, w=[g1])
            pick, rowf, gates = arena.take(BATCH * EXPERTS), arena.take(TOP_K * BATCH), arena.take(TOP_K * BATCH)
            row_no = arena.take(TOP_K * BATCH).bitcast(U32)
            pick3 = pick.rearrange("p (b e) -> p b e", e=EXPERTS)
            g1 = gate
            for k in range(TOP_K):
                for what, result in ((K("expert_row").unsqueeze(1).to_broadcast([P, BATCH, EXPERTS]), rowf), (pv_, gates)):
                    g1 = dve(V.scalar_tensor_tensor, pick3, rv, float(k), what, ALU.is_equal, ALU.mult, w=[g1])
                    g1 = dve(V.tensor_reduce, result[:, k * BATCH:(k + 1) * BATCH], pick3, AXX, ALU.add, w=[g1])
            g2 = dve(V.tensor_scalar, rowf, rowf, C("partition"), None, ALU.add, w=[g1])
            row_done = dve(V.tensor_copy, row_no, rowf, w=[g2])
            chosen, arrived = {}, {}
            for b in range(BATCH):
                for k in range(TOP_K):
                    chosen[b, k] = arena.take(EXPERT_N)
                    arrived[b, k] = pool_queue.dma(chosen[b, k], ins["experts"], experts_loaded[b * TOP_K + k],
                                                   w=[row_done], rows=row_no[:, k * BATCH + b:k * BATCH + b + 1])
            hb = [arena.take(2 * SEQ) for _ in range(3)]
            hb_read = [None] * 3
            units = [(b, k) for b in range(BATCH) for k in range(TOP_K)]
            gated, out = {}, [None] * BATCH

            def up(n):
                b, k = units[n]
                u, bank, bs = n % 3, n % 4, slice(b * SEQ, (b + 1) * SEQ)
                for f in range(2):
                    m = mm(ps[:, bank, f * SEQ:(f + 1) * SEQ], chosen[b, k][:, f * P:(f + 1) * P], n2[:, bs],
                           w=[bank_free[bank], done[b // PER], arrived[b, k]])
                ge = act(S.activation, hb[u], ps[:, bank, :], ACT.Gelu, w=[m, hb_read[u]])
                bank_free[bank] = ge
                gated[n] = dve(V.tensor_scalar, hb[u], hb[u], gates[:, k * BATCH + b:k * BATCH + b + 1], None, ALU.mult, w=[ge, g1])

            def down(n):
                b, k = units[n]
                u, bank, bs = n % 3, 4 + b % 2, slice(b * SEQ, (b + 1) * SEQ)
                for f in range(2):
                    m = mm(ps[:, bank, 0:SEQ], chosen[b, k][:, FF + f * P:FF + (f + 1) * P], hb[u][:, f * SEQ:(f + 1) * SEQ],
                           start=(k == 0 and f == 0), stop=(k == TOP_K - 1 and f == 1), w=[gated[n], bank_free[bank]])
                hb_read[u] = m
                if k == TOP_K - 1:
                    a = dve(V.tensor_tensor, X0[:, bs], X0[:, bs], ps[:, bank, 0:SEQ], ALU.add, w=[m])
                    bank_free[bank] = a
                    out[b] = dve(V.scalar_tensor_tensor, X[:, bs], X0[:, bs], 0.5, X[:, bs], ALU.mult, ALU.add, w=[a])

            for n in range(len(units) + 2):
                if n < len(units):
                    up(n)
                if n >= 2:
                    down(n - 2)
            return [out[PER * c + PER - 1] for c in range(NCHUNK)]

        order = [l0_ffn, l0_attn, l0_ffn, l1_ffn, l1_attn, l1_ffn, l2_ffn, l2_attn, l2_ffn, l3_ffn, l3_attn, l3_ffn]
        for s in stages:
            x_ready = order[s](x_ready)

        stored = pr.sem("stored")
        for c in range(NCHUNK):
            x_ready[c].waited_for = True
        sems = {}
        for q in pr.engines:
            q.count(sems)

        with nc.Block() as block:
            @block.sync
            def _(eng):
                sp.emit(eng)
                for c in range(NCHUNK):
                    cs = slice(c * CHUNK, (c + 1) * CHUNK)
                    eng.wait_ge(x_ready[c].sem, x_ready[c].value)
                    eng.dma_start(out[:, cs], X[:, cs]).then_inc(stored, 16)
                eng.wait_ge(stored, 16 * NCHUNK)
                for t in loads.values():
                    eng.wait_ge(t.sem, t.value)

            @block.tensor
            def _(eng):
                pe.emit(eng)

            @block.scalar
            def _(eng):
                act.emit(eng)

            @block.vector
            def _(eng):
                dve.emit(eng)

            @block.gpsimd
            def _(eng):
                pool_queue.emit(eng)


def constants():
    c = {}
    eye = np.eye(P)
    c["ident"], c["mean"] = eye, np.full((P, P), 1.0 / P)
    c["center"] = eye - 1.0 / P
    i, j = np.arange(P)[:, None], np.arange(P)[None, :]
    c["causal_q"] = np.where(j > i, MASKED, 0.0)
    c["causal_k"] = c["causal_q"].T
    q, k = P + i, WINDOW + np.arange(3 * WINDOW)[None, :]
    c["local_q1"] = np.where((q < k) | (q > k + WINDOW), MASKED, 0.0)
    c["negsel"] = np.where(i % 32 == np.arange(32)[None, :], -1.0, 0.0)
    f4 = np.float32
    half = np.arange(0, L0_DIM, 2, dtype=f4)
    inv_freq = (f4(1.0) / f4(10000.0) ** (half / f4(L0_DIM))).astype(f4)
    t = np.arange(SEQ, dtype=f4)
    fr = (t[:, None] * inv_freq[None, :]).astype(f4)
    fr = np.concatenate([fr, fr], -1).astype(np.float64)
    base = (half + f4(0.4 * L0_DIM)) / f4(1.4 * L0_DIM)
    power = (t - SEQ // 2) / f4(WINDOW // 2)
    sc = base.astype(np.float64)[None, :] ** power.astype(np.float64)[:, None]
    sc = np.concatenate([sc, sc], -1)
    sign = np.where(np.arange(L0_DIM) < L0_DIM // 2, -1.0, 1.0)
    two = lambda a: np.concatenate([a.T, a.T], 0)
    c["cos_q"], c["sin_q"] = two(8.0 * np.cos(fr) * sc), two(8.0 * np.sin(fr) * sc * sign)
    c["cos_k"], c["sin_k"] = two(np.cos(fr) / sc), two(np.sin(fr) / sc * sign)
    c["pos"] = np.broadcast_to(t, (P, SEQ))
    ns, hs = np.zeros((P, 8, 32)), np.zeros((P, 4, P))
    for b in range(8):
        for hh in range(2):
            for part in range(PARTS):
                ns[64 * hh:64 * hh + 64, b, 8 * part + 2 * (b // 4) + hh] = 1.0
                if b >= 4:
                    hs[32 * (b - 4) + 8 * part + 2 + hh, b - 4, 64 * hh:64 * hh + 64] = 1.0
    c["normsel"], c["headsel"] = ns.reshape(P, 8 * 32), hs.reshape(P, 4 * P)
    c["meanrow"] = np.broadcast_to(np.eye(4).reshape(1, 16) / P, (P, 16))
    n = np.arange(16)
    re = np.array([np.cos(2 * np.pi * f * n / 16) for f in range(9)])
    im = np.array([-np.sin(2 * np.pi * f * n / 16) for f in range(9)])
    d = {x: np.zeros((P, P)) for x in ("dft_k1", "dft_k2", "dft_v1", "dft_v2", "idft1", "idft2")}
    for h in range(8):
        r = slice(16 * h, 16 * h + 16)
        for f in range(8):
            a, b = 8 * h + f, 64 + 8 * h + f
            d["dft_k1"][r, a], d["dft_k1"][r, b] = re[f], (re[8] if f == 0 else im[f])
            if f:
                d["dft_k2"][r, a], d["dft_k2"][r, b] = -im[f], re[f]
                d["dft_v1"][r, a], d["dft_v1"][r, b] = re[f], re[f]
                d["dft_v2"][r, a], d["dft_v2"][r, b] = im[f], im[f]
                cr, ci = 2 * np.cos(2 * np.pi * f * n / 16) / 16, -2 * np.sin(2 * np.pi * f * n / 16) / 16
                d["idft1"][r, a], d["idft1"][r, b] = cr, ci
                d["idft2"][r, a], d["idft2"][r, b] = -ci, cr
            else:
                d["dft_v1"][r, a], d["dft_v1"][r, b] = re[0], re[8]
                d["idft1"][r, a], d["idft1"][r, b] = 1.0 / 16, re[8] / 16
    c.update(d)
    c["expert_row"] = np.broadcast_to(P * np.arange(EXPERTS), (P, EXPERTS))
    c["earlier"] = np.broadcast_to((np.arange(8)[None, :] < np.arange(8)[:, None]).astype(float).reshape(1, 64), (P, 64))
    return c


def layout(a):
    f = np.float32
    a = {k: np.asarray(v) for k, v in a.items()}
    col = {}
    g = {}
    rot = np.concatenate([np.arange(32, 64), np.arange(0, 32)])
    for l in range(DEPTH):
        qs, ks = a["L0_ffn_q_scale"][l], a["L0_ffn_k_scale"][l]
        col[f"L0_qs{l}"], col[f"L0_qsr{l}"] = np.tile(qs, 2), np.tile(qs[rot], 2)
        col[f"L0_ks{l}"], col[f"L0_ksr{l}"] = np.tile(ks, 2), np.tile(ks[rot], 2)
        col[f"L0_lg{l}"], col[f"L0_lb{l}"], col[f"L0_b2{l}"] = a["L0_ffn_ln_g"][l], a["L0_ffn_ln_b"][l], a["L0_ffn_b2"][l]
        for half in range(2):
            for j, (at, n) in enumerate(HID_BLOCKS):
                v = np.zeros(P, f)
                v[:n] = a["L0_ffn_b1"][l][half * HID + at:half * HID + at + n]
                col[f"L0_b1{l}_{3 * half + j}"] = v
        wq = a["L0_ffn_wqkv"][l]
        wr = wq[:, :2 * INNER].reshape(P, 16, 64)[:, :, rot].reshape(P, 2 * INNER)
        wo = a["L0_ffn_wo"][l].reshape(4, P, P).transpose(1, 0, 2).reshape(P, INNER)
        w2 = np.zeros((3 * P, P), f)
        w2[:HID] = a["L0_ffn_w2"][l]
        w2 = w2.reshape(3, P, P).transpose(1, 0, 2).reshape(P, 3 * P)
        g[f"L0f{l}"] = [wq, wr, wo, a["L0_ffn_w1"][l], w2]
    w = a["L0_attn_w_qkv"]
    g["L0a"] = [w[:, :P].T, w[:, P:2 * P].T, w[:, 2 * P:].T, a["L0_attn_w_out"]]
    g["L1f"] = [a["L1_ffn_W_fc"].T, a["L1_ffn_W_proj"].T.reshape(4, P, P).transpose(1, 0, 2).reshape(P, 4 * P)]

    def by_feature(w_):
        return w_.reshape(-1, HEADS, KD).transpose(0, 2, 1).reshape(-1, P)

    w, bq = a["L1_attn_w_qkv"], a["L1_attn_b_qkv"]
    g["L1a"] = [by_feature(w[:, :P]), by_feature(w[:, P:2 * P]), w[:, 2 * P:], a["L1_attn_w_out"]]
    col["qL1_0"], col["kL1_0"], col["vL1_0"] = by_feature(bq[None, :P])[0], by_feature(bq[None, P:2 * P])[0], bq[2 * P:]
    col["L1_bo"] = a["L1_attn_b_out"]
    col["L2_b"], col["ph"], col["bmag"], col["bq"] = a["L2_ffn_b"], a["L2_attn_random_phases"], a["L2_attn_b_mag"], a["L2_attn_b_q"]
    for i in range(4):
        col[f"L2_lg{i}"], col[f"L2_lb{i}"] = a["L2_attn_ln_g"][i * P:(i + 1) * P], a["L2_attn_ln_b"][i * P:(i + 1) * P]
    col["L2_b1_0"], col["L2_b1_1"], col["L2_b2"] = a["L2_attn_b1"][:P], a["L2_attn_b1"][P:], a["L2_attn_b2"]
    w1T = a["L2_attn_W1"].T.reshape(4, P, FF).transpose(1, 0, 2).reshape(P, 4 * FF)
    w2T = a["L2_attn_W2"].T.reshape(2, P, P).transpose(1, 0, 2).reshape(P, 2 * P)
    g["L2"] = [a["L2_ffn_W"].T, a["L2_attn_W_mag"].T, a["L2_attn_W_q"].T, w1T, w2T]
    low = np.concatenate([a["L2_ffn_V_r"].T, a["L2_ffn_C"].T], 1)
    col["gamma"] = a["L3_attn_gamma"]
    g["L3a"] = [a["L3_attn_w_qkva"].T]
    for n in ("ln1_g", "ln1_b", "ln2_g", "ln2_b"):
        col[n] = a[f"L3_ffn_{n}"]
    for m in range(M_EXPERTS):
        col[f"qL3_{m}"] = by_feature(a["L3_ffn_mha_bq"][m][None])[0]
        col[f"kL3_{m}"] = by_feature(a["L3_ffn_mha_bk"][m][None])[0]
        col[f"vL3_{m}"] = a["L3_ffn_mha_bv"][m].reshape(P)
    col["bo0"], col["bo1"] = a["L3_ffn_mha_bo"]
    perm = lambda w_: w_.reshape(M_EXPERTS, P, P)
    g["L3m"] = [np.concatenate([by_feature(m) for m in perm(a["L3_ffn_mha_wq"])], 1),
                np.concatenate([by_feature(m) for m in perm(a["L3_ffn_mha_wk"])], 1),
                np.concatenate(list(perm(a["L3_ffn_mha_wv"])), 1), np.concatenate(list(perm(a["L3_ffn_mha_wo"])), 1),
                a["L3_ffn_mha_rw"], a["L3_ffn_ffn_rw"],
                np.broadcast_to(a["L3_ffn_mha_rb"], (P, M_EXPERTS)), np.broadcast_to(a["L3_ffn_ffn_rb"], (P, EXPERTS))]
    experts = np.concatenate([a["L3_ffn_fw1"], a["L3_ffn_fw2"].reshape(EXPERTS, 2, P, P).transpose(0, 2, 1, 3).reshape(EXPERTS, P, FF)], 2)
    col["eps5"], col["eps6"], col["eps8"], col["zero"] = (np.full(P, e) for e in (1e-5, 1e-6, 1e-8, 0.0))
    c = constants()
    part = np.arange(P) % 32 // 8
    col["partition"] = np.arange(P)
    col["past_hi"], col["past_mid"] = np.where(part >= 1, -1.0, 0.0), np.where(part >= 2, -1.0, 0.0)
    tilerow = np.zeros((4, 4, P))
    for t in range(4):
        tilerow[t, t] = 1.0
    out = {
        "x": a["L0_attn_x"].reshape(TOKENS, P).T,
        "const": np.concatenate([c[n] for n in CONST], 1),
        "cols": np.stack([col[n] for n in COLUMNS], 1),
        "tilerow": tilerow.reshape(4, TILEROW_N),
        "low": low,
        "experts": experts.reshape(EXPERTS * P, EXPERT_N),
    }
    for n, parts in g.items():
        out[n] = np.concatenate(parts, 1)
    return {n: np.ascontiguousarray(v, dtype=f) for n, v in out.items()}


def kernel(**inputs):
    import concourse.bacc as bacc
    from concourse.bass_utils import run_bass_kernel_spmd

    nc = bacc.Bacc("TRN2", target_bir_lowering=False, num_devices=1)
    arrays = layout(inputs)
    ins = {n: nc.dram_tensor(f"in_{n}", v.shape, F32, kind="ExternalInput").ap() for n, v in arrays.items()}
    out = nc.dram_tensor("out", (P, TOKENS), F32, kind="ExternalOutput").ap()
    program(nc, ins, out)
    r = run_bass_kernel_spmd(nc, [{f"in_{n}": v for n, v in arrays.items()}], core_ids=[0])
    return r.results[0]["out"].T.reshape(BATCH, SEQ, P)
```
